# Optimizing a Trainium2 kernel written in Bass

```python
import numpy as np
import jax
import jax.numpy as jnp

def _softmax(x, axis=-1):
    return jax.nn.softmax(x, axis=axis)

def _gelu(x):
    return jax.nn.gelu(x, approximate=True)

def _silu(x):
    return jax.nn.silu(x)

def _sigmoid(x):
    return jax.nn.sigmoid(x)

def _layernorm(x, axis=-1, eps=1e-05):
    m = jnp.mean(x, axis=axis, keepdims=True)
    v = jnp.var(x, axis=axis, keepdims=True)
    return (x - m) / jnp.sqrt(v + eps)

def _scatter_add(tgt, idx, src, axis=0):
    return tgt.at[idx].add(src)

def _segment_sum(src, seg, n):
    return jax.ops.segment_sum(src, seg, n)
kernel_name = 'mk_vit_tower_d1_tok_img512_r4_a8257f'

def setup_inputs(seed: int=0):
    np.random.seed(seed)
    _w = jnp.asarray

    def _rec_inputs():
        import jax
        import jax.numpy as jnp
        _rk = jax.random.key(seed)
        x = -0.000147625 + 0.999875 * jax.random.normal(jax.random.fold_in(_rk, 1), (64, 3, 224, 224), jnp.float32)
        return x
    x = _rec_inputs()

    def _L0_tok_setup():
        import jax, jax.numpy as jnp
        import numpy as np
        N_PATCHES = 8
        PATCH = 28
        C = 3
        IN_D = C * PATCH * PATCH
        HID = 128
        SEQ = N_PATCHES * N_PATCHES + 1

        def _positional_embedding(seq_len, dim):
            i = np.arange(seq_len)[:, None].astype(np.float32)
            j = np.arange(dim)[None, :].astype(np.float32)
            ang = i / np.power(100000.0, j / dim)
            pe = np.where(j % 2 == 0, np.sin(ang), np.cos(ang))
            return jnp.asarray(pe, dtype=jnp.float32)
        key = jax.random.key(seed)
        k1, k2, k3, k4 = jax.random.split(key, 4)
        B = 64
        X = jax.random.normal(k1, (B, C, 224, 224), dtype=jnp.float32)
        bound = 1.0 / np.sqrt(IN_D)
        W = jax.random.uniform(k2, (HID, IN_D), minval=-bound, maxval=bound, dtype=jnp.float32)
        b = jax.random.uniform(k3, (HID,), minval=-bound, maxval=bound, dtype=jnp.float32)
        class_token = jax.random.uniform(k4, (1, HID), dtype=jnp.float32)
        pos_embed = _positional_embedding(SEQ, HID)
        return {'X': X, 'W': W, 'b': b, 'class_token': class_token, 'pos_embed': pos_embed}
    _L0_tok_all = _L0_tok_setup()
    _L0_tok_in = {k: v for k, v in _L0_tok_all.items() if k in ('W', 'b', 'class_token', 'pos_embed')}
    del _L0_tok_all

    def _L0_attn_setup():
        import jax, jax.numpy as jnp
        import numpy as np
        from math import sqrt
        key = jax.random.key(seed)
        k1, k2, k3, k4 = jax.random.split(key, 4)
        bs, N, D, H = (2, 1024, 128, 8)
        z = jax.random.normal(k1, (bs, N, D), dtype=jnp.float32)
        w_qkv = jax.random.normal(k2, (3 * D, D), dtype=jnp.float32) * (1.0 / sqrt(D))
        w_agg = jax.random.normal(k3, (D, D), dtype=jnp.float32) * (1.0 / sqrt(D))
        b_agg = jax.random.normal(k4, (D,), dtype=jnp.float32) * 0.01
        return {'z': z, 'w_qkv': w_qkv, 'w_agg': w_agg, 'b_agg': b_agg}
    _L0_attn_all = _L0_attn_setup()
    _L0_attn_in = {k: v for k, v in _L0_attn_all.items() if k in ('w_qkv', 'w_agg', 'b_agg')}
    del _L0_attn_all

    def _L0_ffn_setup():
        import jax, jax.numpy as jnp
        import numpy as np
        from jax import lax
        B, S, IN, D, E, NH = (8, 128, 128, 256, 4, 16)
        DH = D // NH
        EPS = 1e-05
        SCALE = np.float32(1.0 / np.sqrt(DH))

        def _ln(x, g, b):
            m = x.mean(-1, keepdims=True)
            v = ((x - m) ** 2).mean(-1, keepdims=True)
            return (x - m) * lax.rsqrt(v + EPS) * g + b

        def _lstm_dir(x, Wi, Wh, b):
            bsz = x.shape[0]
            h0 = jnp.zeros((bsz, Wh.shape[0]), x.dtype)

            def step(carry, xt):
                h, c = carry
                zg = xt @ Wi + h @ Wh + b
                i, f, g, o = jnp.split(zg, 4, axis=-1)
                c = jax.nn.sigmoid(f) * c + jax.nn.sigmoid(i) * jnp.tanh(g)
                h = jax.nn.sigmoid(o) * jnp.tanh(c)
                return ((h, c), h)
            _, hs = lax.scan(step, (h0, h0), jnp.swapaxes(x, 0, 1))
            return jnp.swapaxes(hs, 0, 1)

        def _expert(x, p):
            ew1, eb1, ew2, eb2, eg, ebeta, aiw, aib, aow, aob, wif, whf, bf, wibk, whbk, bbk, sw1, sb1, sw2, sb2, tw1, tb1, tw2, tb2, dw1, db1, dw2, db2, dg, dbeta = p
            h = _ln(jax.nn.relu(x @ ew1 + eb1) @ ew2 + eb2, eg, ebeta)
            qkv = h @ aiw + aib
            q, k, v = jnp.split(qkv, 3, axis=-1)

            def heads(t):
                return t.reshape(t.shape[0], t.shape[1], NH, DH).transpose(0, 2, 1, 3)
            q, k, v = (heads(q), heads(k), heads(v))
            attn = jax.nn.softmax(jnp.einsum('bhqd,bhkd->bhqk', q, k) * SCALE, axis=-1)
            o = jnp.einsum('bhqk,bhkd->bhqd', attn, v).transpose(0, 2, 1, 3).reshape(h.shape)
            h = o @ aow + aob
            hf = _lstm_dir(h, wif, whf, bf)
            hb = _lstm_dir(h[:, ::-1], wibk, whbk, bbk)[:, ::-1]
            mem = jnp.concatenate([hf, hb], axis=-1)
            gate_s = jax.nn.sigmoid(jax.nn.relu(mem @ sw1 + sb1) @ sw2 + sb2)
            gate_t = jnp.tanh(jax.nn.relu(mem @ tw1 + tb1) @ tw2 + tb2)
            g = gate_s * gate_t
            return _ln(jax.nn.relu(g @ dw1 + db1) @ dw2 + db2, dg, dbeta)

        def _forward(x, router_w, router_b, *p):
            outs = jax.vmap(lambda pe: _expert(x, pe))(tuple(p))
            w = jax.nn.softmax(x @ router_w + router_b, axis=-1)
            return jnp.einsum('ebsd,bse->bsd', outs, w)
        key = jax.random.key(seed)
        ks = iter(jax.random.split(key, 64))

        def rn(shape, scale=0.02):
            return jax.random.normal(next(ks), shape, dtype=jnp.float32) * scale
        z = lambda shape: jnp.zeros(shape, dtype=jnp.float32)
        return {'x': jax.random.normal(next(ks), (B, S, IN), dtype=jnp.float32), 'router_w': rn((IN, E)), 'router_b': z((E,)), 'enc_w1': rn((E, IN, D)), 'enc_b1': z((E, D)), 'enc_w2': rn((E, D, D)), 'enc_b2': z((E, D)), 'enc_g': jnp.ones((E, D), jnp.float32), 'enc_beta': z((E, D)), 'attn_in_w': rn((E, D, 3 * D)), 'attn_in_b': z((E, 3 * D)), 'attn_out_w': rn((E, D, D)), 'attn_out_b': z((E, D)), 'lstm_wi_f': rn((E, D, 4 * D)), 'lstm_wh_f': rn((E, D, 4 * D)), 'lstm_b_f': z((E, 4 * D)), 'lstm_wi_b': rn((E, D, 4 * D)), 'lstm_wh_b': rn((E, D, 4 * D)), 'lstm_b_b': z((E, 4 * D)), 'sig_w1': rn((E, 2 * D, D)), 'sig_b1': z((E, D)), 'sig_w2': rn((E, D, D)), 'sig_b2': z((E, D)), 'tan_w1': rn((E, 2 * D, D)), 'tan_b1': z((E, D)), 'tan_w2': rn((E, D, D)), 'tan_b2': z((E, D)), 'dec_w1': rn((E, D, D)), 'dec_b1': z((E, D)), 'dec_w2': rn((E, D, IN)), 'dec_b2': z((E, IN)), 'dec_g': jnp.ones((E, IN), jnp.float32), 'dec_beta': z((E, IN))}
    _L0_ffn_all = _L0_ffn_setup()
    _L0_ffn_in = {k: v for k, v in _L0_ffn_all.items() if k in ('router_w', 'router_b', 'enc_w1', 'enc_b1', 'enc_w2', 'enc_b2', 'enc_g', 'enc_beta', 'attn_in_w', 'attn_in_b', 'attn_out_w', 'attn_out_b', 'lstm_wi_f', 'lstm_wh_f', 'lstm_b_f', 'lstm_wi_b', 'lstm_wh_b', 'lstm_b_b', 'sig_w1', 'sig_b1', 'sig_w2', 'sig_b2', 'tan_w1', 'tan_b1', 'tan_w2', 'tan_b2', 'dec_w1', 'dec_b1', 'dec_w2', 'dec_b2', 'dec_g', 'dec_beta')}
    del _L0_ffn_all
    return {'x': x, 'L0_tok_W': _L0_tok_in['W'], 'L0_tok_b': _L0_tok_in['b'], 'L0_tok_class_token': _L0_tok_in['class_token'], 'L0_tok_pos_embed': _L0_tok_in['pos_embed'], 'L0_attn_w_qkv': _L0_attn_in['w_qkv'], 'L0_attn_w_agg': _L0_attn_in['w_agg'], 'L0_attn_b_agg': _L0_attn_in['b_agg'], 'L0_ffn_router_w': _L0_ffn_in['router_w'], 'L0_ffn_router_b': _L0_ffn_in['router_b'], 'L0_ffn_enc_w1': _L0_ffn_in['enc_w1'], 'L0_ffn_enc_b1': _L0_ffn_in['enc_b1'], 'L0_ffn_enc_w2': _L0_ffn_in['enc_w2'], 'L0_ffn_enc_b2': _L0_ffn_in['enc_b2'], 'L0_ffn_enc_g': _L0_ffn_in['enc_g'], 'L0_ffn_enc_beta': _L0_ffn_in['enc_beta'], 'L0_ffn_attn_in_w': _L0_ffn_in['attn_in_w'], 'L0_ffn_attn_in_b': _L0_ffn_in['attn_in_b'], 'L0_ffn_attn_out_w': _L0_ffn_in['attn_out_w'], 'L0_ffn_attn_out_b': _L0_ffn_in['attn_out_b'], 'L0_ffn_lstm_wi_f': _L0_ffn_in['lstm_wi_f'], 'L0_ffn_lstm_wh_f': _L0_ffn_in['lstm_wh_f'], 'L0_ffn_lstm_b_f': _L0_ffn_in['lstm_b_f'], 'L0_ffn_lstm_wi_b': _L0_ffn_in['lstm_wi_b'], 'L0_ffn_lstm_wh_b': _L0_ffn_in['lstm_wh_b'], 'L0_ffn_lstm_b_b': _L0_ffn_in['lstm_b_b'], 'L0_ffn_sig_w1': _L0_ffn_in['sig_w1'], 'L0_ffn_sig_b1': _L0_ffn_in['sig_b1'], 'L0_ffn_sig_w2': _L0_ffn_in['sig_w2'], 'L0_ffn_sig_b2': _L0_ffn_in['sig_b2'], 'L0_ffn_tan_w1': _L0_ffn_in['tan_w1'], 'L0_ffn_tan_b1': _L0_ffn_in['tan_b1'], 'L0_ffn_tan_w2': _L0_ffn_in['tan_w2'], 'L0_ffn_tan_b2': _L0_ffn_in['tan_b2'], 'L0_ffn_dec_w1': _L0_ffn_in['dec_w1'], 'L0_ffn_dec_b1': _L0_ffn_in['dec_b1'], 'L0_ffn_dec_w2': _L0_ffn_in['dec_w2'], 'L0_ffn_dec_b2': _L0_ffn_in['dec_b2'], 'L0_ffn_dec_g': _L0_ffn_in['dec_g'], 'L0_ffn_dec_beta': _L0_ffn_in['dec_beta']}

def reference(x, L0_tok_W, L0_tok_b, L0_tok_class_token, L0_tok_pos_embed, L0_attn_w_qkv, L0_attn_w_agg, L0_attn_b_agg, L0_ffn_router_w, L0_ffn_router_b, L0_ffn_enc_w1, L0_ffn_enc_b1, L0_ffn_enc_w2, L0_ffn_enc_b2, L0_ffn_enc_g, L0_ffn_enc_beta, L0_ffn_attn_in_w, L0_ffn_attn_in_b, L0_ffn_attn_out_w, L0_ffn_attn_out_b, L0_ffn_lstm_wi_f, L0_ffn_lstm_wh_f, L0_ffn_lstm_b_f, L0_ffn_lstm_wi_b, L0_ffn_lstm_wh_b, L0_ffn_lstm_b_b, L0_ffn_sig_w1, L0_ffn_sig_b1, L0_ffn_sig_w2, L0_ffn_sig_b2, L0_ffn_tan_w1, L0_ffn_tan_b1, L0_ffn_tan_w2, L0_ffn_tan_b2, L0_ffn_dec_w1, L0_ffn_dec_b1, L0_ffn_dec_w2, L0_ffn_dec_b2, L0_ffn_dec_g, L0_ffn_dec_beta):
    import jax
    import jax.numpy as jnp

    def _L0_tok_ref(X, W, b, class_token, pos_embed):
        import jax, jax.numpy as jnp
        import numpy as np
        N_PATCHES = 8
        PATCH = 28
        C = 3
        IN_D = C * PATCH * PATCH
        HID = 128
        SEQ = N_PATCHES * N_PATCHES + 1

        def _positional_embedding(seq_len, dim):
            i = np.arange(seq_len)[:, None].astype(np.float32)
            j = np.arange(dim)[None, :].astype(np.float32)
            ang = i / np.power(100000.0, j / dim)
            pe = np.where(j % 2 == 0, np.sin(ang), np.cos(ang))
            return jnp.asarray(pe, dtype=jnp.float32)
        B = X.shape[0]
        patches = X.reshape(B, C, N_PATCHES, PATCH, N_PATCHES, PATCH)
        patches = patches.transpose(0, 2, 4, 1, 3, 5).reshape(B, N_PATCHES * N_PATCHES, IN_D)
        tokens = jnp.einsum('bpi,hi->bph', patches, W) + b
        cls = jnp.broadcast_to(class_token[None, :, :], (B, 1, HID))
        tokens = jnp.concatenate([cls, tokens], axis=1)
        return tokens * pos_embed[None, :, :]

    def _L0_attn_ref(z, w_qkv, w_agg, b_agg):
        import jax, jax.numpy as jnp
        import numpy as np
        from math import sqrt
        bs, N, D = z.shape
        H = 8
        Dh = D // H
        qkv = jnp.einsum('bnd,ed->bne', z, w_qkv).reshape(bs, N, 3, H, Dh)
        q, k, v = jnp.moveaxis(qkv, 2, 0)
        q = q.transpose(0, 2, 1, 3)
        k = k.transpose(0, 2, 1, 3)
        v = v.transpose(0, 2, 1, 3)
        scores = jnp.einsum('bhnd,bhmd->bhnm', q, k) / sqrt(Dh)
        attn = jax.nn.softmax(scores, axis=-1)
        sa = jnp.einsum('bhnm,bhmd->bhnd', attn, v)
        sa = sa.transpose(0, 2, 1, 3).reshape(bs, N, H * Dh)
        out = jnp.einsum('bnd,ed->bne', sa, w_agg) + b_agg
        return out

    def _L0_ffn_ref(x, router_w, router_b, enc_w1, enc_b1, enc_w2, enc_b2, enc_g, enc_beta, attn_in_w, attn_in_b, attn_out_w, attn_out_b, lstm_wi_f, lstm_wh_f, lstm_b_f, lstm_wi_b, lstm_wh_b, lstm_b_b, sig_w1, sig_b1, sig_w2, sig_b2, tan_w1, tan_b1, tan_w2, tan_b2, dec_w1, dec_b1, dec_w2, dec_b2, dec_g, dec_beta):
        import jax, jax.numpy as jnp
        import numpy as np
        from jax import lax
        B, S, IN, D, E, NH = (8, 128, 128, 256, 4, 16)
        DH = D // NH
        EPS = 1e-05
        SCALE = np.float32(1.0 / np.sqrt(DH))

        def _ln(x, g, b):
            m = x.mean(-1, keepdims=True)
            v = ((x - m) ** 2).mean(-1, keepdims=True)
            return (x - m) * lax.rsqrt(v + EPS) * g + b

        def _lstm_dir(x, Wi, Wh, b):
            bsz = x.shape[0]
            h0 = jnp.zeros((bsz, Wh.shape[0]), x.dtype)

            def step(carry, xt):
                h, c = carry
                zg = xt @ Wi + h @ Wh + b
                i, f, g, o = jnp.split(zg, 4, axis=-1)
                c = jax.nn.sigmoid(f) * c + jax.nn.sigmoid(i) * jnp.tanh(g)
                h = jax.nn.sigmoid(o) * jnp.tanh(c)
                return ((h, c), h)
            _, hs = lax.scan(step, (h0, h0), jnp.swapaxes(x, 0, 1))
            return jnp.swapaxes(hs, 0, 1)

        def _expert(x, p):
            ew1, eb1, ew2, eb2, eg, ebeta, aiw, aib, aow, aob, wif, whf, bf, wibk, whbk, bbk, sw1, sb1, sw2, sb2, tw1, tb1, tw2, tb2, dw1, db1, dw2, db2, dg, dbeta = p
            h = _ln(jax.nn.relu(x @ ew1 + eb1) @ ew2 + eb2, eg, ebeta)
            qkv = h @ aiw + aib
            q, k, v = jnp.split(qkv, 3, axis=-1)

            def heads(t):
                return t.reshape(t.shape[0], t.shape[1], NH, DH).transpose(0, 2, 1, 3)
            q, k, v = (heads(q), heads(k), heads(v))
            attn = jax.nn.softmax(jnp.einsum('bhqd,bhkd->bhqk', q, k) * SCALE, axis=-1)
            o = jnp.einsum('bhqk,bhkd->bhqd', attn, v).transpose(0, 2, 1, 3).reshape(h.shape)
            h = o @ aow + aob
            hf = _lstm_dir(h, wif, whf, bf)
            hb = _lstm_dir(h[:, ::-1], wibk, whbk, bbk)[:, ::-1]
            mem = jnp.concatenate([hf, hb], axis=-1)
            gate_s = jax.nn.sigmoid(jax.nn.relu(mem @ sw1 + sb1) @ sw2 + sb2)
            gate_t = jnp.tanh(jax.nn.relu(mem @ tw1 + tb1) @ tw2 + tb2)
            g = gate_s * gate_t
            return _ln(jax.nn.relu(g @ dw1 + db1) @ dw2 + db2, dg, dbeta)

        def _forward(x, router_w, router_b, *p):
            outs = jax.vmap(lambda pe: _expert(x, pe))(tuple(p))
            w = jax.nn.softmax(x @ router_w + router_b, axis=-1)
            return jnp.einsum('ebsd,bse->bsd', outs, w)
        return _forward(x, router_w, router_b, enc_w1, enc_b1, enc_w2, enc_b2, enc_g, enc_beta, attn_in_w, attn_in_b, attn_out_w, attn_out_b, lstm_wi_f, lstm_wh_f, lstm_b_f, lstm_wi_b, lstm_wh_b, lstm_b_b, sig_w1, sig_b1, sig_w2, sig_b2, tan_w1, tan_b1, tan_w2, tan_b2, dec_w1, dec_b1, dec_w2, dec_b2, dec_g, dec_beta)
    h = _L0_tok_ref(x, L0_tok_W, L0_tok_b, L0_tok_class_token, L0_tok_pos_embed)
    h = h + _L0_attn_ref(_layernorm(h, axis=-1), L0_attn_w_qkv, L0_attn_w_agg, L0_attn_b_agg)
    h = h + _L0_ffn_ref(_layernorm(h, axis=-1), L0_ffn_router_w, L0_ffn_router_b, L0_ffn_enc_w1, L0_ffn_enc_b1, L0_ffn_enc_w2, L0_ffn_enc_b2, L0_ffn_enc_g, L0_ffn_enc_beta, L0_ffn_attn_in_w, L0_ffn_attn_in_b, L0_ffn_attn_out_w, L0_ffn_attn_out_b, L0_ffn_lstm_wi_f, L0_ffn_lstm_wh_f, L0_ffn_lstm_b_f, L0_ffn_lstm_wi_b, L0_ffn_lstm_wh_b, L0_ffn_lstm_b_b, L0_ffn_sig_w1, L0_ffn_sig_b1, L0_ffn_sig_w2, L0_ffn_sig_b2, L0_ffn_tan_w1, L0_ffn_tan_b1, L0_ffn_tan_w2, L0_ffn_tan_b2, L0_ffn_dec_w1, L0_ffn_dec_b1, L0_ffn_dec_w2, L0_ffn_dec_b2, L0_ffn_dec_g, L0_ffn_dec_beta)
    return h

_drawn_inputs = setup_inputs


def setup_inputs(seed=0):
    import zlib

    import numpy as np

    out = dict(_drawn_inputs(seed))
    spreads = {'L0_ffn_router_b': (0.0, 0.341),
     'L0_ffn_enc_b1': (0.0, 0.8),
     'L0_ffn_enc_b2': (0.0, 0.8),
     'L0_ffn_enc_g': (1.0, 0.6),
     'L0_ffn_enc_beta': (0.0, 0.8),
     'L0_ffn_attn_in_b': (0.0, 0.8),
     'L0_ffn_attn_out_b': (0.0, 0.8),
     'L0_ffn_lstm_b_f': (0.0, 0.8),
     'L0_ffn_lstm_b_b': (0.0, 0.8),
     'L0_ffn_sig_b1': (0.0, 0.8),
     'L0_ffn_sig_b2': (0.0, 0.8),
     'L0_ffn_tan_b1': (0.0, 0.8),
     'L0_ffn_tan_b2': (0.0, 0.294),
     'L0_ffn_dec_b1': (0.0, 0.1),
     'L0_ffn_dec_b2': (0.0, 0.1),
     'L0_ffn_dec_g': (1.0, 0.2),
     'L0_ffn_dec_beta': (0.0, 0.1)}
    factors = {'L0_attn_b_agg': 3.697,
     'L0_ffn_enc_w1': 8.0,
     'L0_ffn_enc_w2': 8.0,
     'L0_ffn_attn_in_w': 8.0,
     'L0_ffn_attn_out_w': 8.0,
     'L0_ffn_lstm_wi_f': 8.0,
     'L0_ffn_lstm_wh_f': 8.0,
     'L0_ffn_lstm_wi_b': 8.0,
     'L0_ffn_lstm_wh_b': 8.0,
     'L0_ffn_sig_w1': 8.0,
     'L0_ffn_sig_w2': 8.0,
     'L0_ffn_tan_w1': 8.0,
     'L0_ffn_tan_w2': 8.0}
    for name, (base, spread) in spreads.items():
        noise = np.random.default_rng([zlib.crc32(name.encode()), seed]).standard_normal(out[name].shape)
        drawn = base * np.exp(spread * noise) if base else spread * noise
        out[name] = jnp.asarray(drawn.astype(out[name].dtype))
    for name, factor in factors.items():
        out[name] = (out[name] * factor).astype(out[name].dtype)
    return out
```

```python
from contextlib import ExitStack

import concourse.bass as bass
from concourse import mybir

F32 = mybir.dt.float32
ALU = mybir.AluOpType
ACT = mybir.ActivationFunctionType
AX = mybir.AxisListType
ds = bass.ds

P = 128
IMAGES, CHANNELS, GRID, PATCH = 64, 3, 8, 28
ROWS = CHANNELS * PATCH
SIDE = GRID * PATCH
SEQ = GRID * GRID + 1
TOKENS = IMAGES * SEQ
HID = 128
D = 256
KD = D // P
EXPERTS = 4
HEAD = 16
EPS = 1e-5
BASE = 1
SCALE = HEAD ** -0.5

GROUP = 4
UNIT = GROUP * SEQ
PAIRS = IMAGES // GROUP // 2
WIDE = 416
WSTEPS, WTRIPS = 5, 2
assert WSTEPS * WTRIPS * WIDE == TOKENS


def semaphores(nc, ctx, tag=""):
    made = []

    def sem(name):
        made.append(ctx.enter_context(nc.semaphore(tag + name)))
        return made[-1]
    return sem, made


def open_block(nc, ctx, made):
    def clear():
        with nc.Block() as block:
            @block.sync
            def _(sp):
                for s in made:
                    sp.sem_clear(s)
    ctx.callback(clear)
    with nc.Block() as block:
        @block.sync
        def _(sp):
            for s in made:
                sp.sem_inc(s, BASE)
    return ctx.enter_context(nc.Block())


def make_identity(pool, tile, zeroed, done):
    pool.memset(tile[:, :], 0.0).then_inc(zeroed, 1)
    pool.wait_ge(zeroed, BASE + 1)
    pool.affine_select(out=tile[:, :], in_=tile[:, :], compare_op=ALU.not_equal, fill=1.0, base=0,
                       pattern=[[-1, P]], channel_multiplier=1).then_inc(done, 1)


def tokens_stage(nc, ps, io, h0, ident):
    XI = 4
    SLOTS = 2
    PADDED = 96
    TRIPS = IMAGES // XI // SLOTS
    NP = GRID * GRID
    with ExitStack() as ctx:
        sb = lambda name, shape: ctx.enter_context(nc.sbuf_tensor(name, shape, F32))
        sem, made = semaphores(nc, ctx)
        image = sb("image", [PADDED, SLOTS, XI, GRID, SIDE])
        w_rows = sb("w_rows", [P, ROWS * PATCH])
        w_cols = sb("w_cols", [PADDED, PATCH, P])
        pos_rows = sb("pos_rows", [SEQ, P])
        pos = sb("pos", [P, SEQ])
        bias = sb("tok_bias", [P, 1])
        cls = sb("cls", [P, 1])
        clsp = sb("clsp", [P, 1])
        loaded = [sem(f"image_loaded{i}") for i in range(SLOTS)]
        consts, w_in = sem("consts_loaded"), sem("w_loaded")
        id_zero, id_done = sem("id_zeroed"), sem("id_done")
        turned, kept = sem("w_turned"), sem("w_kept")
        padded = sem("rows_padded")
        summed, stored, cls_done = sem("tok_summed"), sem("tok_stored"), sem("cls_done")
        block = open_block(nc, ctx, made)
        turns = PATCH // 4

        @block.sync
        def _(sp):
            sp.dma_start(w_rows[:, :], io["tok_W"]).then_inc(w_in, 16)
            sp.dma_start(pos_rows[:, :], io["pos"]).then_inc(consts, 16)
            sp.dma_start(bias[:, :], io["tok_b"].rearrange("(p a) -> p a", a=1)).then_inc(consts, 16)
            sp.dma_start(cls[:, :], io["cls"].rearrange("a p -> p a")).then_inc(consts, 16)
            sp.wait_ge(padded, BASE + 3)
            with sp.Fori(0, TRIPS) as i:
                for s in range(SLOTS):
                    sp.wait_ge(summed, BASE + i * SLOTS)
                    for c in range(CHANNELS):
                        for b in range(XI):
                            src = io["x"][ds((i * SLOTS + s) * XI + b, 1), c].rearrange("a (g p) w -> p (a g) w", p=PATCH)
                            sp.dma_start(image[c * PATCH:(c + 1) * PATCH, s, b], src).then_inc(loaded[s], 16)

        @block.gpsimd
        def _(pool):
            make_identity(pool, ident, id_zero, id_done)
            pool.wait_ge(id_done, BASE + 1)
            pool.memset(image[64:PADDED, 1], 0.0).then_inc(padded, 1)

        @block.tensor
        def _(pe):
            pe.wait_ge(w_in, BASE + 16)
            pe.wait_ge(id_done, BASE + 1)
            w_view = w_rows[:, :].rearrange("p (r q) -> p r q", q=PATCH)
            for g in range(turns):
                if g >= 4:
                    pe.wait_ge(kept, BASE + g - 3)
                for j in range(4):
                    m = pe.transpose(ps[0:ROWS, g % 4, j * P:(j + 1) * P], w_view[:, :, 4 * g + j], ident[:, :])
                m.then_inc(turned, 1)
            pe.wait_ge(consts, BASE + 48)
            pe.wait_ge(kept, BASE + turns)
            pe.transpose(ps[:, 0, 0:SEQ], pos_rows[:, :], ident[0:SEQ, 0:SEQ]).then_inc(turned, 1)
            pe.wait_ge(kept, BASE + turns + 1)
            with pe.Fori(0, TRIPS) as i:
                for s in range(SLOTS):
                    pe.wait_ge(loaded[s], BASE + (i + 1) * 16 * CHANNELS * XI)
                    pe.wait_ge(stored, BASE + i * SLOTS)
                    cols = image[:, s].rearrange("p b g (j q) -> p b g j q", q=PATCH)
                    for q in range(PATCH):
                        m = pe.matmul(ps[:, s % 2, 0:XI * NP], w_cols[:, q, :], cols[:, :, :, :, q],
                                      start=(q == 0), stop=(q == PATCH - 1))
                    m.then_inc(summed, 1)

        @block.vector
        def _(dve):
            dve.memset(image[64:PADDED, 0], 0.0).then_inc(padded, 1)
            dve.memset(w_cols[64:PADDED], 0.0).then_inc(padded, 1)
            dve.wait_ge(padded, BASE + 3)
            for g in range(turns):
                dve.wait_ge(turned, BASE + g + 1)
                dve.tensor_copy(w_cols[0:ROWS, 4 * g:4 * g + 4, :],
                                ps[0:ROWS, g % 4, :].rearrange("p (j m) -> p j m", j=4)).then_inc(kept, 1)
            dve.wait_ge(turned, BASE + turns + 1)
            dve.tensor_copy(pos[:, :], ps[:, 0, 0:SEQ]).then_inc(kept, 1)
            dve.wait_ge(kept, BASE + turns + 1)
            dve.tensor_tensor(clsp[:, :], cls[:, :], pos[:, 0:1], ALU.mult).then_inc(cls_done, 1)
            dve.wait_ge(cls_done, BASE + 1)
            h0_view = h0[:, :].rearrange("p (b s) -> p b s", s=SEQ)
            dve.tensor_copy(h0_view[:, :, 0], clsp[:, :].broadcast_to([P, IMAGES])).then_inc(cls_done, 1)
            with dve.Fori(0, TRIPS) as i:
                for s in range(SLOTS):
                    dve.wait_ge(summed, BASE + i * SLOTS + s + 1)
                    out = h0[:, ds((i * SLOTS + s) * XI * SEQ, XI * SEQ)].rearrange("p (b s) -> p b s", s=SEQ)
                    dve.scalar_tensor_tensor(
                        out=out[:, :, 1:SEQ], in0=ps[:, s % 2, 0:XI * NP].rearrange("p (b t) -> p b t", t=NP),
                        scalar=bias[:, 0:1], in1=pos[:, 1:SEQ].unsqueeze(1).broadcast_to([P, XI, NP]),
                        op0=ALU.add, op1=ALU.mult).then_inc(stored, 1)


def norm_stage(nc, ps, tag, src, dst, add, spill):
    with ExitStack() as ctx:
        sb = lambda name, shape: ctx.enter_context(nc.sbuf_tensor(tag + name, shape, F32))
        sem, made = semaphores(nc, ctx, tag)
        center = sb("center", [P, P])
        mean = sb("mean", [P, P])
        eps = sb("eps", [P, 1])
        xc = sb("xc", [P, 3, WIDE])
        sq = sb("sq", [P, 2, WIDE])
        sd = sb("sd", [P, 2, WIDE])
        rs = sb("rs", [P, 2, WIDE])
        zero, ready = sem("zero"), sem("ready")
        added, centered, copied = sem("added"), sem("centered"), sem("copied")
        squared, varied, rooted = sem("squared"), sem("varied"), sem("rooted")
        inverted, normed, spilled = sem("inverted"), sem("normed"), sem("spilled")
        block = open_block(nc, ctx, made)
        n = WSTEPS

        @block.gpsimd
        def _(pool):
            pool.memset(mean[:, :], 1.0 / P).then_inc(ready, 1)
            pool.memset(eps[:, :], EPS).then_inc(ready, 1)
            pool.memset(center[:, :], -1.0 / P).then_inc(zero, 1)
            pool.wait_ge(zero, BASE + 1)
            pool.affine_select(out=center[:, :], in_=center[:, :], compare_op=ALU.not_equal, fill=1.0 - 1.0 / P,
                               base=0, pattern=[[-1, P]], channel_multiplier=1).then_inc(ready, 1)
            if add is not None:
                with pool.Fori(0, WTRIPS) as i:
                    for s in range(n):
                        at = ds((i * n + s) * WIDE, WIDE)
                        pool.tensor_tensor(src[:, at], src[:, at], add[:, at], ALU.add).then_inc(added, 1)

        @block.tensor
        def _(pe):
            pe.wait_ge(ready, BASE + 3)
            with pe.Fori(0, WTRIPS) as i:
                for s in range(n + 1):
                    if s < n:
                        if add is not None:
                            pe.wait_ge(added, BASE + i * n + s + 1)
                        pe.wait_ge(copied, BASE + i * n + (s - 1 if s >= 2 else 0))
                        pe.matmul(ps[:, s % 2, 0:WIDE], center[:, :], src[:, ds((i * n + s) * WIDE, WIDE)],
                                  start=True, stop=True).then_inc(centered, 1)
                    if s >= 1:
                        v = s - 1
                        pe.wait_ge(squared, BASE + i * n + v + 1)
                        pe.wait_ge(rooted, BASE + i * n + (v - 1 if v >= 2 else 0))
                        pe.matmul(ps[:, 2 + v % 2, 0:WIDE], mean[:, :], sq[:, v % 2, :],
                                  start=True, stop=True).then_inc(varied, 1)

        @block.scalar
        def _(act):
            with act.Fori(0, WTRIPS) as i:
                for s in range(n + 1):
                    if s < n:
                        act.wait_ge(copied, BASE + i * n + s + 1)
                        act.wait_ge(varied, BASE + i * n + (s - 1 if s >= 2 else 0))
                        act.activation(sq[:, s % 2, :], xc[:, s % 3, :], ACT.Square).then_inc(squared, 1)
                    if s >= 1:
                        v = s - 1
                        act.wait_ge(varied, BASE + i * n + v + 1)
                        act.wait_ge(inverted, BASE + i * n + (v - 1 if v >= 2 else 0))
                        act.activation(sd[:, v % 2, :], ps[:, 2 + v % 2, 0:WIDE], ACT.Sqrt,
                                       bias=eps[:, 0:1]).then_inc(rooted, 1)

        @block.vector
        def _(dve):
            with dve.Fori(0, WTRIPS) as i:
                for s in range(n + 2):
                    if s < n:
                        dve.wait_ge(centered, BASE + i * n + s + 1)
                        dve.wait_ge(squared, BASE + i * n + max(s - 2, 0))
                        dve.wait_ge(normed, BASE + i * n + max(s - 2, 0))
                        dve.tensor_copy(xc[:, s % 3, :], ps[:, s % 2, 0:WIDE]).then_inc(copied, 1)
                    if s >= 2:
                        v = s - 2
                        dve.wait_ge(rooted, BASE + i * n + v + 1)
                        dve.reciprocal(rs[:, v % 2, :], sd[:, v % 2, :]).then_inc(inverted, 1)
                        dve.wait_ge(inverted, BASE + i * n + v + 1)
                        dve.tensor_tensor(dst[:, ds((i * n + v) * WIDE, WIDE)], xc[:, v % 3, :], rs[:, v % 2, :],
                                          ALU.mult).then_inc(normed, 1)

        if spill:
            @block.sync
            def _(sp):
                sp.wait_ge(normed, BASE + WTRIPS * n)
                sp.dma_start(spill[0], src[:, :]).then_inc(spilled, 16)
                sp.dma_start(spill[1], dst[:, :]).then_inc(spilled, 16)
                sp.wait_ge(spilled, BASE + 32)


class Attention:

    def __init__(self, nc, ctx, make_sem, tag, C):
        sb = lambda name, shape: ctx.enter_context(nc.sbuf_tensor(tag + name, shape, F32))
        sem = lambda name: make_sem(tag + name)
        self.C, self.NH = C, P // HEAD
        self.per_unit = GROUP * C
        self.steps = 2 * self.per_unit
        self.x = sb("x", [P, 2, C, UNIT])
        self.q = sb("q", [P, 2, C, UNIT])
        self.k = sb("k", [P, 2, C, UNIT])
        self.km = sb("km", [P, 2, self.NH, SEQ])
        self.v = sb("v", [SEQ, 2 * GROUP, C * 4, 4, HEAD])
        self.p = sb("p", [SEQ, 4, self.NH, SEQ])
        self.pt = sb("pt", [SEQ, 2, self.NH, SEQ])
        self.o = sb("o", [P, 2, C, UNIT])
        self.mx = sb("mx", [SEQ, 2, self.NH])
        self.sm = sb("sm", [SEQ, 4, self.NH])
        self.ri = sb("ri", [SEQ, 4, self.NH])
        self.mask = sb("mask", [P, self.NH])
        (self.v_zeroed, self.mask_done, self.x_copied, self.keys_masked, self.scored, self.maxed, self.shifted,
         self.exped, self.summed, self.inverted, self.normed, self.turned, self.turn_kept, self.weighed,
         self.o_kept, self.piece_done, self.piece_kept) = [sem(n) for n in (
             "v_zeroed", "mask_done", "x_copied", "keys_masked", "scored", "maxed", "shifted", "exped", "summed",
             "inverted", "normed", "turned", "turn_kept", "weighed", "o_kept", "piece_done", "piece_kept")]
        unit = [("q", c) for c in range(C)] + [("k", c) for c in range(C)] + [("v", b) for b in range(GROUP)]
        at = {s: [] for s in range(-1, self.steps + 4)}
        at[-1] = [(kind, 0, m) for kind, m in unit]
        per = -(-len(unit) // self.per_unit)
        for n, (kind, m) in enumerate(unit):
            at[n // per].append((kind, 1, m))
        for unit_no in range(2):
            at[(unit_no + 1) * self.per_unit + 3] += [("o", unit_no, m) for m in range(C)]
        self.pieces_at = at
        order = [x for s in range(-1, self.steps + 4) for x in at[s]]
        self.index = {x: n for n, x in enumerate(order)}
        self.pieces = len(order)
        assert self.pieces % 2 == 0

    def step(self, s):
        return s // self.per_unit, s % self.per_unit // self.C, s % self.C

    def pool_setup(self, pool):
        pool.memset(self.v[:, :, :, :, :], 0.0).then_inc(self.v_zeroed, 1)
        pool.memset(self.mask[:, :], 1.0).then_inc(self.mask_done, 1)
        pool.wait_ge(self.mask_done, BASE + 1)
        pool.affine_select(out=self.mask[:, :], in_=self.mask[:, :], compare_op=ALU.is_ge, fill=0.0, base=0,
                           pattern=[[-HEAD, self.NH]], channel_multiplier=1).then_inc(self.mask_done, 1)
        pool.wait_ge(self.mask_done, BASE + 2)
        pool.affine_select(out=self.mask[:, :], in_=self.mask[:, :], compare_op=ALU.is_ge, fill=0.0, base=HEAD - 1,
                           pattern=[[HEAD, self.NH]], channel_multiplier=-1).then_inc(self.mask_done, 1)
        pool.wait_ge(self.mask_done, BASE + 3)

    def pool_trip(self, pool, trip, i, src, src_ready):
        n, C = self.steps, self.C
        if src_ready is not None:
            pool.wait_ge(src_ready[0], BASE + src_ready[1])
        pool.wait_ge(self.piece_done, BASE + trip * self.pieces)
        for u in range(2):
            for c in range(C):
                pool.tensor_copy(self.x[:, u, c, :],
                                 src[:, c, ds((i * 2 + u) * UNIT, UNIT)]).then_inc(self.x_copied, 1)
        for s in range(-1, n + 1):
            m = s + 1
            if m < n:
                u, b, c = self.step(m)
                pool.wait_ge(self.piece_kept, BASE + trip * self.pieces + self.index["k", u, c] + 1)
                pool.wait_ge(self.scored, BASE + trip * n + max(m - 1, 0))
                pool.tensor_tensor(
                    self.km[:, m % 2],
                    self.k[:, u, c, b * SEQ:(b + 1) * SEQ].unsqueeze(1).broadcast_to([P, self.NH, SEQ]),
                    self.mask[:, :].unsqueeze(2).broadcast_to([P, self.NH, SEQ]),
                    ALU.mult).then_inc(self.keys_masked, 1)
            if s >= 1:
                v = s - 1
                pool.wait_ge(self.inverted, BASE + trip * n + v + 1)
                pool.tensor_tensor(self.p[:, v % 4], self.p[:, v % 4],
                                   self.ri[:, v % 4, :].unsqueeze(2).broadcast_to([SEQ, self.NH, SEQ]),
                                   ALU.mult).then_inc(self.normed, 1)

    def pe_pieces(self, pe, trip, s, ps, w_in, w_out):
        C = self.C
        for kind, u, m in self.pieces_at[s]:
            n = self.index[kind, u, m]
            pe.wait_ge(self.piece_kept, BASE + trip * self.pieces + max(n - 1, 0))
            bank = ps[:, 6 + n % 2, :]
            if kind == "o":
                pe.wait_ge(self.o_kept, BASE + trip * self.steps + (u + 1) * self.per_unit)
            elif s < 0:
                pe.wait_ge(self.x_copied, BASE + (trip + 1) * 2 * C)
            for k in range(C):
                flags = dict(start=(k == 0), stop=(k == C - 1))
                if kind == "q" or kind == "k":
                    at = (m if kind == "q" else C + m) * P
                    mm = pe.matmul(bank[:, 0:UNIT], w_in[:, k, at:at + P], self.x[:, u, k, :], **flags)
                elif kind == "v":
                    mm = pe.matmul(bank[0:SEQ, 0:C * P], self.x[:, u, k, m * SEQ:(m + 1) * SEQ],
                                   w_in[:, k, 2 * C * P:3 * C * P], **flags)
                else:
                    mm = pe.matmul(bank[:, 0:UNIT], w_out[:, k, m * P:(m + 1) * P], self.o[:, u, k, :], **flags)
            mm.then_inc(self.piece_done, 1)

    def pe_trip(self, pe, trip, ps, w_in, w_out, ident):
        n, NH = self.steps, self.NH
        self.pe_pieces(pe, trip, -1, ps, w_in, w_out)
        for s in range(n + 4):
            if s < n:
                u, b, c = self.step(s)
                pe.wait_ge(self.piece_kept, BASE + trip * self.pieces + self.index["q", u, c] + 1)
                pe.wait_ge(self.keys_masked, BASE + trip * n + s + 1)
                pe.wait_ge(self.shifted, BASE + trip * n + s)
                for j in range(2):
                    mm = pe.matmul(ps[0:SEQ, j, 0:4 * SEQ], self.q[:, u, c, b * SEQ:(b + 1) * SEQ],
                                   self.km[:, s % 2, 4 * j:4 * j + 4, :], start=True, stop=True)
                mm.then_inc(self.scored, 1)
            self.pe_pieces(pe, trip, s, ps, w_in, w_out)
            if 2 <= s < n + 2:
                v = s - 2
                pe.wait_ge(self.normed, BASE + trip * n + v + 1)
                pe.wait_ge(self.turn_kept, BASE + trip * n + v)
                for h in range(NH):
                    mm = pe.transpose(ps[0:SEQ, 2 + h // 4, (h % 4) * SEQ:(h % 4 + 1) * SEQ],
                                      self.p[:, v % 4, h, :], ident[0:SEQ, 0:SEQ])
                mm.then_inc(self.turned, 1)
            if 3 <= s < n + 3:
                v = s - 3
                u, b, c = self.step(v)
                pe.wait_ge(self.turn_kept, BASE + trip * n + v + 1)
                pe.wait_ge(self.piece_kept, BASE + trip * self.pieces + self.index["v", u, b] + 1)
                pe.wait_ge(self.o_kept, BASE + trip * n + max(v - 1, 0))
                for odd in range(2):
                    for j in range(4):
                        mm = pe.matmul(
                            ps[32 * j:32 * j + 32, 4 + v % 2, 0:SEQ],
                            self.v[:, u * GROUP + b, 4 * c + j, 2 * odd:2 * odd + 2, :].rearrange("p a d -> p (a d)"),
                            self.pt[:, v % 2, 2 * j + odd, :], start=(odd == 0), stop=(odd == 1))
                mm.then_inc(self.weighed, 1)

    def dve_trip(self, dve, trip, ps):
        n, NH = self.steps, self.NH
        scores = ps[0:SEQ, 0:2, 0:4 * SEQ].rearrange("p a (h k) -> p a h k", k=SEQ)
        for s in range(n + 1):
            if s < n:
                dve.wait_ge(self.scored, BASE + trip * n + s + 1)
                dve.tensor_reduce(self.mx[:, s % 2, :].rearrange("p (a h) -> p a h", a=2), scores, AX.X,
                                  ALU.max).then_inc(self.maxed, 1)
                dve.wait_ge(self.maxed, BASE + trip * n + s + 1)
                dve.wait_ge(self.turned, BASE + trip * n + max(s - 3, 0))
                dve.tensor_tensor(
                    self.p[:, s % 4].rearrange("p (a h) k -> p a h k", a=2), scores,
                    self.mx[:, s % 2, :].rearrange("p (a h) -> p a h", a=2).unsqueeze(3)
                        .broadcast_to([SEQ, 2, NH // 2, SEQ]), ALU.subtract).then_inc(self.shifted, 1)
            if s >= 1:
                v = s - 1
                dve.wait_ge(self.exped, BASE + trip * n + v + 1)
                dve.tensor_reduce(self.sm[:, v % 4, :], self.p[:, v % 4], AX.X, ALU.add).then_inc(self.summed, 1)
                dve.wait_ge(self.summed, BASE + trip * n + v + 1)
                dve.reciprocal(self.ri[:, v % 4, :], self.sm[:, v % 4, :]).then_inc(self.inverted, 1)

    def act_pieces(self, act, trip, s, ps, bias_q, bias_o, store_o):
        C = self.C
        for kind, u, m in self.pieces_at[s]:
            n = self.index[kind, u, m]
            act.wait_ge(self.piece_done, BASE + trip * self.pieces + n + 1)
            bank = ps[:, 6 + n % 2, :]
            if kind == "q" or kind == "k":
                dst = (self.q if kind == "q" else self.k)[:, u, m, :]
                col = m if kind == "q" else C + m
                if bias_q is None:
                    op = act.copy(dst, bank[:, 0:UNIT])
                else:
                    op = act.activation(dst, bank[:, 0:UNIT], ACT.Identity, bias=bias_q[:, col:col + 1])
            elif kind == "v":
                if trip is not None and s < 0:
                    act.wait_ge(self.v_zeroed, BASE + 1)
                op = act.copy(self.v[:, u * GROUP + m, :, 0:4:3, :],
                              bank[0:SEQ, 0:C * P].rearrange("p (j a d) -> p j a d", a=2, d=HEAD))
            else:
                op = store_o(act, u, m, bank[:, 0:UNIT], bias_o[:, m:m + 1])
            op.then_inc(self.piece_kept, 1)

    def act_trip(self, act, trip, ps, bias_q, bias_o, store_o):
        n, NH = self.steps, self.NH
        self.act_pieces(act, trip, -1, ps, bias_q, bias_o, store_o)
        for s in range(n + 4):
            if s < n:
                act.wait_ge(self.shifted, BASE + trip * n + s + 1)
                act.activation(self.p[:, s % 4], self.p[:, s % 4], ACT.Exp, scale=SCALE).then_inc(self.exped, 1)
            self.act_pieces(act, trip, s, ps, bias_q, bias_o, store_o)
            if 2 <= s < n + 2:
                v = s - 2
                act.wait_ge(self.turned, BASE + trip * n + v + 1)
                act.wait_ge(self.weighed, BASE + trip * n + max(v - 1, 0))
                act.copy(self.pt[:, v % 2].rearrange("p (a h) k -> p a h k", a=2),
                         ps[0:SEQ, 2:4, 0:4 * SEQ].rearrange("p a (h k) -> p a h k", k=SEQ)).then_inc(self.turn_kept, 1)
            if 3 <= s < n + 3:
                v = s - 3
                u, b, c = self.step(v)
                act.wait_ge(self.weighed, BASE + trip * n + v + 1)
                act.copy(self.o[:, u, c, b * SEQ:(b + 1) * SEQ], ps[:, 4 + v % 2, 0:SEQ]).then_inc(self.o_kept, 1)


def first_attention_stage(nc, ps, io, z, out, ident):
    with ExitStack() as ctx:
        sb = lambda name, shape: ctx.enter_context(nc.sbuf_tensor(name, shape, F32))
        sem, made = semaphores(nc, ctx)
        att = Attention(nc, ctx, sem, "a1_", 1)
        rows = sb("a1_rows", [P, 4, HID])
        cols = sb("a1_cols", [P, 4, P])
        bias = sb("a1_bias", [P, 1])
        loaded, turned, kept = sem("a1_loaded"), sem("a1_w_turned"), sem("a1_w_kept")
        block = open_block(nc, ctx, made)
        w_in, w_out = cols[:, 0:3, :].rearrange("p a b -> p (a b)").unsqueeze(1), cols[:, 3:4, :]

        @block.sync
        def _(sp):
            sp.dma_start(rows[:, 0:3, :], io["w_qkv"].rearrange("(a p) d -> p a d", p=P)).then_inc(loaded, 16)
            sp.dma_start(rows[:, 3, :], io["w_agg"]).then_inc(loaded, 16)
            sp.dma_start(bias[:, :], io["b_agg"].rearrange("(p a) -> p a", a=1)).then_inc(loaded, 16)

        @block.gpsimd
        def _(pool):
            att.pool_setup(pool)
            with pool.Fori(0, PAIRS) as i:
                att.pool_trip(pool, i, i, z[:, :].unsqueeze(1), None)

        @block.tensor
        def _(pe):
            pe.wait_ge(loaded, BASE + 48)
            for a in range(4):
                m = pe.transpose(ps[:, 0, a * P:(a + 1) * P], rows[:, a, :], ident[:, :])
            m.then_inc(turned, 1)
            pe.wait_ge(kept, BASE + 1)
            with pe.Fori(0, PAIRS) as i:
                att.pe_trip(pe, i, ps, w_in, w_out, ident)

        @block.vector
        def _(dve):
            dve.wait_ge(turned, BASE + 1)
            dve.tensor_copy(cols[:, :, :], ps[:, 0, :].rearrange("p (a m) -> p a m", a=4)).then_inc(kept, 1)
            with dve.Fori(0, PAIRS) as i:
                att.dve_trip(dve, i, ps)

        @block.scalar
        def _(act):
            with act.Fori(0, PAIRS) as i:
                def store(act, u, m, bank, b):
                    return act.activation(out[:, ds((i * 2 + u) * UNIT, UNIT)], bank, ACT.Identity, bias=b)
                att.act_trip(act, i, ps, None, bias, store)


def front(nc, ps, io, h1_dram, z2_dram):
    with ExitStack() as ctx:
        sb = lambda name, shape: ctx.enter_context(nc.sbuf_tensor(name, shape, F32))
        ident = sb("ident", [P, P])
        h = sb("h", [P, TOKENS])
        tokens_stage(nc, ps, io, h, ident)
        z = sb("z", [P, TOKENS])
        attended = sb("attended", [P, TOKENS])
        norm_stage(nc, ps, "n1_", h, z, None, None)
        first_attention_stage(nc, ps, io, z, attended, ident)
        norm_stage(nc, ps, "n2_", h, z, attended, (h1_dram, z2_dram))


VECTORS = dict(b1=(0, KD), b2=(2, KD), g=(4, KD), beta=(6, KD), in_b=(8, 3 * KD), out_b=(14, KD))
NVEC = 16


def experts_stage(nc, ps, io, z2_dram, x_dram):
    with ExitStack() as ctx:
        sb = lambda name, shape: ctx.enter_context(nc.sbuf_tensor(name, shape, F32))
        sem, made = semaphores(nc, ctx)
        ident = sb("x_ident", [P, P])
        z = sb("x_z", [P, TOKENS])
        h = sb("x_h", [P, KD, TOKENS])
        xo = sb("x_out", [P, SEQ, KD, IMAGES])
        vec_rows = sb("x_vec_rows", [EXPERTS * NVEC, P])
        vec_all = sb("x_vec_all", [P, EXPERTS, NVEC])
        vec = sb("x_vec", [P, NVEC])
        raw_w1 = sb("raw_w1", [P, D])
        raw_w2 = sb("raw_w2", [P, KD, D])
        raw_in = sb("raw_in", [P, KD, 3 * D])
        raw_out = sb("raw_out", [P, KD, D])
        w1 = sb("w1", [P, D])
        w2 = sb("w2", [P, KD, D])
        w_in = sb("w_in", [P, KD, 3 * D])
        w_out = sb("w_out", [P, KD, D])
        row_sum = sb("row_sum", [P, KD])
        row_mean = sb("row_mean", [P, KD])
        b2_mean = sb("b2_mean", [P, 1])
        b2c = sb("b2c", [P, KD])
        in_b = sb("in_b", [P, 3 * KD])
        out_b = sb("out_b", [P, KD])
        mean = sb("x_mean", [P, P])
        eps = sb("x_eps", [P, 1])
        h1 = sb("x_h1", [P, 2, KD, WIDE])
        hc = sb("x_hc", [P, 2, KD, WIDE])
        sq = sb("x_sq", [P, 2, KD, WIDE])
        sd = sb("x_sd", [P, WIDE])
        rs = sb("x_rs", [P, WIDE])
        att = Attention(nc, ctx, sem, "ax_", KD)
        consts, z_in, id_zero, id_done, ones = (sem("x_consts"), sem("x_z_in"), sem("x_id_zero"), sem("x_id_done"),
                                                sem("x_ones"))
        vec_turned, vec_kept = sem("x_vec_turned"), sem("x_vec_kept")
        raw_loaded, prepared = sem("raw_loaded"), sem("prepared")
        prep_step, prep_sums = sem("prep_step"), sem("prep_sums")
        h1_done, h1_kept, h2_done, h2_kept = sem("h1_done"), sem("h1_kept"), sem("h2_done"), sem("h2_kept")
        squared, varied, rooted, inverted, h_ready = (sem("x_squared"), sem("x_varied"), sem("x_rooted"),
                                                      sem("x_inverted"), sem("x_h_ready"))
        saved = sem("x_saved")
        block = open_block(nc, ctx, made)
        n, STEPS = WSTEPS, WSTEPS * WTRIPS
        PREP = 16
        last_piece = 2 * att.pieces // 2

        @block.sync
        def _(sp):
            sp.dma_start(z[:, :], z2_dram).then_inc(z_in, 16)
            for name, key in (("b1", "enc_b1"), ("b2", "enc_b2"), ("g", "enc_g"), ("beta", "enc_beta"),
                              ("in_b", "attn_in_b"), ("out_b", "attn_out_b")):
                at, k = VECTORS[name]
                for e in range(EXPERTS):
                    row = e * NVEC + at
                    sp.dma_start(vec_rows[row:row + k, :],
                                 io[key][e].rearrange("(k p) -> k p", p=P)).then_inc(consts, 16)

            def load(e):
                sp.dma_start(raw_w1[:, :], io["enc_w1"][ds(e, 1)].rearrange("a k n -> (a k) n")).then_inc(raw_loaded, 16)
                for raw, name in ((raw_w2, "enc_w2"), (raw_in, "attn_in_w"), (raw_out, "attn_out_w")):
                    sp.dma_start(raw[:, :, :], io[name][ds(e, 1)].rearrange("a (k p) n -> p (a k) n", p=P)).then_inc(raw_loaded, 16)

            def save(e):
                sp.wait_ge(att.piece_kept, BASE + (e + 1) * PAIRS * att.pieces)
                sp.dma_start(x_dram[ds(e, 1)].rearrange("a t f k b -> f (a t) (k b)"),
                             xo[:, :, :, :].rearrange("p t k b -> p t (k b)")).then_inc(saved, 16)

            load(0)
            with sp.Fori(0, EXPERTS - 1) as e:
                sp.wait_ge(prepared, BASE + e + 1)
                load(e + 1)
                save(e)
            save(EXPERTS - 1)
            sp.wait_ge(saved, BASE + 16 * EXPERTS)

        @block.gpsimd
        def _(pool):
            make_identity(pool, ident, id_zero, id_done)
            pool.memset(mean[:, :], 1.0 / D).then_inc(ones, 1)
            pool.memset(eps[:, :], EPS).then_inc(ones, 1)
            pool.wait_ge(id_done, BASE + 1)
            pool.wait_ge(ones, BASE + 2)
            att.pool_setup(pool)
            with pool.Fori(0, EXPERTS) as e:
                with pool.Fori(0, PAIRS) as i:
                    att.pool_trip(pool, e * PAIRS + i, i, h, (h_ready, e * STEPS + STEPS))

        @block.tensor
        def _(pe):
            pe.wait_ge(z_in, BASE + 16)
            pe.wait_ge(ones, BASE + 2)
            pe.wait_ge(id_done, BASE + 1)
            pe.wait_ge(consts, BASE + 16 * EXPERTS * len(VECTORS))
            pe.transpose(ps[:, 0, 0:EXPERTS * NVEC], vec_rows[:, :],
                         ident[0:EXPERTS * NVEC, 0:EXPERTS * NVEC]).then_inc(vec_turned, 1)
            with pe.Fori(0, EXPERTS) as e:
                pe.wait_ge(raw_loaded, BASE + (e + 1) * 64)
                pe.wait_ge(prep_step, BASE + e * PREP + 1)
                at = VECTORS["b2"][0]
                pe.matmul(ps[:, 5, 0:KD], mean[:, :], vec[:, at:at + KD], start=True, stop=True).then_inc(prep_sums, 1)
                at = VECTORS["beta"][0]
                for m in range(3 * KD):
                    for k in range(KD):
                        mm = pe.matmul(ps[:, 6, m:m + 1], raw_in[:, k, m * P:(m + 1) * P], vec[:, at + k:at + k + 1],
                                       start=(k == 0), stop=(k == KD - 1))
                mm.then_inc(prep_sums, 1)
                pe.wait_ge(prep_step, BASE + e * PREP + 3)
                for m in range(KD):
                    for k in range(KD):
                        mm = pe.matmul(ps[:, 7, m:m + 1], raw_out[:, k, m * P:(m + 1) * P],
                                       in_b[:, 2 * KD + k:2 * KD + k + 1], start=(k == 0), stop=(k == KD - 1))
                mm.then_inc(prep_sums, 1)
                with pe.Fori(0, WTRIPS) as i:
                    base = e * STEPS + i * n
                    for s in range(n + 2):
                        if s == 0:
                            pe.wait_ge(prepared, BASE + e + 1)
                        if s < n:
                            pe.wait_ge(h1_kept, BASE + (base + s) * KD)
                            for m in range(KD):
                                pe.matmul(ps[:, m, 0:WIDE], w1[:, m * P:(m + 1) * P], z[:, ds((i * n + s) * WIDE, WIDE)],
                                          start=True, stop=True).then_inc(h1_done, 1)
                        if 1 <= s <= n:
                            v = s - 1
                            pe.wait_ge(h1_kept, BASE + (base + v + 1) * KD)
                            pe.wait_ge(h2_kept, BASE + (base + v) * KD)
                            for m in range(KD):
                                for k in range(KD):
                                    mm = pe.matmul(ps[:, 2 + m, 0:WIDE], w2[:, k, m * P:(m + 1) * P], h1[:, v % 2, k, :],
                                                   start=(k == 0), stop=(k == KD - 1))
                                mm.then_inc(h2_done, 1)
                        if s >= 2:
                            v = s - 2
                            pe.wait_ge(squared, BASE + base + v + 1)
                            pe.wait_ge(rooted, BASE + base + v)
                            for k in range(KD):
                                mm = pe.matmul(ps[:, 4, 0:WIDE], mean[:, :], sq[:, v % 2, k, :],
                                               start=(k == 0), stop=(k == KD - 1))
                            mm.then_inc(varied, 1)
                with pe.Fori(0, PAIRS) as i:
                    att.pe_trip(pe, e * PAIRS + i, ps, w_in, w_out, ident)

        @block.vector
        def _(dve):
            dve.wait_ge(vec_turned, BASE + 1)
            dve.tensor_copy(vec_all[:, :, :], ps[:, 0, 0:EXPERTS * NVEC].rearrange("p (e v) -> p e v", v=NVEC)).then_inc(vec_kept, 1)
            dve.wait_ge(vec_kept, BASE + 1)
            with dve.Fori(0, EXPERTS) as e:
                V = {name: vec[:, at:at + k] for name, (at, k) in VECTORS.items()}
                b = e * PREP
                dve.wait_ge(att.piece_kept, BASE + e * PAIRS * att.pieces)
                dve.wait_ge(raw_loaded, BASE + (e + 1) * 64)
                dve.tensor_copy(vec[:, :], vec_all[:, ds(e, 1), :].rearrange("p a v -> p (a v)")).then_inc(prep_step, 1)
                dve.tensor_reduce(row_sum[:, :], raw_w2[:, :, :], AX.X, ALU.add).then_inc(prep_step, 1)
                dve.wait_ge(prep_sums, BASE + e * 3 + 2)
                dve.wait_ge(prep_step, BASE + b + 2)
                dve.tensor_tensor(in_b[:, :], ps[:, 6, 0:3 * KD], V["in_b"], ALU.add).then_inc(prep_step, 1)
                dve.tensor_reduce(b2_mean[:, :], ps[:, 5, 0:KD], AX.X, ALU.add).then_inc(prep_step, 1)
                dve.tensor_scalar(row_mean[:, :], row_sum[:, :], 1.0 / D, None, ALU.mult).then_inc(prep_step, 1)
                dve.wait_ge(prep_step, BASE + b + 5)
                dve.tensor_scalar(b2c[:, :], V["b2"], b2_mean[:, 0:1], None, ALU.subtract).then_inc(prep_step, 1)
                for k in range(KD):
                    dve.tensor_scalar(w2[:, k, :], raw_w2[:, k, :], row_mean[:, k:k + 1], None,
                                      ALU.subtract).then_inc(prep_step, 1)
                for k in range(KD):
                    dve.tensor_scalar(w_in[:, k, :], raw_in[:, k, :], V["g"][:, k:k + 1], None,
                                      ALU.mult).then_inc(prep_step, 1)
                dve.tensor_copy(w1[:, :], raw_w1[:, :]).then_inc(prep_step, 1)
                dve.tensor_copy(w_out[:, :, :], raw_out[:, :, :]).then_inc(prep_step, 1)
                dve.wait_ge(prep_sums, BASE + e * 3 + 3)
                dve.tensor_tensor(out_b[:, :], ps[:, 7, 0:KD], V["out_b"], ALU.add).then_inc(prep_step, 1)
                dve.sem_inc(prep_step, PREP - 13)
                dve.wait_ge(prep_step, BASE + b + PREP)
                dve.sem_inc(prepared, 1)
                with dve.Fori(0, WTRIPS) as i:
                    base = e * STEPS + i * n
                    for s in range(n + 2):
                        if 1 <= s <= n:
                            v = s - 1
                            dve.wait_ge(squared, BASE + base + max(v - 1, 0))
                            dve.wait_ge(h_ready, BASE + base + max(v - 1, 0))
                            for m in range(KD):
                                dve.wait_ge(h2_done, BASE + (base + v) * KD + m + 1)
                                dve.tensor_scalar(hc[:, v % 2, m, :], ps[:, 2 + m, 0:WIDE], b2c[:, m:m + 1], None,
                                                  ALU.add).then_inc(h2_kept, 1)
                        if s >= 2:
                            v = s - 2
                            dve.wait_ge(rooted, BASE + base + v + 1)
                            dve.wait_ge(h_ready, BASE + base + v)
                            dve.reciprocal(rs[:, :], sd[:, :]).then_inc(inverted, 1)
                            dve.wait_ge(inverted, BASE + base + v + 1)
                            dve.tensor_tensor(h[:, :, ds((i * n + v) * WIDE, WIDE)], hc[:, v % 2],
                                              rs[:, :].unsqueeze(1).broadcast_to([P, KD, WIDE]),
                                              ALU.mult).then_inc(h_ready, 1)
                with dve.Fori(0, PAIRS) as i:
                    att.dve_trip(dve, e * PAIRS + i, ps)

        @block.scalar
        def _(act):
            with act.Fori(0, EXPERTS) as e:
                act.wait_ge(prepared, BASE + e + 1)
                at = VECTORS["b1"][0]
                with act.Fori(0, WTRIPS) as i:
                    base = e * STEPS + i * n
                    for s in range(n + 2):
                        if s < n:
                            for m in range(KD):
                                act.wait_ge(h1_done, BASE + (base + s) * KD + m + 1)
                                act.wait_ge(h2_done, BASE + (base + max(s - 1, 0)) * KD)
                                act.activation(h1[:, s % 2, m, :], ps[:, m, 0:WIDE], ACT.Relu,
                                               bias=vec[:, at + m:at + m + 1]).then_inc(h1_kept, 1)
                        if 1 <= s <= n:
                            v = s - 1
                            act.wait_ge(h2_kept, BASE + (base + v + 1) * KD)
                            act.wait_ge(varied, BASE + base + max(v - 1, 0))
                            act.activation(sq[:, v % 2], hc[:, v % 2], ACT.Square).then_inc(squared, 1)
                        if s >= 2:
                            v = s - 2
                            act.wait_ge(varied, BASE + base + v + 1)
                            act.wait_ge(inverted, BASE + base + v)
                            act.activation(sd[:, :], ps[:, 4, 0:WIDE], ACT.Sqrt, bias=eps[:, 0:1]).then_inc(rooted, 1)
                act.wait_ge(saved, BASE + e * 16)
                with act.Fori(0, PAIRS) as i:
                    def store(act, u, m, bank, b):
                        dst = xo[:, :, m, ds((i * 2 + u) * GROUP, GROUP)].rearrange("p t b -> p b t")
                        return act.activation(dst, bank.rearrange("p (b t) -> p b t", t=SEQ), ACT.Identity, bias=b)
                    att.act_trip(act, e * PAIRS + i, ps, in_b, out_b, store)


def lstm_stage(nc, ps, io, x_dram, mem_dram):
    HALF = IMAGES
    G4 = 4 * D
    COLUMNS = ((0, 0, 2 * D), (2 * D, 3 * D, D), (3 * D, 2 * D, D))
    WLOADS = 2 * 2 * EXPERTS * len(COLUMNS)
    TRIPS = (SEQ - 1) // 2
    with ExitStack() as ctx:
        sb = lambda name, shape: ctx.enter_context(nc.sbuf_tensor(name, shape, F32))
        sem, made = semaphores(nc, ctx)
        ident = sb("l_ident", [P, P])
        w = sb("l_w", [P, EXPERTS, 2, 2 * KD, G4])
        bias = sb("l_bias", [P, EXPERTS, G4])
        xs = sb("l_x", [P, 2, 2, EXPERTS, KD, IMAGES])
        hT = sb("l_hT", [P, EXPERTS, 2, KD, IMAGES])
        cell = sb("l_cell", [P, EXPERTS, D])
        gates = sb("l_gates", [P, 2, G4])
        ig = sb("l_ig", [P, D])
        tc = sb("l_tc", [P, D])
        hid = sb("l_hid", [P, 2, D])
        w_in, bias_in = sem("l_w_in"), sem("l_bias_in")
        id_zero, id_done = sem("l_id_zero"), sem("l_id_done")
        x_in = [[sem(f"l_x_in{q}{d}") for d in range(2)] for q in range(2)]
        summed, biased, gated, ig_done, fc_done, cell_done, squashed, h_done, turned, hT_done = [
            sem("l_" + s) for s in ("summed", "biased", "gated", "ig_done", "fc_done", "cell_done", "squashed",
                                    "h_done", "turned", "hT_done")]
        saved = [sem(f"l_saved{e}") for e in range(EXPERTS)]
        block = open_block(nc, ctx, made)

        def load_x(sp, t, q, products):
            sp.wait_ge(summed, BASE + products)
            for d in range(2):
                pos = t if d == 0 else SEQ - 1 - t
                src = x_dram[:, ds(pos, 1)].rearrange("e a f k b -> f (e a) (k b)")
                sp.dma_start(xs[:, q, d].rearrange("p e k b -> p e (k b)"), src).then_inc(x_in[q][d], 16)

        def save_h(sp, t, e):
            sp.wait_ge(hT_done, BASE + t * EXPERTS + e + 1)
            for d in range(2):
                pos = t if d == 0 else SEQ - 1 - t
                sp.dma_start(mem_dram[e, d][ds(pos, 1)].rearrange("a f k b -> f (a k b)"),
                             hT[:, e, d].rearrange("p k b -> p (k b)")).then_inc(saved[e], 16)

        @block.sync
        def _(sp):
            load_x(sp, 0, 0, 0)
            for d, name in enumerate(("lstm_b_f", "lstm_b_b")):
                for e in range(EXPERTS):
                    for to, frm, width in COLUMNS:
                        sp.dma_start(bias[d * HALF:(d + 1) * HALF, e, to:to + width],
                                     io[name][e, frm:frm + width].partition_broadcast(HALF)).then_inc(bias_in, 16)
            for d, (wi, wh) in enumerate((("lstm_wi_f", "lstm_wh_f"), ("lstm_wi_b", "lstm_wh_b"))):
                for j, name in enumerate((wi, wh)):
                    for e in range(EXPERTS):
                        src = io[name][e].rearrange("(k p) n -> p k n", p=P)
                        dst = w[:, e, d, KD * j:KD * j + KD, :]
                        for to, frm, width in COLUMNS:
                            sp.dma_start(dst[:, :, to:to + width], src[:, :, frm:frm + width]).then_inc(w_in, 16)
            load_x(sp, 1, 1, 0)
            for e in range(EXPERTS):
                save_h(sp, 0, e)

            def trip(i, last):
                for r in range(2):
                    t = i * 2 + 1 + r
                    if not (last and r == 1):
                        load_x(sp, t + 1, r, t * EXPERTS)
                    for e in range(EXPERTS):
                        save_h(sp, t, e)

            with sp.Fori(0, TRIPS - 1) as i:
                trip(i, False)
            trip(TRIPS - 1, True)
            for e in range(EXPERTS):
                sp.wait_ge(saved[e], BASE + SEQ * 32)

        @block.gpsimd
        def _(pool):
            make_identity(pool, ident, id_zero, id_done)

        @block.tensor
        def _(pe):
            def products(t, e, first):
                v = t * EXPERTS + e
                z = v % 2 if first else e % 2
                if not first or e >= 2:
                    pe.wait_ge(biased, BASE + v - 1)
                for kk in range(2 * KD):
                    if kk == KD and first:
                        break
                    if kk == KD:
                        pe.wait_ge(hT_done, BASE + v - EXPERTS + 1)
                    for n in range(2):
                        for d in range(2):
                            lhsT = xs[:, PAR(t, first), d, e, kk, :] if kk < KD else hT[:, e, d, kk - KD, :]
                            mm = pe.matmul(ps[d * HALF:(d + 1) * HALF, 2 * z + n, :], lhsT,
                                           w[:, e, d, kk, n * 512:(n + 1) * 512], start=(kk == 0),
                                           stop=(kk == (KD if first else 2 * KD) - 1))
                mm.then_inc(summed, 1)

            def turn(v, par):
                pe.wait_ge(h_done, BASE + v + 1)
                for k in range(KD):
                    mm = pe.transpose(ps[:, 6 + par, k * P:(k + 1) * P], hid[:, par, k * P:(k + 1) * P], ident[:, :])
                mm.then_inc(turned, 1)

            PAR = lambda t, first: 0 if first else parity[0]
            parity = [0]
            pe.wait_ge(w_in, BASE + 16 * WLOADS)
            pe.wait_ge(id_done, BASE + 1)
            for d in range(2):
                pe.wait_ge(x_in[0][d], BASE + 16)
            for e in range(EXPERTS):
                products(0, e, True)
                if e:
                    if e >= 3:
                        pe.wait_ge(hT_done, BASE + e - 2)
                    turn(e - 1, (e - 1) % 2)
            with pe.Fori(0, TRIPS) as i:
                for r in range(2):
                    t, parity[0] = i * 2 + 1 + r, 1 - r
                    for d in range(2):
                        pe.wait_ge(x_in[1 - r][d], BASE + (i + 1 + r) * 16)
                    for e in range(EXPERTS):
                        v = t * EXPERTS + e
                        products(t, e, False)
                        pe.wait_ge(hT_done, BASE + v - 2)
                        turn(v - 1, (e - 1) % 2)
            turn(SEQ * EXPERTS - 1, 1)

        @block.vector
        def _(dve):
            dve.wait_ge(bias_in, BASE + 16 * 2 * EXPERTS * len(COLUMNS))

            def update(t, e, first):
                v, z = t * EXPERTS + e, e % 2
                gz = gates[:, z, :]
                dve.wait_ge(summed, BASE + v + 1)
                if not first or e >= 2:
                    dve.wait_ge(h_done, BASE + v - 1)
                dve.tensor_tensor(gz.rearrange("p (n c) -> p n c", n=2), ps[:, 2 * z:2 * z + 2, :],
                                  bias[:, e, :].rearrange("p (n c) -> p n c", n=2), ALU.add).then_inc(biased, 1)
                dve.wait_ge(gated, BASE + (v + 1) * 2)
                if first:
                    dve.tensor_tensor(cell[:, e, :], gz[:, 0:D], gz[:, 3 * D:4 * D], ALU.mult).then_inc(cell_done, 1)
                else:
                    dve.tensor_tensor(ig[:, :], gz[:, 0:D], gz[:, 3 * D:4 * D], ALU.mult).then_inc(ig_done, 1)
                    dve.tensor_tensor(cell[:, e, :], gz[:, D:2 * D], cell[:, e, :], ALU.mult).then_inc(fc_done, 1)
                    dve.wait_ge(ig_done, BASE + v - EXPERTS + 1)
                    dve.wait_ge(fc_done, BASE + v - EXPERTS + 1)
                    dve.tensor_tensor(cell[:, e, :], cell[:, e, :], ig[:, :], ALU.add).then_inc(cell_done, 1)
                dve.wait_ge(squashed, BASE + v + 1)
                if not first or e >= 2:
                    dve.wait_ge(turned, BASE + v - 1)
                dve.tensor_tensor(hid[:, z, :], gz[:, 2 * D:3 * D], tc[:, :], ALU.mult).then_inc(h_done, 1)

            for e in range(EXPERTS):
                update(0, e, True)
            with dve.Fori(0, TRIPS) as i:
                for r in range(2):
                    for e in range(EXPERTS):
                        update(i * 2 + 1 + r, e, False)

        @block.scalar
        def _(act):
            def keep_h(v, e, t):
                act.wait_ge(turned, BASE + v + 1)
                if t is not None:
                    act.wait_ge(saved[e], BASE + t * 32)
                act.copy(hT[:, e], ps[:, 6 + e % 2, 0:2 * P].rearrange("p (k d b) -> p d k b", k=KD, d=2)).then_inc(hT_done, 1)

            def squash(t, e):
                v, z = t * EXPERTS + e, e % 2
                act.wait_ge(biased, BASE + v + 1)
                act.activation(gates[:, z, 0:3 * D], gates[:, z, 0:3 * D], ACT.Sigmoid).then_inc(gated, 1)
                act.activation(gates[:, z, 3 * D:4 * D], gates[:, z, 3 * D:4 * D], ACT.Tanh).then_inc(gated, 1)
                act.wait_ge(cell_done, BASE + v + 1)
                act.wait_ge(h_done, BASE + v)
                act.activation(tc[:, :], cell[:, e, :], ACT.Tanh).then_inc(squashed, 1)

            for e in range(EXPERTS):
                if e:
                    keep_h(e - 1, e - 1, None)
                squash(0, e)
            with act.Fori(0, TRIPS) as i:
                for r in range(2):
                    t = i * 2 + 1 + r
                    for e in range(EXPERTS):
                        keep_h(t * EXPERTS + e - 1, (e - 1) % EXPERTS, t if e else t - 1)
                        squash(t, e)
            keep_h(SEQ * EXPERTS - 1, EXPERTS - 1, SEQ - 1)


HEAD_VECTORS = dict(sig_b1=(0, KD), sig_b2=(2, KD), tan_b1=(4, KD), tan_b2=(6, KD), dec_b1=(8, KD), dec_b2=(10, 1),
                    dec_g=(11, 1), dec_beta=(12, 1))
NHEAD = 13


def head_stage(nc, ps, io, h1_dram, z2_dram, mem_dram, out):
    TC = 5
    W = TC * IMAGES
    CHUNKS = SEQ // TC
    with ExitStack() as ctx:
        sb = lambda name, shape: ctx.enter_context(nc.sbuf_tensor(name, shape, F32))
        sem, made = semaphores(nc, ctx)
        ident = sb("h_ident", [P, P])
        h1 = sb("h_h1", [P, TOKENS])
        z2 = sb("h_z2", [P, TOKENS])
        s1 = sb("h_s1", [P, EXPERTS, 2 * KD, D])
        t1 = sb("h_t1", [P, EXPERTS, 2 * KD, D])
        s2 = sb("h_s2", [P, EXPERTS, KD, D])
        t2 = sb("h_t2", [P, EXPERTS, KD, D])
        d1 = sb("h_d1", [P, EXPERTS, KD, D])
        d2 = sb("h_d2", [P, EXPERTS, KD, P])
        d2_sum = sb("h_d2_sum", [P, EXPERTS, KD])
        d2_mean = sb("h_d2_mean", [P, EXPERTS, KD])
        vec_rows = sb("h_vec_rows", [EXPERTS * NHEAD, P])
        vec = sb("h_vec", [P, EXPERTS, NHEAD])
        b2c = sb("h_b2c", [P, EXPERTS])
        rw = sb("h_rw", [P, EXPERTS])
        rwb = sb("h_rwb", [P, EXPERTS, P])
        rb = sb("h_rb", [P, EXPERTS])
        mean = sb("h_mean", [P, P])
        eps = sb("h_eps", [P, 1])
        mem = sb("h_mem", [P, 2, 2, TC, KD, IMAGES])
        rs1 = sb("h_rs1", [P, KD, W])
        rt1 = sb("h_rt1", [P, KD, W])
        gs = sb("h_gs", [P, KD, W])
        gt = sb("h_gt", [P, KD, W])
        gg = sb("h_gg", [P, KD, W])
        rd1 = sb("h_rd1", [P, KD, W])
        dc = sb("h_dc", [P, EXPERTS, W])
        sq = sb("h_sq", [P, W])
        var = sb("h_var", [P, EXPERTS, W])
        sd = sb("h_sd", [P, EXPERTS, W])
        inv = sb("h_inv", [P, EXPERTS, W])
        y = sb("h_y", [P, EXPERTS, W])
        PAIRS_OUT = -(-TC // 2)
        acc = sb("h_acc", [P, PAIRS_OUT * P])
        lg = sb("h_lg", [P, EXPERTS, W])
        lmax = sb("h_lmax", [P, W])
        lsum = sb("h_lsum", [P, W])
        linv = sb("h_linv", [P, W])
        rows = sb("h_rows", [P, PAIRS_OUT, P])
        names = ("s1_done s1_kept t1_done t1_kept s2_done s2_kept t2_done t2_kept d1_done d1_kept d2_done d2_kept "
                 "squared var_done var_kept gated logits logits_kept lmaxed lshifted lexped lsummed linverted lweighed "
                 "rooted inverted normed scaled stepped mixed turned rows_kept")
        S = {n: sem("h_" + n) for n in names.split()}
        w_in, v_in, r_in, id_zero, id_done, ones, prep, prep_pe = [
            sem("h_" + n) for n in ("w_in", "v_in", "r_in", "id_zero", "id_done", "ones", "prep", "prep_pe")]
        mem_in = [sem(f"h_mem_in{q}") for q in range(2)]
        out_done, vec_turned, vec_kept = sem("h_out_done"), sem("h_vec_turned"), sem("h_vec_kept")
        block = open_block(nc, ctx, made)
        E = EXPERTS
        tiles = lambda a: a.rearrange("p (t b) -> p t b", b=IMAGES)
        major = lambda a: a.rearrange("p (b s) -> p s b", s=SEQ)

        @block.sync
        def _(sp):
            for name, (at, k) in HEAD_VECTORS.items():
                for e in range(E):
                    row = e * NHEAD + at
                    sp.dma_start(vec_rows[row:row + k, :],
                                 io[name][e].rearrange("(k p) -> k p", p=P)).then_inc(v_in, 16)
            sp.dma_start(rw[:, :], io["router_w"]).then_inc(v_in, 16)
            sp.dma_start(rb[:, :], io["router_b"].partition_broadcast(P)).then_inc(v_in, 16)
            for dst, name in ((s1, "sig_w1"), (t1, "tan_w1"), (s2, "sig_w2"), (t2, "tan_w2"), (d1, "dec_w1"), (d2, "dec_w2")):
                sp.dma_start(dst[:, :, :, :].rearrange("p e k n -> p (e k) n"),
                             io[name].rearrange("e (k p) n -> p (e k) n", p=P)).then_inc(w_in, 16)
            sp.dma_start(h1[:, :], h1_dram).then_inc(r_in, 16)
            sp.dma_start(z2[:, :], z2_dram).then_inc(r_in, 16)
            with sp.Fori(0, CHUNKS) as c:
                for e in range(E):
                    sp.wait_ge(S["t1_done"], BASE + max(e - 1, 0) * KD + c * E * KD)
                    for d in range(2):
                        sp.dma_start(mem[:, e % 2, d].rearrange("p t k b -> p t (k b)"),
                                     mem_dram[e, d][ds(c * TC, TC)].rearrange("t f k b -> f t (k b)")).then_inc(mem_in[e % 2], 16)

        @block.gpsimd
        def _(pool):
            make_identity(pool, ident, id_zero, id_done)
            pool.memset(mean[:, :], 1.0 / P).then_inc(ones, 1)
            pool.memset(eps[:, :], EPS).then_inc(ones, 1)
            pool.memset(acc[:, :], 0.0).then_inc(ones, 1)
            pool.wait_ge(ones, BASE + 3)
            pool.wait_ge(v_in, BASE + 16 * (E * len(HEAD_VECTORS) + 2))
            pool.wait_ge(r_in, BASE + 32)
            pool.wait_ge(id_done, BASE + 1)

            def mix(c):
                for e in range(E):
                    n = c * E + e
                    pool.wait_ge(S["scaled"], BASE + n + 1)
                    if e == 0:
                        pool.wait_ge(S["turned"], BASE + c)
                        pool.tensor_tensor(tiles(acc[:, 0:W]), tiles(y[:, e, :]),
                                           major(h1[:, :])[:, ds(c * TC, TC), :], ALU.add).then_inc(S["stepped"], 1)
                    else:
                        pool.tensor_tensor(acc[:, 0:W], acc[:, 0:W], y[:, e, :], ALU.add).then_inc(S["stepped"], 1)
                    pool.wait_ge(S["stepped"], BASE + n + 1)
                pool.sem_inc(S["mixed"], 1)

            with pool.Fori(0, CHUNKS) as c:
                mix(c)

        @block.tensor
        def _(pe):
            pe.wait_ge(ones, BASE + 2)
            pe.wait_ge(v_in, BASE + 16 * (E * len(HEAD_VECTORS) + 2))
            pe.wait_ge(id_done, BASE + 1)
            pe.transpose(ps[:, 1, 0:E * NHEAD], vec_rows[:, :],
                         ident[0:E * NHEAD, 0:E * NHEAD]).then_inc(vec_turned, 1)
            pe.wait_ge(vec_kept, BASE + 1)
            for e in range(E):
                at, _ = HEAD_VECTORS["dec_b2"]
                mm = pe.matmul(ps[:, 0, e:e + 1], mean[:, :], vec[:, e, at:at + 1], start=True, stop=True)
            mm.then_inc(prep_pe, 1)
            pe.wait_ge(w_in, BASE + 96)
            pe.wait_ge(prep, BASE + 8 + 2)
            pe.wait_ge(r_in, BASE + 32)
            pe.wait_ge(id_done, BASE + 1)

            def group(c, e, done, banks, stat, moving, nk, extra=()):
                for m, bank in enumerate(banks):
                    for k in range(nk):
                        mm = pe.matmul(ps[:, bank, 0:W], stat(k, m), moving(k), start=(k == 0), stop=(k == nk - 1))
                    mm.then_inc(S[done], 1)

            def chunk(c, first):
                for e in range(E + 1):
                    n, p = c * E + e, c * E + e - 1
                    live, prev = e < E, e >= 1
                    if live:
                        q = e % 2
                        pe.wait_ge(mem_in[q], BASE + (c * 2 + e // 2 + 1) * 32)
                        mv = lambda k, q=q: mem[:, q, k // KD, :, k % KD, :]
                        pe.wait_ge(S["s1_kept"], BASE + n * KD)
                        pe.wait_ge(S["logits_kept"], BASE + c * E)
                        group(c, e, "s1_done", (0, 1), lambda k, m: s1[:, e, k, m * P:(m + 1) * P], mv, 2 * KD)
                    if prev:
                        pe.wait_ge(S["gated"], BASE + p + 1)
                        pe.wait_ge(S["d2_kept"], BASE + p)
                        pe.wait_ge(S["var_kept"], BASE + p)
                        group(c, e - 1, "d1_done", (6, 7), lambda k, m: d1[:, e - 1, k, m * P:(m + 1) * P],
                              lambda k: gg[:, k, :], KD)
                    if live:
                        pe.wait_ge(S["t1_kept"], BASE + n * KD)
                        group(c, e, "t1_done", (2, 3), lambda k, m: t1[:, e, k, m * P:(m + 1) * P], mv, 2 * KD)
                    if prev:
                        pe.wait_ge(S["d1_kept"], BASE + (p + 1) * KD)
                        group(c, e - 1, "d2_done", (6,), lambda k, m: d2[:, e - 1, k, :], lambda k: rd1[:, k, :], KD)
                    if live:
                        pe.wait_ge(S["s1_kept"], BASE + (n + 1) * KD)
                        pe.wait_ge(S["t2_kept"], BASE + n * KD)
                        pe.wait_ge(S["rows_kept"], BASE + c)
                        group(c, e, "s2_done", (4, 5), lambda k, m: s2[:, e, k, m * P:(m + 1) * P],
                              lambda k: rs1[:, k, :], KD)
                    if prev:
                        pe.wait_ge(S["squared"], BASE + p + 1)
                        group(c, e - 1, "var_done", (7,), lambda k, m: mean[:, :], lambda k: sq[:, :], 1)
                    if live:
                        pe.wait_ge(S["t1_kept"], BASE + (n + 1) * KD)
                        pe.wait_ge(S["s2_kept"], BASE + (n + 1) * KD)
                        group(c, e, "t2_done", (4, 5), lambda k, m: t2[:, e, k, m * P:(m + 1) * P],
                              lambda k: rt1[:, k, :], KD)
                pe.wait_ge(S["t1_kept"], BASE + (c + 1) * E * KD)
                pe.wait_ge(S["s1_kept"], BASE + (c + 1) * E * KD)
                for e in range(E):
                    pe.matmul(ps[:, e, 0:W], rwb[:, e, :], major(z2[:, :])[:, ds(c * TC, TC), :],
                              start=True, stop=True).then_inc(S["logits"], 1)

            def turn_out(c):
                pe.wait_ge(S["mixed"], BASE + c + 1)
                pe.wait_ge(S["t2_kept"], BASE + (c + 1) * E * KD)
                for j in range(PAIRS_OUT):
                    mm = pe.transpose(ps[:, 4, j * P:(j + 1) * P], acc[:, j * P:(j + 1) * P], ident[:, :])
                mm.then_inc(S["turned"], 1)

            with pe.Fori(0, CHUNKS) as c:
                chunk(c, False)
                turn_out(c)

        @block.vector
        def _(dve):
            dve.wait_ge(vec_turned, BASE + 1)
            dve.tensor_copy(vec[:, :, :], ps[:, 1, 0:E * NHEAD].rearrange("p (e v) -> p e v", v=NHEAD)).then_inc(vec_kept, 1)
            dve.wait_ge(v_in, BASE + 16 * (E * len(HEAD_VECTORS) + 2))
            dve.tensor_copy(rwb[:, :, :], rw[:, :].unsqueeze(2).broadcast_to([P, E, P])).then_inc(prep, 1)
            dve.wait_ge(prep_pe, BASE + 1)
            at, _ = HEAD_VECTORS["dec_b2"]
            dve.tensor_tensor(b2c[:, :], vec[:, :, at], ps[:, 0, 0:E], ALU.subtract).then_inc(prep, 1)
            dve.wait_ge(w_in, BASE + 96)
            dve.tensor_reduce(d2_sum[:, :, :], d2[:, :, :, :], AX.X, ALU.add).then_inc(prep, 1)
            dve.wait_ge(prep, BASE + 3)
            dve.tensor_scalar(d2_mean[:, :, :], d2_sum[:, :, :], 1.0 / P, None, ALU.mult).then_inc(prep, 1)
            dve.wait_ge(prep, BASE + 4)
            dve.tensor_tensor(d2[:, :, :, :], d2[:, :, :, :], d2_mean[:, :, :].unsqueeze(3).broadcast_to([P, E, KD, P]),
                              ALU.subtract).then_inc(prep, 6)

            def relu(c, e, done, kept, banks, dst, name):
                at, _ = HEAD_VECTORS[name]
                n = c * E + e
                for m, bank in enumerate(banks):
                    dve.wait_ge(S[done], BASE + n * KD + m + 1)
                    dve.tensor_scalar(dst[:, m, :], ps[:, bank, 0:W], vec[:, e, at + m:at + m + 1], 0.0,
                                      ALU.add, ALU.max).then_inc(S[kept], 1)

            def chunk(c):
                for e in range(E + 1):
                    live, prev = e < E, e >= 1
                    n, p = c * E + e, c * E + e - 1
                    if prev:
                        relu(c, e - 1, "d1_done", "d1_kept", (6, 7), rd1, "dec_b1")
                    if live:
                        dve.wait_ge(S["t2_done"], BASE + n * KD)
                        relu(c, e, "t1_done", "t1_kept", (2, 3), rt1, "tan_b1")
                    if prev:
                        dve.wait_ge(S["d2_done"], BASE + p + 1)
                        dve.tensor_scalar(dc[:, e - 1, :], ps[:, 6, 0:W], b2c[:, e - 1:e], None,
                                          ALU.add).then_inc(S["d2_kept"], 1)
                        dve.wait_ge(S["var_done"], BASE + p + 1)
                        dve.tensor_copy(var[:, e - 1, :], ps[:, 7, 0:W]).then_inc(S["var_kept"], 1)
                    if live:
                        dve.wait_ge(S["t2_kept"], BASE + (n + 1) * KD)
                        dve.tensor_tensor(gg[:, :, :], gs[:, :, :], gt[:, :, :], ALU.mult).then_inc(S["gated"], 1)
                dve.wait_ge(S["mixed"], BASE + c)
                for e in range(E):
                    dve.wait_ge(S["logits"], BASE + c * E + e + 1)
                    dve.tensor_scalar(lg[:, e, :], ps[:, e, 0:W], rb[:, e:e + 1], None, ALU.add).then_inc(S["logits_kept"], 1)
                over = lg[:, :, :].rearrange("p e w -> p w e")
                all_ = lambda a: a[:, :].unsqueeze(1).broadcast_to([P, E, W])
                dve.wait_ge(S["logits_kept"], BASE + (c + 1) * E)
                dve.tensor_reduce(lmax[:, :], over, AX.X, ALU.max).then_inc(S["lmaxed"], 1)
                dve.wait_ge(S["lmaxed"], BASE + c + 1)
                dve.tensor_tensor(lg[:, :, :], lg[:, :, :], all_(lmax), ALU.subtract).then_inc(S["lshifted"], 1)
                dve.wait_ge(S["lexped"], BASE + c + 1)
                dve.tensor_reduce(lsum[:, :], over, AX.X, ALU.add).then_inc(S["lsummed"], 1)
                dve.wait_ge(S["lsummed"], BASE + c + 1)
                dve.reciprocal(linv[:, :], lsum[:, :]).then_inc(S["linverted"], 1)
                dve.wait_ge(S["linverted"], BASE + c + 1)
                dve.tensor_tensor(lg[:, :, :], lg[:, :, :], all_(linv), ALU.mult).then_inc(S["lweighed"], 1)

            def scale(c):
                for e in range(E):
                    n = c * E + e
                    dve.wait_ge(S["rooted"], BASE + c + 1)
                    dve.reciprocal(inv[:, e, :], sd[:, e, :]).then_inc(S["inverted"], 1)
                    dve.wait_ge(S["inverted"], BASE + n + 1)
                    dve.wait_ge(S["mixed"], BASE + c)
                    at, _ = HEAD_VECTORS["dec_g"]
                    dve.scalar_tensor_tensor(out=y[:, e, :], in0=dc[:, e, :], scalar=vec[:, e, at:at + 1],
                                             in1=inv[:, e, :], op0=ALU.mult, op1=ALU.mult).then_inc(S["normed"], 1)
                    dve.wait_ge(S["normed"], BASE + n + 1)
                    dve.scalar_tensor_tensor(out=y[:, e, :], in0=y[:, e, :], scalar=vec[:, e, at + 1:at + 2],
                                             in1=lg[:, e, :], op0=ALU.add, op1=ALU.mult).then_inc(S["scaled"], 1)

            with dve.Fori(0, CHUNKS) as c:
                chunk(c)
                scale(c)

        @block.scalar
        def _(act):
            def leave(c, e, done, kept, banks, dst, name, func):
                at, _ = HEAD_VECTORS[name]
                n = c * E + e
                for m, bank in enumerate(banks):
                    act.wait_ge(S[done], BASE + n * KD + m + 1)
                    act.activation(dst[:, m, :], ps[:, bank, 0:W], func, bias=vec[:, e, at + m:at + m + 1]).then_inc(S[kept], 1)

            def chunk(c):
                for e in range(E + 1):
                    live, prev = e < E, e >= 1
                    n, p = c * E + e, c * E + e - 1
                    if live:
                        leave(c, e, "s1_done", "s1_kept", (0, 1), rs1, "sig_b1", ACT.Relu)
                    if prev:
                        act.wait_ge(S["d2_kept"], BASE + p + 1)
                        act.wait_ge(S["var_done"], BASE + p)
                        act.activation(sq[:, :], dc[:, e - 1, :], ACT.Square).then_inc(S["squared"], 1)
                    if live:
                        act.wait_ge(S["gated"], BASE + n)
                        leave(c, e, "s2_done", "s2_kept", (4, 5), gs, "sig_b2", ACT.Sigmoid)
                        leave(c, e, "t2_done", "t2_kept", (4, 5), gt, "tan_b2", ACT.Tanh)
                act.wait_ge(S["lshifted"], BASE + c + 1)
                act.activation(lg[:, :, :], lg[:, :, :], ACT.Exp).then_inc(S["lexped"], 1)

            def finish(c):
                act.wait_ge(S["var_kept"], BASE + (c + 1) * E)
                act.wait_ge(S["inverted"], BASE + c * E)
                act.activation(sd[:, :, :], var[:, :, :], ACT.Sqrt, bias=eps[:, 0:1]).then_inc(S["rooted"], 1)

            def rows_out(c):
                act.wait_ge(S["turned"], BASE + c + 1)
                act.wait_ge(out_done, BASE + c * 32)
                act.copy(rows[:, :, :], ps[:, 4, 0:PAIRS_OUT * P].rearrange("p (j f) -> p j f", f=P)).then_inc(S["rows_kept"], 1)
                act.wait_ge(S["rows_kept"], BASE + c + 1)
                here = out[:, ds(c * TC, TC), :]
                for odd in range(2):
                    act.dma_start(here[:, odd:TC:2, :],
                                  rows[odd * IMAGES:(odd + 1) * IMAGES, 0:(TC + 1 - odd) // 2, :]).then_inc(out_done, 16)

            act.wait_ge(ones, BASE + 2)
            act.wait_ge(vec_kept, BASE + 1)
            with act.Fori(0, CHUNKS) as c:
                chunk(c)
                finish(c)
                rows_out(c)
            act.wait_ge(out_done, BASE + CHUNKS * 32)


def vit_tower(nc, inputs, out):
    first = dict(x="x", tok_W="L0_tok_W", tok_b="L0_tok_b", cls="L0_tok_class_token", pos="L0_tok_pos_embed",
                 w_qkv="L0_attn_w_qkv", w_agg="L0_attn_w_agg", b_agg="L0_attn_b_agg")
    experts = {name[len("L0_ffn_"):]: ap for name, ap in inputs.items() if name.startswith("L0_ffn_")}
    scratch = lambda name, *shape: nc.dram_tensor(name, shape, F32).ap()
    h1 = scratch("h1_scratch", P, TOKENS)
    z2 = scratch("z2_scratch", P, TOKENS)
    x = scratch("x_scratch", EXPERTS, SEQ, P, KD, IMAGES)
    mem = scratch("mem_scratch", EXPERTS, 2, SEQ, P, KD, IMAGES)
    with nc.psum_tensor("banks", [P, 8, 512], F32) as ps:
        stages(nc, ps, first, experts, inputs, h1, z2, x, mem, out)


def stages(nc, ps, first, experts, inputs, h1, z2, x, mem, out):
    front(nc, ps, {key: inputs[name] for key, name in first.items()}, h1, z2)
    experts_stage(nc, ps, experts, z2, x)
    lstm_stage(nc, ps, experts, x, mem)
    head_stage(nc, ps, experts, h1, z2, mem, out)


_FFN = ("router_w router_b enc_w1 enc_b1 enc_w2 enc_b2 enc_g enc_beta attn_in_w attn_in_b attn_out_w attn_out_b "
        "lstm_wi_f lstm_wh_f lstm_b_f lstm_wi_b lstm_wh_b lstm_b_b sig_w1 sig_b1 sig_w2 sig_b2 tan_w1 tan_b1 tan_w2 "
        "tan_b2 dec_w1 dec_b1 dec_w2 dec_b2 dec_g dec_beta").split()
_INS = ["x", "L0_tok_W", "L0_tok_b", "L0_tok_class_token", "L0_tok_pos_embed", "L0_attn_w_qkv", "L0_attn_w_agg",
        "L0_attn_b_agg"] + ["L0_ffn_" + n for n in _FFN]
_OUTS = [((64, 65, 128), "float32")]


def kernel(**inputs):
    import numpy as _np
    import concourse.bacc as _bacc
    from concourse import mybir as _mybir
    from concourse.bass_utils import run_bass_kernel_spmd as _run

    nc = _bacc.Bacc("TRN2", target_bir_lowering=False, num_devices=1)
    arrays, args = {}, {}
    for name in _INS:
        a = _np.ascontiguousarray(inputs[name])
        arrays[f"in_{name}_dram"] = a
        args[name] = nc.dram_tensor(f"in_{name}_dram", a.shape, _mybir.dt.from_np(a.dtype), kind="ExternalInput").ap()
    (shape, dtype), = _OUTS
    out = nc.dram_tensor("out_0_dram", shape, _mybir.dt.from_np(_np.dtype(dtype)), kind="ExternalOutput").ap()
    vit_tower(nc, args, out)
    r = _run(nc, [arrays], core_ids=[0])
    return r.results[0]["out_0_dram"]
```

```python
from contextlib import ExitStack

import concourse.bass as bass
from concourse import mybir

F32 = mybir.dt.float32
ALU = mybir.AluOpType
ACT = mybir.ActivationFunctionType
AX = mybir.AxisListType
ds = bass.ds

P = 128
IMAGES, CHANNELS, GRID, PATCH = 64, 3, 8, 28
ROWS = CHANNELS * PATCH
SIDE = GRID * PATCH
SEQ = GRID * GRID + 1
TOKENS = IMAGES * SEQ
HID = 128
D = 256
KD = D // P
EXPERTS = 4
HEAD = 16
EPS = 1e-5
BASE = 1
SCALE = HEAD ** -0.5

GROUP = 4
UNIT = GROUP * SEQ
WIDE = 416
WSTEPS, WTRIPS = 5, 2
assert WSTEPS * WTRIPS * WIDE == TOKENS


def semaphores(nc, ctx, tag=""):
    made = []

    def sem(name):
        made.append(ctx.enter_context(nc.semaphore(tag + name)))
        return made[-1]
    return sem, made


def open_block(nc, ctx, made):
    def clear():
        with nc.Block() as block:
            @block.sync
            def _(sp):
                for s in made:
                    sp.sem_clear(s)
    ctx.callback(clear)
    with nc.Block() as block:
        @block.sync
        def _(sp):
            for s in made:
                sp.sem_inc(s, BASE)
    return ctx.enter_context(nc.Block())


def make_identity(pool, tile, zeroed, done):
    pool.memset(tile[:, :], 0.0).then_inc(zeroed, 1)
    pool.wait_ge(zeroed, BASE + 1)
    pool.affine_select(out=tile[:, :], in_=tile[:, :], compare_op=ALU.not_equal, fill=1.0, base=0,
                       pattern=[[-1, P]], channel_multiplier=1).then_inc(done, 1)


def tokens_stage(nc, ps, io, h0, ident):
    XI = 4
    SLOTS = 2
    PADDED = 96
    TRIPS = IMAGES // XI // SLOTS
    NP = GRID * GRID
    with ExitStack() as ctx:
        sb = lambda name, shape: ctx.enter_context(nc.sbuf_tensor(name, shape, F32))
        sem, made = semaphores(nc, ctx)
        image = sb("image", [PADDED, SLOTS, XI, GRID, SIDE])
        w_rows = sb("w_rows", [P, ROWS * PATCH])
        w_cols = sb("w_cols", [PADDED, PATCH, P])
        pos_rows = sb("pos_rows", [SEQ, P])
        pos = sb("pos", [P, SEQ])
        bias = sb("tok_bias", [P, 1])
        cls = sb("cls", [P, 1])
        clsp = sb("clsp", [P, 1])
        loaded = [sem(f"image_loaded{i}") for i in range(SLOTS)]
        consts, w_in = sem("consts_loaded"), sem("w_loaded")
        id_zero, id_done = sem("id_zeroed"), sem("id_done")
        turned, kept = sem("w_turned"), sem("w_kept")
        padded = sem("rows_padded")
        summed, stored, cls_done = sem("tok_summed"), sem("tok_stored"), sem("cls_done")
        block = open_block(nc, ctx, made)
        turns = PATCH // 4

        @block.sync
        def _(sp):
            sp.dma_start(w_rows[:, :], io["tok_W"]).then_inc(w_in, 16)
            sp.dma_start(pos_rows[:, :], io["pos"]).then_inc(consts, 16)
            sp.dma_start(bias[:, :], io["tok_b"].rearrange("(p a) -> p a", a=1)).then_inc(consts, 16)
            sp.dma_start(cls[:, :], io["cls"].rearrange("a p -> p a")).then_inc(consts, 16)
            sp.wait_ge(padded, BASE + 3)
            with sp.Fori(0, TRIPS) as i:
                for s in range(SLOTS):
                    sp.wait_ge(summed, BASE + i * SLOTS)
                    for c in range(CHANNELS):
                        for b in range(XI):
                            src = io["x"][ds((i * SLOTS + s) * XI + b, 1), c].rearrange("a (g p) w -> p (a g) w", p=PATCH)
                            sp.dma_start(image[c * PATCH:(c + 1) * PATCH, s, b], src).then_inc(loaded[s], 16)

        @block.gpsimd
        def _(pool):
            make_identity(pool, ident, id_zero, id_done)
            pool.wait_ge(id_done, BASE + 1)
            pool.memset(image[64:PADDED, 1], 0.0).then_inc(padded, 1)

        @block.tensor
        def _(pe):
            pe.wait_ge(w_in, BASE + 16)
            pe.wait_ge(id_done, BASE + 1)
            w_view = w_rows[:, :].rearrange("p (r q) -> p r q", q=PATCH)
            for g in range(turns):
                if g >= 4:
                    pe.wait_ge(kept, BASE + g - 3)
                for j in range(4):
                    m = pe.transpose(ps[0:ROWS, g % 4, j * P:(j + 1) * P], w_view[:, :, 4 * g + j], ident[:, :])
                m.then_inc(turned, 1)
            pe.wait_ge(consts, BASE + 48)
            pe.wait_ge(kept, BASE + turns)
            pe.transpose(ps[:, 0, 0:SEQ], pos_rows[:, :], ident[0:SEQ, 0:SEQ]).then_inc(turned, 1)
            pe.wait_ge(kept, BASE + turns + 1)
            with pe.Fori(0, TRIPS) as i:
                for s in range(SLOTS):
                    pe.wait_ge(loaded[s], BASE + (i + 1) * 16 * CHANNELS * XI)
                    pe.wait_ge(stored, BASE + i * SLOTS)
                    cols = image[:, s].rearrange("p b g (j q) -> p b g j q", q=PATCH)
                    for q in range(PATCH):
                        m = pe.matmul(ps[:, s % 2, 0:XI * NP], w_cols[:, q, :], cols[:, :, :, :, q],
                                      start=(q == 0), stop=(q == PATCH - 1))
                    m.then_inc(summed, 1)

        @block.vector
        def _(dve):
            dve.memset(image[64:PADDED, 0], 0.0).then_inc(padded, 1)
            dve.memset(w_cols[64:PADDED], 0.0).then_inc(padded, 1)
            dve.wait_ge(padded, BASE + 3)
            for g in range(turns):
                dve.wait_ge(turned, BASE + g + 1)
                dve.tensor_copy(w_cols[0:ROWS, 4 * g:4 * g + 4, :],
                                ps[0:ROWS, g % 4, :].rearrange("p (j m) -> p j m", j=4)).then_inc(kept, 1)
            dve.wait_ge(turned, BASE + turns + 1)
            dve.tensor_copy(pos[:, :], ps[:, 0, 0:SEQ]).then_inc(kept, 1)
            dve.wait_ge(kept, BASE + turns + 1)
            dve.tensor_tensor(clsp[:, :], cls[:, :], pos[:, 0:1], ALU.mult).then_inc(cls_done, 1)
            dve.wait_ge(cls_done, BASE + 1)
            h0_view = h0[:, :].rearrange("p (b s) -> p b s", s=SEQ)
            dve.tensor_copy(h0_view[:, :, 0], clsp[:, :].broadcast_to([P, IMAGES])).then_inc(cls_done, 1)
            with dve.Fori(0, TRIPS) as i:
                for s in range(SLOTS):
                    dve.wait_ge(summed, BASE + i * SLOTS + s + 1)
                    out = h0[:, ds((i * SLOTS + s) * XI * SEQ, XI * SEQ)].rearrange("p (b s) -> p b s", s=SEQ)
                    dve.scalar_tensor_tensor(
                        out=out[:, :, 1:SEQ], in0=ps[:, s % 2, 0:XI * NP].rearrange("p (b t) -> p b t", t=NP),
                        scalar=bias[:, 0:1], in1=pos[:, 1:SEQ].unsqueeze(1).broadcast_to([P, XI, NP]),
                        op0=ALU.add, op1=ALU.mult).then_inc(stored, 1)


def norm_stage(nc, ps, tag, src, dst, add, spill):
    with ExitStack() as ctx:
        sb = lambda name, shape: ctx.enter_context(nc.sbuf_tensor(tag + name, shape, F32))
        sem, made = semaphores(nc, ctx, tag)
        center = sb("center", [P, P])
        mean = sb("mean", [P, P])
        eps = sb("eps", [P, 1])
        xc = sb("xc", [P, 3, WIDE])
        sq = sb("sq", [P, 2, WIDE])
        sd = sb("sd", [P, 2, WIDE])
        rs = sb("rs", [P, 2, WIDE])
        zero, ready = sem("zero"), sem("ready")
        added, centered, copied = sem("added"), sem("centered"), sem("copied")
        squared, varied, rooted = sem("squared"), sem("varied"), sem("rooted")
        inverted, normed, spilled = sem("inverted"), sem("normed"), sem("spilled")
        block = open_block(nc, ctx, made)
        n = WSTEPS

        @block.gpsimd
        def _(pool):
            pool.memset(mean[:, :], 1.0 / P).then_inc(ready, 1)
            pool.memset(eps[:, :], EPS).then_inc(ready, 1)
            pool.memset(center[:, :], -1.0 / P).then_inc(zero, 1)
            pool.wait_ge(zero, BASE + 1)
            pool.affine_select(out=center[:, :], in_=center[:, :], compare_op=ALU.not_equal, fill=1.0 - 1.0 / P,
                               base=0, pattern=[[-1, P]], channel_multiplier=1).then_inc(ready, 1)
            if add is not None:
                with pool.Fori(0, WTRIPS) as i:
                    for s in range(n):
                        at = ds((i * n + s) * WIDE, WIDE)
                        pool.tensor_tensor(src[:, at], src[:, at], add[:, at], ALU.add).then_inc(added, 1)

        @block.tensor
        def _(pe):
            pe.wait_ge(ready, BASE + 3)
            with pe.Fori(0, WTRIPS) as i:
                for s in range(n + 1):
                    if s < n:
                        if add is not None:
                            pe.wait_ge(added, BASE + i * n + s + 1)
                        pe.wait_ge(copied, BASE + i * n + (s - 1 if s >= 2 else 0))
                        pe.matmul(ps[:, s % 2, 0:WIDE], center[:, :], src[:, ds((i * n + s) * WIDE, WIDE)],
                                  start=True, stop=True).then_inc(centered, 1)
                    if s >= 1:
                        v = s - 1
                        pe.wait_ge(squared, BASE + i * n + v + 1)
                        pe.wait_ge(rooted, BASE + i * n + (v - 1 if v >= 2 else 0))
                        pe.matmul(ps[:, 2 + v % 2, 0:WIDE], mean[:, :], sq[:, v % 2, :],
                                  start=True, stop=True).then_inc(varied, 1)

        @block.scalar
        def _(act):
            with act.Fori(0, WTRIPS) as i:
                for s in range(n + 1):
                    if s < n:
                        act.wait_ge(copied, BASE + i * n + s + 1)
                        act.wait_ge(varied, BASE + i * n + (s - 1 if s >= 2 else 0))
                        act.activation(sq[:, s % 2, :], xc[:, s % 3, :], ACT.Square).then_inc(squared, 1)
                    if s >= 1:
                        v = s - 1
                        act.wait_ge(varied, BASE + i * n + v + 1)
                        act.wait_ge(inverted, BASE + i * n + (v - 1 if v >= 2 else 0))
                        act.activation(sd[:, v % 2, :], ps[:, 2 + v % 2, 0:WIDE], ACT.Sqrt,
                                       bias=eps[:, 0:1]).then_inc(rooted, 1)

        @block.vector
        def _(dve):
            with dve.Fori(0, WTRIPS) as i:
                for s in range(n + 2):
                    if s < n:
                        dve.wait_ge(centered, BASE + i * n + s + 1)
                        dve.wait_ge(squared, BASE + i * n + max(s - 2, 0))
                        dve.wait_ge(normed, BASE + i * n + max(s - 2, 0))
                        dve.tensor_copy(xc[:, s % 3, :], ps[:, s % 2, 0:WIDE]).then_inc(copied, 1)
                    if s >= 2:
                        v = s - 2
                        dve.wait_ge(rooted, BASE + i * n + v + 1)
                        dve.reciprocal(rs[:, v % 2, :], sd[:, v % 2, :]).then_inc(inverted, 1)
                        dve.wait_ge(inverted, BASE + i * n + v + 1)
                        dve.tensor_tensor(dst[:, ds((i * n + v) * WIDE, WIDE)], xc[:, v % 3, :], rs[:, v % 2, :],
                                          ALU.mult).then_inc(normed, 1)

        if spill:
            @block.sync
            def _(sp):
                sp.wait_ge(normed, BASE + WTRIPS * n)
                sp.dma_start(spill[0], src[:, :]).then_inc(spilled, 16)
                sp.dma_start(spill[1], dst[:, :]).then_inc(spilled, 16)
                sp.wait_ge(spilled, BASE + 32)


class Attention:
    TURN, WEIGH = 2, 3
    UNITS = IMAGES // GROUP
    ROWS_T = 96

    def __init__(self, nc, ctx, make_sem, tag, C):
        sb = lambda name, shape: ctx.enter_context(nc.sbuf_tensor(tag + name, shape, F32))
        sem = lambda name: make_sem(tag + name)
        self.C, self.NH = C, P // HEAD
        self.steps = GROUP * C
        assert self.steps % 4 == 0
        self.x = sb("x", [P, 2, C, UNIT])
        self.q = sb("q", [P, 2, C, UNIT])
        self.k = sb("k", [P, 2, C, UNIT])
        self.km = sb("km", [P, 2, self.NH, SEQ])
        self.v = sb("v", [SEQ, 2 * GROUP, C * 4, 4, HEAD])
        self.p = sb("p", [self.ROWS_T, 4, self.NH, SEQ])
        self.pt = sb("pt", [SEQ, 2, self.NH, SEQ])
        self.o = sb("o", [P, 2, C, UNIT])
        self.mx = sb("mx", [SEQ, 2, self.NH])
        self.sm = sb("sm", [SEQ, 4, self.NH])
        self.ri = sb("ri", [SEQ, 4, self.NH])
        self.mask = sb("mask", [P, self.NH])
        (self.v_zeroed, self.p_zeroed, self.mask_done, self.x_copied, self.keys_masked, self.scored, self.maxed,
         self.shifted, self.exped, self.summed, self.inverted, self.normed, self.turned, self.turn_kept,
         self.weighed, self.o_kept, self.piece_done, self.piece_kept, self.out_done, self.out_kept) = [
             sem(n) for n in (
                 "v_zeroed", "p_zeroed", "mask_done", "x_copied", "keys_masked", "scored", "maxed", "shifted", "exped",
                 "summed", "inverted", "normed", "turned", "turn_kept", "weighed", "o_kept", "piece_done",
                 "piece_kept", "out_done", "out_kept")]
        self.order = [("q", c) for c in range(C)] + [("k", c) for c in range(C)] + [("v", b) for b in range(GROUP)]
        self.pieces = len(self.order)
        self.index = {x: n for n, x in enumerate(self.order)}
        assert self.pieces % 2 == 0
        per = -(-self.pieces // self.steps)
        self.after = [self.order[s * per:(s + 1) * per] for s in range(self.steps)]

    def place(self, s):
        return s % self.steps // self.C, s % self.C

    def run(self, eng, base, unit):
        unit(base, 0, 0, True, False)
        with eng.Fori(0, self.UNITS // 2 - 1) as i:
            for r in range(2):
                unit(base + i * 2 + 1 + r, i * 2 + 1 + r, 1 - r, False, False)
        unit(base + self.UNITS - 1, self.UNITS - 1, 1, False, True)

    def pool_setup(self, pool):
        pool.memset(self.v[:, :, :, :, :], 0.0).then_inc(self.v_zeroed, 1)
        pool.memset(self.mask[:, :], 1.0).then_inc(self.mask_done, 1)
        pool.wait_ge(self.mask_done, BASE + 1)
        pool.affine_select(out=self.mask[:, :], in_=self.mask[:, :], compare_op=ALU.is_ge, fill=0.0, base=0,
                           pattern=[[-HEAD, self.NH]], channel_multiplier=1).then_inc(self.mask_done, 1)
        pool.wait_ge(self.mask_done, BASE + 2)
        pool.affine_select(out=self.mask[:, :], in_=self.mask[:, :], compare_op=ALU.is_ge, fill=0.0, base=HEAD - 1,
                           pattern=[[HEAD, self.NH]], channel_multiplier=-1).then_inc(self.mask_done, 1)
        pool.wait_ge(self.mask_done, BASE + 3)

    def pool_run(self, pool, base):
        n, NP = self.steps, self.pieces

        def mask_keys(unit, par, s, start):
            b, c = self.place(s)
            pool.wait_ge(self.piece_kept, BASE + unit * NP + self.index["k", c] + 1)
            pool.wait_ge(self.scored, BASE + unit * n + (0 if start else s - 1))
            pool.tensor_tensor(
                self.km[:, s % 2],
                self.k[:, par, c, b * SEQ:(b + 1) * SEQ].unsqueeze(1).broadcast_to([P, self.NH, SEQ]),
                self.mask[:, :].unsqueeze(2).broadcast_to([P, self.NH, SEQ]), ALU.mult).then_inc(self.keys_masked, 1)

        def norm(unit, s):
            pool.wait_ge(self.inverted, BASE + unit * n + s)
            v = (s - 1) % 4
            pool.tensor_tensor(self.p[0:SEQ, v], self.p[0:SEQ, v],
                               self.ri[:, v, :].unsqueeze(2).broadcast_to([SEQ, self.NH, SEQ]),
                               ALU.mult).then_inc(self.normed, 1)

        def unit_(unit, at, par, first, last):
            for s in range(n):
                if s + 1 < n:
                    mask_keys(unit, par, s + 1, False)
                elif not last:
                    mask_keys(unit + 1, 1 - par, 0, False)
                if s or not first:
                    norm(unit, s)

        mask_keys(base, 0, 0, True)
        self.run(pool, base, unit_)
        norm(base + self.UNITS, 0)

    def pe_piece(self, pe, ps, w_in, unit, par, idx):
        C = self.C
        kind, m = self.order[idx]
        bank = ps[:, 6 + idx % 2, :]
        for k in range(C):
            flags = dict(start=(k == 0), stop=(k == C - 1))
            if kind == "v":
                mm = pe.matmul(bank[0:SEQ, 0:C * P], self.x[:, par, k, m * SEQ:(m + 1) * SEQ],
                               w_in[:, k, 2 * C * P:3 * C * P], **flags)
            else:
                at = (m if kind == "q" else C + m) * P
                mm = pe.matmul(bank[:, 0:UNIT], w_in[:, k, at:at + P], self.x[:, par, k, :], **flags)
        mm.then_inc(self.piece_done, 1)

    def pe_run(self, pe, base, ps, w_in, w_out, ident):
        C, NH, n, NP, R = self.C, self.NH, self.steps, self.pieces, self.ROWS_T

        def behind(unit, par, s, first, pieces):
            g = unit * n + s
            if s >= self.TURN or not first:
                pe.wait_ge(self.normed, BASE + g - self.TURN + 1)
                pe.wait_ge(self.turn_kept, BASE + g - self.TURN)
                for h in range(NH):
                    mm = pe.transpose(ps[0:SEQ, 2 + h // 4, (h % 4) * R:(h % 4 + 1) * R],
                                      self.p[:, (s - self.TURN) % 4, h, :], ident[0:R, 0:R])
                mm.then_inc(self.turned, 1)
            if s >= self.WEIGH or not first:
                v = s - self.WEIGH
                own = v >= 0
                (b, c), vpar = self.place(v), par if own else 1 - par
                pe.wait_ge(self.turn_kept, BASE + g - self.WEIGH + 1)
                pe.wait_ge(self.piece_kept, BASE + (unit if own else unit - 1) * NP + self.index["v", b] + 1)
                pe.wait_ge(self.o_kept, BASE + unit * n + (max(v - 1, 0) if first else v - 1))
                for odd in range(2):
                    for j in range(4):
                        mm = pe.matmul(
                            ps[32 * j:32 * j + 32, 4 + v % 2, 0:SEQ],
                            self.v[:, vpar * GROUP + b, 4 * c + j, 2 * odd:2 * odd + 2, :].rearrange("p a d -> p (a d)"),
                            self.pt[:, v % 2, 2 * j + odd, :], start=(odd == 0), stop=(odd == 1))
                mm.then_inc(self.weighed, 1)
            if s == self.WEIGH and not first:
                pe.wait_ge(self.o_kept, BASE + unit * n)
                pe.wait_ge(self.piece_kept, BASE + pieces)
                for m in range(C):
                    for k in range(C):
                        mm = pe.matmul(ps[:, 6 + m, 0:UNIT], w_out[:, k, m * P:(m + 1) * P],
                                       self.o[:, 1 - par, k, :], start=(k == 0), stop=(k == C - 1))
                    mm.then_inc(self.out_done, 1)

        def unit_(unit, at, par, first, last):
            issued = 0
            for s in range(n):
                b, c = self.place(s)
                g = unit * n + s
                pe.wait_ge(self.piece_kept, BASE + unit * NP + self.index["q", c] + 1)
                pe.wait_ge(self.keys_masked, BASE + g + 1)
                pe.wait_ge(self.shifted, BASE + g)
                for j in range(2):
                    mm = pe.matmul(ps[0:SEQ, j, 0:4 * SEQ], self.q[:, par, c, b * SEQ:(b + 1) * SEQ],
                                   self.km[:, s % 2, 4 * j:4 * j + 4, :], start=True, stop=True)
                mm.then_inc(self.scored, 1)
                behind(unit, par, s, first, (unit + 1) * NP + issued)
                for piece in [] if last else self.after[s]:
                    idx = self.index[piece]
                    issued = idx + 1
                    pe.wait_ge(self.x_copied, BASE + unit + 2)
                    pe.wait_ge(self.piece_kept, BASE + (unit + 1) * NP + idx - 1)
                    pe.wait_ge(self.out_kept, BASE + (unit if first or s >= self.WEIGH else unit - 1) * C)
                    self.pe_piece(pe, ps, w_in, unit + 1, 1 - par, idx)

        pe.wait_ge(self.x_copied, BASE + base + 1)
        pe.wait_ge(self.v_zeroed, BASE + 1)
        pe.wait_ge(self.p_zeroed, BASE + 1)
        for idx in range(NP):
            pe.wait_ge(self.piece_kept, BASE + base * NP + max(idx - 1, 0))
            self.pe_piece(pe, ps, w_in, base, 0, idx)
        self.run(pe, base, unit_)
        for s in range(self.WEIGH + 1):
            if s == self.WEIGH:
                end = base + self.UNITS
                pe.wait_ge(self.o_kept, BASE + end * n)
                for m in range(C):
                    for k in range(C):
                        mm = pe.matmul(ps[:, 6 + m, 0:UNIT], w_out[:, k, m * P:(m + 1) * P],
                                       self.o[:, 1, k, :], start=(k == 0), stop=(k == C - 1))
                    mm.then_inc(self.out_done, 1)
            else:
                self.pe_tail(pe, ps, base + self.UNITS, s, ident)

    def pe_tail(self, pe, ps, end, s, ident):
        n, R = self.steps, self.ROWS_T
        g = end * n + s
        if s < self.TURN:
            pe.wait_ge(self.normed, BASE + g - self.TURN + 1)
            pe.wait_ge(self.turn_kept, BASE + g - self.TURN)
            for h in range(self.NH):
                mm = pe.transpose(ps[0:SEQ, 2 + h // 4, (h % 4) * R:(h % 4 + 1) * R],
                                  self.p[:, (s - self.TURN) % 4, h, :], ident[0:R, 0:R])
            mm.then_inc(self.turned, 1)
        v = s - self.WEIGH
        b, c = self.place(v)
        pe.wait_ge(self.turn_kept, BASE + g - self.WEIGH + 1)
        pe.wait_ge(self.o_kept, BASE + g - self.WEIGH - 1)
        for odd in range(2):
            for j in range(4):
                mm = pe.matmul(
                    ps[32 * j:32 * j + 32, 4 + v % 2, 0:SEQ],
                    self.v[:, GROUP + b, 4 * c + j, 2 * odd:2 * odd + 2, :].rearrange("p a d -> p (a d)"),
                    self.pt[:, v % 2, 2 * j + odd, :], start=(odd == 0), stop=(odd == 1))
        mm.then_inc(self.weighed, 1)

    def dve_setup(self, dve):
        dve.memset(self.p[64:self.ROWS_T], 0.0).then_inc(self.p_zeroed, 1)
        dve.wait_ge(self.p_zeroed, BASE + 1)

    def dve_run(self, dve, base, ps, src):
        n, NH = self.steps, self.NH

        def take(at, par, before):
            dve.wait_ge(self.piece_done, BASE + before * self.pieces)
            dve.tensor_copy(self.x[:, par], src[:, :, ds(at * UNIT, UNIT)]).then_inc(self.x_copied, 1)

        scores = ps[0:SEQ, 0:2, 0:4 * SEQ].rearrange("p a (h k) -> p a h k", k=SEQ)

        def sums(unit, s):
            g, v = unit * n + s, (s - 1) % 4
            dve.wait_ge(self.exped, BASE + g)
            dve.tensor_reduce(self.sm[:, v, :], self.p[0:SEQ, v], AX.X, ALU.add).then_inc(self.summed, 1)
            dve.wait_ge(self.summed, BASE + g)
            dve.reciprocal(self.ri[:, v, :], self.sm[:, v, :]).then_inc(self.inverted, 1)

        def unit_(unit, at, par, first, last):
            for s in range(n):
                g = unit * n + s
                if s == 0 and not last:
                    take(at + 1, 1 - par, unit)
                dve.wait_ge(self.scored, BASE + g + 1)
                dve.tensor_reduce(self.mx[:, s % 2, :].rearrange("p (a h) -> p a h", a=2), scores, AX.X,
                                  ALU.max).then_inc(self.maxed, 1)
                dve.wait_ge(self.maxed, BASE + g + 1)
                dve.wait_ge(self.turned, BASE + unit * n + (max(s - 3, 0) if first else s - 3))
                dve.tensor_tensor(
                    self.p[0:SEQ, s % 4].rearrange("p (a h) k -> p a h k", a=2), scores,
                    self.mx[:, s % 2, :].rearrange("p (a h) -> p a h", a=2).unsqueeze(3)
                        .broadcast_to([SEQ, 2, NH // 2, SEQ]), ALU.subtract).then_inc(self.shifted, 1)
                if s or not first:
                    sums(unit, s)

        take(0, 0, base)
        self.run(dve, base, unit_)
        sums(base + self.UNITS, 0)

    def act_piece(self, act, ps, bias_q, unit, par, idx):
        C = self.C
        kind, m = self.order[idx]
        act.wait_ge(self.piece_done, BASE + unit * self.pieces + idx + 1)
        bank = ps[:, 6 + idx % 2, :]
        if kind == "v":
            op = act.copy(self.v[:, par * GROUP + m, :, 0:4:3, :],
                          bank[0:SEQ, 0:C * P].rearrange("p (j a d) -> p j a d", a=2, d=HEAD))
        else:
            dst = (self.q if kind == "q" else self.k)[:, par, m, :]
            if bias_q is None:
                op = act.copy(dst, bank[:, 0:UNIT])
            else:
                col = m if kind == "q" else C + m
                op = act.activation(dst, bank[:, 0:UNIT], ACT.Identity, bias=bias_q[:, col:col + 1])
        op.then_inc(self.piece_kept, 1)

    def act_run(self, act, base, ps, bias_q, bias_o, store_o):
        C, n, R = self.C, self.steps, self.ROWS_T

        def keep_turned(unit, s, first):
            g = unit * n + s
            act.wait_ge(self.turned, BASE + g - self.TURN + 1)
            act.wait_ge(self.weighed, BASE + unit * n + (max(s - 3, 0) if first else s - 3))
            act.copy(self.pt[:, (s - self.TURN) % 2].rearrange("p (a h) k -> p a h k", a=2),
                     ps[0:SEQ, 2:4, 0:4 * R].rearrange("p a (h k) -> p a h k", k=R)[:, :, :, 0:SEQ]).then_inc(self.turn_kept, 1)

        def keep_weighed(unit, par, s):
            v = s - self.WEIGH
            b, c = self.place(v)
            act.wait_ge(self.weighed, BASE + unit * n + v + 1)
            act.copy(self.o[:, par if v >= 0 else 1 - par, c, b * SEQ:(b + 1) * SEQ],
                     ps[:, 4 + v % 2, 0:SEQ]).then_inc(self.o_kept, 1)

        def outputs(unit, at):
            for m in range(C):
                act.wait_ge(self.out_done, BASE + (unit - 1) * C + m + 1)
                store_o(at - 1, m, ps[:, 6 + m, 0:UNIT], bias_o[:, m:m + 1]).then_inc(self.out_kept, 1)

        def unit_(unit, at, par, first, last):
            for s in range(n):
                if s >= self.TURN or not first:
                    keep_turned(unit, s, first)
                act.wait_ge(self.shifted, BASE + unit * n + s + 1)
                act.activation(self.p[0:SEQ, s % 4], self.p[0:SEQ, s % 4], ACT.Exp, scale=SCALE).then_inc(self.exped, 1)
                if s >= self.WEIGH or not first:
                    keep_weighed(unit, par, s)
                if s == self.WEIGH and not first:
                    outputs(unit, at)
                for piece in [] if last else self.after[s]:
                    self.act_piece(act, ps, bias_q, unit + 1, 1 - par, self.index[piece])

        for idx in range(self.pieces):
            self.act_piece(act, ps, bias_q, base, 0, idx)
        self.run(act, base, unit_)
        end = base + self.UNITS
        for s in range(self.WEIGH):
            if s < self.TURN:
                keep_turned(end, s, False)
            keep_weighed(end, 0, s)
        outputs(end, self.UNITS)


def first_attention_stage(nc, ps, io, z, out, ident):
    with ExitStack() as ctx:
        sb = lambda name, shape: ctx.enter_context(nc.sbuf_tensor(name, shape, F32))
        sem, made = semaphores(nc, ctx)
        att = Attention(nc, ctx, sem, "a1_", 1)
        rows = sb("a1_rows", [P, 4, HID])
        cols = sb("a1_cols", [P, 4, P])
        bias = sb("a1_bias", [P, 1])
        loaded, turned, kept = sem("a1_loaded"), sem("a1_w_turned"), sem("a1_w_kept")
        block = open_block(nc, ctx, made)
        w_in, w_out = cols[:, 0:3, :].rearrange("p a b -> p (a b)").unsqueeze(1), cols[:, 3:4, :]

        @block.sync
        def _(sp):
            sp.dma_start(rows[:, 0:3, :], io["w_qkv"].rearrange("(a p) d -> p a d", p=P)).then_inc(loaded, 16)
            sp.dma_start(rows[:, 3, :], io["w_agg"]).then_inc(loaded, 16)
            sp.dma_start(bias[:, :], io["b_agg"].rearrange("(p a) -> p a", a=1)).then_inc(loaded, 16)

        @block.gpsimd
        def _(pool):
            att.pool_setup(pool)
            att.pool_run(pool, 0)

        @block.tensor
        def _(pe):
            pe.wait_ge(loaded, BASE + 48)
            for a in range(4):
                m = pe.transpose(ps[:, 0, a * P:(a + 1) * P], rows[:, a, :], ident[:, :])
            m.then_inc(turned, 1)
            pe.wait_ge(kept, BASE + 1)
            att.pe_run(pe, 0, ps, w_in, w_out, ident)

        @block.vector
        def _(dve):
            dve.wait_ge(turned, BASE + 1)
            dve.tensor_copy(cols[:, :, :], ps[:, 0, :].rearrange("p (a m) -> p a m", a=4)).then_inc(kept, 1)
            att.dve_setup(dve)
            att.dve_run(dve, 0, ps, z[:, :].unsqueeze(1))

        @block.scalar
        def _(act):
            def store(at, m, bank, b):
                return act.activation(out[:, ds(at * UNIT, UNIT)], bank, ACT.Identity, bias=b)
            act.wait_ge(att.v_zeroed, BASE + 1)
            act.wait_ge(loaded, BASE + 48)
            att.act_run(act, 0, ps, None, bias, store)


def front(nc, ps, io, h1_dram, z2_dram):
    with ExitStack() as ctx:
        sb = lambda name, shape: ctx.enter_context(nc.sbuf_tensor(name, shape, F32))
        ident = sb("ident", [P, P])
        h = sb("h", [P, TOKENS])
        tokens_stage(nc, ps, io, h, ident)
        z = sb("z", [P, TOKENS])
        attended = sb("attended", [P, TOKENS])
        norm_stage(nc, ps, "n1_", h, z, None, None)
        first_attention_stage(nc, ps, io, z, attended, ident)
        norm_stage(nc, ps, "n2_", h, z, attended, (h1_dram, z2_dram))


VECTORS = dict(b1=(0, KD), b2=(2, KD), g=(4, KD), beta=(6, KD), in_b=(8, 3 * KD), out_b=(14, KD))
NVEC = 16


def experts_stage(nc, ps, io, z2_dram, x_dram):
    with ExitStack() as ctx:
        sb = lambda name, shape: ctx.enter_context(nc.sbuf_tensor(name, shape, F32))
        sem, made = semaphores(nc, ctx)
        ident = sb("x_ident", [P, P])
        z = sb("x_z", [P, TOKENS])
        h = sb("x_h", [P, KD, TOKENS])
        xo = sb("x_out", [P, SEQ, KD, IMAGES])
        vec_rows = sb("x_vec_rows", [EXPERTS * NVEC, P])
        vec_all = sb("x_vec_all", [P, EXPERTS, NVEC])
        vec = sb("x_vec", [P, NVEC])
        raw_w1 = sb("raw_w1", [P, D])
        raw_w2 = sb("raw_w2", [P, KD, D])
        raw_in = sb("raw_in", [P, KD, 3 * D])
        raw_out = sb("raw_out", [P, KD, D])
        w1 = sb("w1", [P, D])
        w2 = sb("w2", [P, KD, D])
        w_in = sb("w_in", [P, KD, 3 * D])
        w_out = sb("w_out", [P, KD, D])
        row_sum = sb("row_sum", [P, KD])
        row_mean = sb("row_mean", [P, KD])
        b2_mean = sb("b2_mean", [P, 1])
        b2c = sb("b2c", [P, KD])
        in_b = sb("in_b", [P, 3 * KD])
        out_b = sb("out_b", [P, KD])
        mean = sb("x_mean", [P, P])
        eps = sb("x_eps", [P, 1])
        h1 = sb("x_h1", [P, 2, KD, WIDE])
        hc = sb("x_hc", [P, 2, KD, WIDE])
        sq = sb("x_sq", [P, 2, KD, WIDE])
        sd = sb("x_sd", [P, WIDE])
        rs = sb("x_rs", [P, WIDE])
        att = Attention(nc, ctx, sem, "ax_", KD)
        consts, z_in, id_zero, id_done, ones = (sem("x_consts"), sem("x_z_in"), sem("x_id_zero"), sem("x_id_done"),
                                                sem("x_ones"))
        vec_turned, vec_kept = sem("x_vec_turned"), sem("x_vec_kept")
        raw_loaded, prepared = sem("raw_loaded"), sem("prepared")
        prep_step, prep_sums = sem("prep_step"), sem("prep_sums")
        h1_done, h1_kept, h2_done, h2_kept = sem("h1_done"), sem("h1_kept"), sem("h2_done"), sem("h2_kept")
        squared, varied, rooted, inverted, h_ready = (sem("x_squared"), sem("x_varied"), sem("x_rooted"),
                                                      sem("x_inverted"), sem("x_h_ready"))
        saved = sem("x_saved")
        block = open_block(nc, ctx, made)
        n, STEPS = WSTEPS, WSTEPS * WTRIPS
        PREP = 16

        @block.sync
        def _(sp):
            sp.dma_start(z[:, :], z2_dram).then_inc(z_in, 16)
            for name, key in (("b1", "enc_b1"), ("b2", "enc_b2"), ("g", "enc_g"), ("beta", "enc_beta"),
                              ("in_b", "attn_in_b"), ("out_b", "attn_out_b")):
                at, k = VECTORS[name]
                for e in range(EXPERTS):
                    row = e * NVEC + at
                    sp.dma_start(vec_rows[row:row + k, :],
                                 io[key][e].rearrange("(k p) -> k p", p=P)).then_inc(consts, 16)

            def load(e):
                sp.dma_start(raw_w1[:, :], io["enc_w1"][ds(e, 1)].rearrange("a k n -> (a k) n")).then_inc(raw_loaded, 16)
                for raw, name in ((raw_w2, "enc_w2"), (raw_in, "attn_in_w"), (raw_out, "attn_out_w")):
                    sp.dma_start(raw[:, :, :], io[name][ds(e, 1)].rearrange("a (k p) n -> p (a k) n", p=P)).then_inc(raw_loaded, 16)

            def save(e):
                sp.wait_ge(att.out_kept, BASE + (e + 1) * att.UNITS * KD)
                sp.dma_start(x_dram[ds(e, 1)].rearrange("a t f k b -> f (a t) (k b)"),
                             xo[:, :, :, :].rearrange("p t k b -> p t (k b)")).then_inc(saved, 16)

            load(0)
            with sp.Fori(0, EXPERTS - 1) as e:
                sp.wait_ge(prepared, BASE + e + 1)
                load(e + 1)
                save(e)
            save(EXPERTS - 1)
            sp.wait_ge(saved, BASE + 16 * EXPERTS)

        @block.gpsimd
        def _(pool):
            make_identity(pool, ident, id_zero, id_done)
            pool.memset(mean[:, :], 1.0 / D).then_inc(ones, 1)
            pool.memset(eps[:, :], EPS).then_inc(ones, 1)
            pool.wait_ge(id_done, BASE + 1)
            pool.wait_ge(ones, BASE + 2)
            att.pool_setup(pool)
            with pool.Fori(0, EXPERTS) as e:
                att.pool_run(pool, e * att.UNITS)

        @block.tensor
        def _(pe):
            pe.wait_ge(z_in, BASE + 16)
            pe.wait_ge(ones, BASE + 2)
            pe.wait_ge(id_done, BASE + 1)
            pe.wait_ge(consts, BASE + 16 * EXPERTS * len(VECTORS))
            pe.transpose(ps[:, 0, 0:EXPERTS * NVEC], vec_rows[:, :],
                         ident[0:EXPERTS * NVEC, 0:EXPERTS * NVEC]).then_inc(vec_turned, 1)
            with pe.Fori(0, EXPERTS) as e:
                pe.wait_ge(raw_loaded, BASE + (e + 1) * 64)
                pe.wait_ge(prep_step, BASE + e * PREP + 1)
                at = VECTORS["b2"][0]
                pe.matmul(ps[:, 5, 0:KD], mean[:, :], vec[:, at:at + KD], start=True, stop=True).then_inc(prep_sums, 1)
                at = VECTORS["beta"][0]
                for m in range(3 * KD):
                    for k in range(KD):
                        mm = pe.matmul(ps[:, 6, m:m + 1], raw_in[:, k, m * P:(m + 1) * P], vec[:, at + k:at + k + 1],
                                       start=(k == 0), stop=(k == KD - 1))
                mm.then_inc(prep_sums, 1)
                pe.wait_ge(prep_step, BASE + e * PREP + 3)
                for m in range(KD):
                    for k in range(KD):
                        mm = pe.matmul(ps[:, 7, m:m + 1], raw_out[:, k, m * P:(m + 1) * P],
                                       in_b[:, 2 * KD + k:2 * KD + k + 1], start=(k == 0), stop=(k == KD - 1))
                mm.then_inc(prep_sums, 1)
                with pe.Fori(0, WTRIPS) as i:
                    base = e * STEPS + i * n
                    for s in range(n + 2):
                        if s == 0:
                            pe.wait_ge(prepared, BASE + e + 1)
                        if s < n:
                            pe.wait_ge(h1_kept, BASE + (base + s) * KD)
                            for m in range(KD):
                                pe.matmul(ps[:, m, 0:WIDE], w1[:, m * P:(m + 1) * P], z[:, ds((i * n + s) * WIDE, WIDE)],
                                          start=True, stop=True).then_inc(h1_done, 1)
                        if 1 <= s <= n:
                            v = s - 1
                            pe.wait_ge(h1_kept, BASE + (base + v + 1) * KD)
                            pe.wait_ge(h2_kept, BASE + (base + v) * KD)
                            for m in range(KD):
                                for k in range(KD):
                                    mm = pe.matmul(ps[:, 2 + m, 0:WIDE], w2[:, k, m * P:(m + 1) * P], h1[:, v % 2, k, :],
                                                   start=(k == 0), stop=(k == KD - 1))
                                mm.then_inc(h2_done, 1)
                        if s >= 2:
                            v = s - 2
                            pe.wait_ge(squared, BASE + base + v + 1)
                            pe.wait_ge(rooted, BASE + base + v)
                            for k in range(KD):
                                mm = pe.matmul(ps[:, 4, 0:WIDE], mean[:, :], sq[:, v % 2, k, :],
                                               start=(k == 0), stop=(k == KD - 1))
                            mm.then_inc(varied, 1)
                att.pe_run(pe, e * att.UNITS, ps, w_in, w_out, ident)

        @block.vector
        def _(dve):
            att.dve_setup(dve)
            dve.wait_ge(vec_turned, BASE + 1)
            dve.tensor_copy(vec_all[:, :, :], ps[:, 0, 0:EXPERTS * NVEC].rearrange("p (e v) -> p e v", v=NVEC)).then_inc(vec_kept, 1)
            dve.wait_ge(vec_kept, BASE + 1)
            with dve.Fori(0, EXPERTS) as e:
                V = {name: vec[:, at:at + k] for name, (at, k) in VECTORS.items()}
                b = e * PREP
                dve.wait_ge(att.out_kept, BASE + e * att.UNITS * KD)
                dve.wait_ge(raw_loaded, BASE + (e + 1) * 64)
                dve.tensor_copy(vec[:, :], vec_all[:, ds(e, 1), :].rearrange("p a v -> p (a v)")).then_inc(prep_step, 1)
                dve.tensor_reduce(row_sum[:, :], raw_w2[:, :, :], AX.X, ALU.add).then_inc(prep_step, 1)
                dve.wait_ge(prep_sums, BASE + e * 3 + 2)
                dve.wait_ge(prep_step, BASE + b + 2)
                dve.tensor_tensor(in_b[:, :], ps[:, 6, 0:3 * KD], V["in_b"], ALU.add).then_inc(prep_step, 1)
                dve.tensor_reduce(b2_mean[:, :], ps[:, 5, 0:KD], AX.X, ALU.add).then_inc(prep_step, 1)
                dve.tensor_scalar(row_mean[:, :], row_sum[:, :], 1.0 / D, None, ALU.mult).then_inc(prep_step, 1)
                dve.wait_ge(prep_step, BASE + b + 5)
                dve.tensor_scalar(b2c[:, :], V["b2"], b2_mean[:, 0:1], None, ALU.subtract).then_inc(prep_step, 1)
                for k in range(KD):
                    dve.tensor_scalar(w2[:, k, :], raw_w2[:, k, :], row_mean[:, k:k + 1], None,
                                      ALU.subtract).then_inc(prep_step, 1)
                for k in range(KD):
                    dve.tensor_scalar(w_in[:, k, :], raw_in[:, k, :], V["g"][:, k:k + 1], None,
                                      ALU.mult).then_inc(prep_step, 1)
                dve.tensor_copy(w1[:, :], raw_w1[:, :]).then_inc(prep_step, 1)
                dve.tensor_copy(w_out[:, :, :], raw_out[:, :, :]).then_inc(prep_step, 1)
                dve.wait_ge(prep_sums, BASE + e * 3 + 3)
                dve.tensor_tensor(out_b[:, :], ps[:, 7, 0:KD], V["out_b"], ALU.add).then_inc(prep_step, 1)
                dve.sem_inc(prep_step, PREP - 13)
                dve.wait_ge(prep_step, BASE + b + PREP)
                dve.sem_inc(prepared, 1)
                with dve.Fori(0, WTRIPS) as i:
                    base = e * STEPS + i * n
                    for s in range(n + 2):
                        if 1 <= s <= n:
                            v = s - 1
                            dve.wait_ge(squared, BASE + base + max(v - 1, 0))
                            dve.wait_ge(h_ready, BASE + base + max(v - 1, 0))
                            for m in range(KD):
                                dve.wait_ge(h2_done, BASE + (base + v) * KD + m + 1)
                                dve.tensor_scalar(hc[:, v % 2, m, :], ps[:, 2 + m, 0:WIDE], b2c[:, m:m + 1], None,
                                                  ALU.add).then_inc(h2_kept, 1)
                        if s >= 2:
                            v = s - 2
                            dve.wait_ge(rooted, BASE + base + v + 1)
                            dve.wait_ge(h_ready, BASE + base + v)
                            dve.reciprocal(rs[:, :], sd[:, :]).then_inc(inverted, 1)
                            dve.wait_ge(inverted, BASE + base + v + 1)
                            dve.tensor_tensor(h[:, :, ds((i * n + v) * WIDE, WIDE)], hc[:, v % 2],
                                              rs[:, :].unsqueeze(1).broadcast_to([P, KD, WIDE]),
                                              ALU.mult).then_inc(h_ready, 1)
                dve.wait_ge(h_ready, BASE + (e + 1) * STEPS)
                att.dve_run(dve, e * att.UNITS, ps, h)

        @block.scalar
        def _(act):
            with act.Fori(0, EXPERTS) as e:
                act.wait_ge(prepared, BASE + e + 1)
                at = VECTORS["b1"][0]
                with act.Fori(0, WTRIPS) as i:
                    base = e * STEPS + i * n
                    for s in range(n + 2):
                        if s < n:
                            for m in range(KD):
                                act.wait_ge(h1_done, BASE + (base + s) * KD + m + 1)
                                act.wait_ge(h2_done, BASE + (base + max(s - 1, 0)) * KD)
                                act.activation(h1[:, s % 2, m, :], ps[:, m, 0:WIDE], ACT.Relu,
                                               bias=vec[:, at + m:at + m + 1]).then_inc(h1_kept, 1)
                        if 1 <= s <= n:
                            v = s - 1
                            act.wait_ge(h2_kept, BASE + (base + v + 1) * KD)
                            act.wait_ge(varied, BASE + base + max(v - 1, 0))
                            act.activation(sq[:, v % 2], hc[:, v % 2], ACT.Square).then_inc(squared, 1)
                        if s >= 2:
                            v = s - 2
                            act.wait_ge(varied, BASE + base + v + 1)
                            act.wait_ge(inverted, BASE + base + v)
                            act.activation(sd[:, :], ps[:, 4, 0:WIDE], ACT.Sqrt, bias=eps[:, 0:1]).then_inc(rooted, 1)
                act.wait_ge(saved, BASE + e * 16)
                def store(at, m, bank, b):
                    dst = xo[:, :, m, ds(at * GROUP, GROUP)].rearrange("p t b -> p b t")
                    return act.activation(dst, bank.rearrange("p (b t) -> p b t", t=SEQ), ACT.Identity, bias=b)
                act.wait_ge(att.v_zeroed, BASE + 1)
                att.act_run(act, e * att.UNITS, ps, in_b, out_b, store)


def lstm_stage(nc, ps, io, x_dram, mem_dram):
    HALF = IMAGES
    G4 = 4 * D
    COLUMNS = ((0, 0, 2 * D), (2 * D, 3 * D, D), (3 * D, 2 * D, D))
    WLOADS = 2 * 2 * EXPERTS * len(COLUMNS)
    TRIPS = (SEQ - 1) // 2
    with ExitStack() as ctx:
        sb = lambda name, shape: ctx.enter_context(nc.sbuf_tensor(name, shape, F32))
        sem, made = semaphores(nc, ctx)
        ident = sb("l_ident", [P, P])
        w = sb("l_w", [P, EXPERTS, 2, 2 * KD, G4])
        bias = sb("l_bias", [P, EXPERTS, G4])
        xs = sb("l_x", [P, 2, 2, EXPERTS, KD, IMAGES])
        hT = sb("l_hT", [P, EXPERTS, 2, KD, IMAGES])
        cell = sb("l_cell", [P, EXPERTS, D])
        gates = sb("l_gates", [P, 2, G4])
        ig = sb("l_ig", [P, D])
        tc = sb("l_tc", [P, D])
        hid = sb("l_hid", [P, 2, D])
        w_in, bias_in = sem("l_w_in"), sem("l_bias_in")
        id_zero, id_done = sem("l_id_zero"), sem("l_id_done")
        x_in = [[sem(f"l_x_in{q}{d}") for d in range(2)] for q in range(2)]
        summed, biased, gated, ig_done, fc_done, cell_done, squashed, h_done, turned, hT_done = [
            sem("l_" + s) for s in ("summed", "biased", "gated", "ig_done", "fc_done", "cell_done", "squashed",
                                    "h_done", "turned", "hT_done")]
        saved = [sem(f"l_saved{e}") for e in range(EXPERTS)]
        block = open_block(nc, ctx, made)

        def load_x(sp, t, q, products):
            sp.wait_ge(summed, BASE + products)
            for d in range(2):
                pos = t if d == 0 else SEQ - 1 - t
                src = x_dram[:, ds(pos, 1)].rearrange("e a f k b -> f (e a) (k b)")
                sp.dma_start(xs[:, q, d].rearrange("p e k b -> p e (k b)"), src).then_inc(x_in[q][d], 16)

        def save_h(sp, t, e):
            sp.wait_ge(hT_done, BASE + t * EXPERTS + e + 1)
            for d in range(2):
                pos = t if d == 0 else SEQ - 1 - t
                sp.dma_start(mem_dram[e, d][ds(pos, 1)].rearrange("a f k b -> f (a k b)"),
                             hT[:, e, d].rearrange("p k b -> p (k b)")).then_inc(saved[e], 16)

        @block.sync
        def _(sp):
            load_x(sp, 0, 0, 0)
            for d, name in enumerate(("lstm_b_f", "lstm_b_b")):
                for e in range(EXPERTS):
                    for to, frm, width in COLUMNS:
                        sp.dma_start(bias[d * HALF:(d + 1) * HALF, e, to:to + width],
                                     io[name][e, frm:frm + width].partition_broadcast(HALF)).then_inc(bias_in, 16)
            for d, (wi, wh) in enumerate((("lstm_wi_f", "lstm_wh_f"), ("lstm_wi_b", "lstm_wh_b"))):
                for j, name in enumerate((wi, wh)):
                    for e in range(EXPERTS):
                        src = io[name][e].rearrange("(k p) n -> p k n", p=P)
                        dst = w[:, e, d, KD * j:KD * j + KD, :]
                        for to, frm, width in COLUMNS:
                            sp.dma_start(dst[:, :, to:to + width], src[:, :, frm:frm + width]).then_inc(w_in, 16)
            load_x(sp, 1, 1, 0)
            for e in range(EXPERTS):
                save_h(sp, 0, e)

            def trip(i, last):
                for r in range(2):
                    t = i * 2 + 1 + r
                    if not (last and r == 1):
                        load_x(sp, t + 1, r, t * EXPERTS)
                    for e in range(EXPERTS):
                        save_h(sp, t, e)

            with sp.Fori(0, TRIPS - 1) as i:
                trip(i, False)
            trip(TRIPS - 1, True)
            for e in range(EXPERTS):
                sp.wait_ge(saved[e], BASE + SEQ * 32)

        @block.gpsimd
        def _(pool):
            make_identity(pool, ident, id_zero, id_done)

        @block.tensor
        def _(pe):
            def products(t, e, first):
                v = t * EXPERTS + e
                z = v % 2 if first else e % 2
                if not first or e >= 2:
                    pe.wait_ge(biased, BASE + v - 1)
                for kk in range(2 * KD):
                    if kk == KD and first:
                        break
                    if kk == KD:
                        pe.wait_ge(hT_done, BASE + v - EXPERTS + 1)
                    for n in range(2):
                        for d in range(2):
                            lhsT = xs[:, PAR(t, first), d, e, kk, :] if kk < KD else hT[:, e, d, kk - KD, :]
                            mm = pe.matmul(ps[d * HALF:(d + 1) * HALF, 2 * z + n, :], lhsT,
                                           w[:, e, d, kk, n * 512:(n + 1) * 512], start=(kk == 0),
                                           stop=(kk == (KD if first else 2 * KD) - 1))
                mm.then_inc(summed, 1)

            def turn(v, par):
                pe.wait_ge(h_done, BASE + v + 1)
                for k in range(KD):
                    mm = pe.transpose(ps[:, 6 + par, k * P:(k + 1) * P], hid[:, par, k * P:(k + 1) * P], ident[:, :])
                mm.then_inc(turned, 1)

            PAR = lambda t, first: 0 if first else parity[0]
            parity = [0]
            pe.wait_ge(w_in, BASE + 16 * WLOADS)
            pe.wait_ge(id_done, BASE + 1)
            for d in range(2):
                pe.wait_ge(x_in[0][d], BASE + 16)
            for e in range(EXPERTS):
                products(0, e, True)
                if e:
                    if e >= 3:
                        pe.wait_ge(hT_done, BASE + e - 2)
                    turn(e - 1, (e - 1) % 2)
            with pe.Fori(0, TRIPS) as i:
                for r in range(2):
                    t, parity[0] = i * 2 + 1 + r, 1 - r
                    for d in range(2):
                        pe.wait_ge(x_in[1 - r][d], BASE + (i + 1 + r) * 16)
                    for e in range(EXPERTS):
                        v = t * EXPERTS + e
                        products(t, e, False)
                        pe.wait_ge(hT_done, BASE + v - 2)
                        turn(v - 1, (e - 1) % 2)
            turn(SEQ * EXPERTS - 1, 1)

        @block.vector
        def _(dve):
            dve.wait_ge(bias_in, BASE + 16 * 2 * EXPERTS * len(COLUMNS))

            def update(t, e, first):
                v, z = t * EXPERTS + e, e % 2
                gz = gates[:, z, :]
                dve.wait_ge(summed, BASE + v + 1)
                if not first or e >= 2:
                    dve.wait_ge(h_done, BASE + v - 1)
                dve.tensor_tensor(gz.rearrange("p (n c) -> p n c", n=2), ps[:, 2 * z:2 * z + 2, :],
                                  bias[:, e, :].rearrange("p (n c) -> p n c", n=2), ALU.add).then_inc(biased, 1)
                dve.wait_ge(gated, BASE + (v + 1) * 2)
                if first:
                    dve.tensor_tensor(cell[:, e, :], gz[:, 0:D], gz[:, 3 * D:4 * D], ALU.mult).then_inc(cell_done, 1)
                else:
                    dve.tensor_tensor(ig[:, :], gz[:, 0:D], gz[:, 3 * D:4 * D], ALU.mult).then_inc(ig_done, 1)
                    dve.tensor_tensor(cell[:, e, :], gz[:, D:2 * D], cell[:, e, :], ALU.mult).then_inc(fc_done, 1)
                    dve.wait_ge(ig_done, BASE + v - EXPERTS + 1)
                    dve.wait_ge(fc_done, BASE + v - EXPERTS + 1)
                    dve.tensor_tensor(cell[:, e, :], cell[:, e, :], ig[:, :], ALU.add).then_inc(cell_done, 1)
                dve.wait_ge(squashed, BASE + v + 1)
                if not first or e >= 2:
                    dve.wait_ge(turned, BASE + v - 1)
                dve.tensor_tensor(hid[:, z, :], gz[:, 2 * D:3 * D], tc[:, :], ALU.mult).then_inc(h_done, 1)

            for e in range(EXPERTS):
                update(0, e, True)
            with dve.Fori(0, TRIPS) as i:
                for r in range(2):
                    for e in range(EXPERTS):
                        update(i * 2 + 1 + r, e, False)

        @block.scalar
        def _(act):
            def keep_h(v, e, t):
                act.wait_ge(turned, BASE + v + 1)
                if t is not None:
                    act.wait_ge(saved[e], BASE + t * 32)
                act.copy(hT[:, e], ps[:, 6 + e % 2, 0:2 * P].rearrange("p (k d b) -> p d k b", k=KD, d=2)).then_inc(hT_done, 1)

            def squash(t, e):
                v, z = t * EXPERTS + e, e % 2
                act.wait_ge(biased, BASE + v + 1)
                act.activation(gates[:, z, 0:3 * D], gates[:, z, 0:3 * D], ACT.Sigmoid).then_inc(gated, 1)
                act.activation(gates[:, z, 3 * D:4 * D], gates[:, z, 3 * D:4 * D], ACT.Tanh).then_inc(gated, 1)
                act.wait_ge(cell_done, BASE + v + 1)
                act.wait_ge(h_done, BASE + v)
                act.activation(tc[:, :], cell[:, e, :], ACT.Tanh).then_inc(squashed, 1)

            for e in range(EXPERTS):
                if e:
                    keep_h(e - 1, e - 1, None)
                squash(0, e)
            with act.Fori(0, TRIPS) as i:
                for r in range(2):
                    t = i * 2 + 1 + r
                    for e in range(EXPERTS):
                        keep_h(t * EXPERTS + e - 1, (e - 1) % EXPERTS, t if e else t - 1)
                        squash(t, e)
            keep_h(SEQ * EXPERTS - 1, EXPERTS - 1, SEQ - 1)


HEAD_VECTORS = dict(sig_b1=(0, KD), sig_b2=(2, KD), tan_b1=(4, KD), tan_b2=(6, KD), dec_b1=(8, KD), dec_b2=(10, 1),
                    dec_g=(11, 1), dec_beta=(12, 1))
NHEAD = 13


def head_stage(nc, ps, io, h1_dram, z2_dram, mem_dram, out):
    TC = 5
    W = TC * IMAGES
    CHUNKS = SEQ // TC
    with ExitStack() as ctx:
        sb = lambda name, shape: ctx.enter_context(nc.sbuf_tensor(name, shape, F32))
        sem, made = semaphores(nc, ctx)
        ident = sb("h_ident", [P, P])
        h1 = sb("h_h1", [P, TOKENS])
        z2 = sb("h_z2", [P, TOKENS])
        s1 = sb("h_s1", [P, EXPERTS, 2 * KD, D])
        t1 = sb("h_t1", [P, EXPERTS, 2 * KD, D])
        s2 = sb("h_s2", [P, EXPERTS, KD, D])
        t2 = sb("h_t2", [P, EXPERTS, KD, D])
        d1 = sb("h_d1", [P, EXPERTS, KD, D])
        d2 = sb("h_d2", [P, EXPERTS, KD, P])
        d2_sum = sb("h_d2_sum", [P, EXPERTS, KD])
        d2_mean = sb("h_d2_mean", [P, EXPERTS, KD])
        vec_rows = sb("h_vec_rows", [EXPERTS * NHEAD, P])
        vec = sb("h_vec", [P, EXPERTS, NHEAD])
        b2c = sb("h_b2c", [P, EXPERTS])
        rw = sb("h_rw", [P, EXPERTS])
        rwb = sb("h_rwb", [P, EXPERTS, P])
        rb = sb("h_rb", [P, EXPERTS])
        mean = sb("h_mean", [P, P])
        eps = sb("h_eps", [P, 1])
        mem = sb("h_mem", [P, 2, 2, TC, KD, IMAGES])
        rs1 = sb("h_rs1", [P, KD, W])
        rt1 = sb("h_rt1", [P, KD, W])
        gs = sb("h_gs", [P, KD, W])
        gt = sb("h_gt", [P, KD, W])
        gg = sb("h_gg", [P, KD, W])
        rd1 = sb("h_rd1", [P, KD, W])
        dc = sb("h_dc", [P, EXPERTS, W])
        sq = sb("h_sq", [P, W])
        var = sb("h_var", [P, EXPERTS, W])
        sd = sb("h_sd", [P, EXPERTS, W])
        inv = sb("h_inv", [P, EXPERTS, W])
        y = sb("h_y", [P, EXPERTS, W])
        PAIRS_OUT = -(-TC // 2)
        acc = sb("h_acc", [P, PAIRS_OUT * P])
        logit = sb("h_logit", [P, EXPERTS, W])
        lg = sb("h_lg", [P, EXPERTS, W])
        lmax = sb("h_lmax", [P, W])
        lsum = sb("h_lsum", [P, W])
        linv = sb("h_linv", [P, W])
        rows = sb("h_rows", [P, PAIRS_OUT, P])
        names = ("s1_done s1_kept t1_done t1_kept s2_done s2_kept t2_done t2_kept d1_done d1_kept d2_done d2_kept "
                 "squared var_done var_kept gated logits logits_kept lmaxed lshifted lexped lsummed linverted "
                 "rooted inverted normed scaled stepped divided mixed turned rows_kept")
        S = {n: sem("h_" + n) for n in names.split()}
        w_in, v_in, r_in, id_zero, id_done, ones, prep, prep_pe = [
            sem("h_" + n) for n in ("w_in", "v_in", "r_in", "id_zero", "id_done", "ones", "prep", "prep_pe")]
        mem_in = [sem(f"h_mem_in{q}") for q in range(2)]
        out_done, vec_turned, vec_kept = sem("h_out_done"), sem("h_vec_turned"), sem("h_vec_kept")
        block = open_block(nc, ctx, made)
        E = EXPERTS
        tiles = lambda a: a.rearrange("p (t b) -> p t b", b=IMAGES)
        major = lambda a: a.rearrange("p (b s) -> p s b", s=SEQ)

        @block.sync
        def _(sp):
            for name, (at, k) in HEAD_VECTORS.items():
                for e in range(E):
                    row = e * NHEAD + at
                    sp.dma_start(vec_rows[row:row + k, :],
                                 io[name][e].rearrange("(k p) -> k p", p=P)).then_inc(v_in, 16)
            sp.dma_start(rw[:, :], io["router_w"]).then_inc(v_in, 16)
            sp.dma_start(rb[:, :], io["router_b"].partition_broadcast(P)).then_inc(v_in, 16)
            for dst, name in ((s1, "sig_w1"), (t1, "tan_w1"), (s2, "sig_w2"), (t2, "tan_w2"), (d1, "dec_w1"), (d2, "dec_w2")):
                sp.dma_start(dst[:, :, :, :].rearrange("p e k n -> p (e k) n"),
                             io[name].rearrange("e (k p) n -> p (e k) n", p=P)).then_inc(w_in, 16)
            sp.dma_start(h1[:, :], h1_dram).then_inc(r_in, 16)
            sp.dma_start(z2[:, :], z2_dram).then_inc(r_in, 16)
            with sp.Fori(0, CHUNKS) as c:
                for e in range(E):
                    sp.wait_ge(S["t1_done"], BASE + max(e - 1, 0) * KD + c * E * KD)
                    for d in range(2):
                        sp.dma_start(mem[:, e % 2, d].rearrange("p t k b -> p t (k b)"),
                                     mem_dram[e, d][ds(c * TC, TC)].rearrange("t f k b -> f t (k b)")).then_inc(mem_in[e % 2], 16)

        @block.gpsimd
        def _(pool):
            make_identity(pool, ident, id_zero, id_done)
            pool.memset(mean[:, :], 1.0 / P).then_inc(ones, 1)
            pool.memset(eps[:, :], EPS).then_inc(ones, 1)
            pool.memset(acc[:, :], 0.0).then_inc(ones, 1)
            pool.wait_ge(ones, BASE + 3)
            pool.wait_ge(v_in, BASE + 16 * (E * len(HEAD_VECTORS) + 2))
            pool.wait_ge(r_in, BASE + 32)
            pool.wait_ge(id_done, BASE + 1)

            def mix(c):
                pool.wait_ge(S["turned"], BASE + c)
                for e in range(1, E):
                    n = c * (E - 1) + e
                    pool.wait_ge(S["scaled"], BASE + c * E + e + 1)
                    if e > 1:
                        pool.wait_ge(S["stepped"], BASE + n - 1)
                    pool.tensor_tensor(acc[:, 0:W], y[:, 0, :] if e == 1 else acc[:, 0:W], y[:, e, :],
                                       ALU.add).then_inc(S["stepped"], 1)
                pool.wait_ge(S["stepped"], BASE + (c + 1) * (E - 1))
                pool.wait_ge(S["linverted"], BASE + c + 1)
                pool.tensor_tensor(acc[:, 0:W], acc[:, 0:W], linv[:, :], ALU.mult).then_inc(S["divided"], 1)
                pool.wait_ge(S["divided"], BASE + c + 1)
                pool.tensor_tensor(tiles(acc[:, 0:W]), tiles(acc[:, 0:W]), major(h1[:, :])[:, ds(c * TC, TC), :],
                                   ALU.add).then_inc(S["mixed"], 1)

            with pool.Fori(0, CHUNKS) as c:
                mix(c)

        @block.tensor
        def _(pe):
            pe.wait_ge(ones, BASE + 2)
            pe.wait_ge(v_in, BASE + 16 * (E * len(HEAD_VECTORS) + 2))
            pe.wait_ge(id_done, BASE + 1)
            pe.transpose(ps[:, 1, 0:E * NHEAD], vec_rows[:, :],
                         ident[0:E * NHEAD, 0:E * NHEAD]).then_inc(vec_turned, 1)
            pe.wait_ge(vec_kept, BASE + 1)
            for e in range(E):
                at, _ = HEAD_VECTORS["dec_b2"]
                mm = pe.matmul(ps[:, 0, e:e + 1], mean[:, :], vec[:, e, at:at + 1], start=True, stop=True)
            mm.then_inc(prep_pe, 1)
            pe.wait_ge(w_in, BASE + 96)
            pe.wait_ge(prep, BASE + 8 + 2)
            pe.wait_ge(r_in, BASE + 32)
            pe.wait_ge(id_done, BASE + 1)

            def group(done, banks, stat, moving, nk):
                for m, bank in enumerate(banks):
                    for k in range(nk):
                        mm = pe.matmul(ps[:, bank, 0:W], stat(k, m), moving(k), start=(k == 0), stop=(k == nk - 1))
                    mm.then_inc(S[done], 1)

            def decode(p, e, step):
                if step == 0:
                    pe.wait_ge(S["gated"], BASE + p + 1)
                    group("d1_done", (6, 7), lambda k, m: d1[:, e, k, m * P:(m + 1) * P], lambda k: gg[:, k, :], KD)
                elif step == 1:
                    pe.wait_ge(S["d1_kept"], BASE + (p + 1) * KD)
                    group("d2_done", (6,), lambda k, m: d2[:, e, k, :], lambda k: rd1[:, k, :], KD)
                else:
                    pe.wait_ge(S["squared"], BASE + p + 1)
                    group("var_done", (7,), lambda k, m: mean[:, :], lambda k: sq[:, :], 1)

            def chunk(c, first):
                for e in range(E):
                    n = c * E + e
                    prev, before = not (first and e == 0), (e - 1) % E
                    q = e % 2
                    pe.wait_ge(mem_in[q], BASE + (c * 2 + e // 2 + 1) * 32)
                    mv = lambda k, q=q: mem[:, q, k // KD, :, k % KD, :]
                    pe.wait_ge(S["s1_kept"], BASE + n * KD)
                    group("s1_done", (0, 1), lambda k, m: s1[:, e, k, m * P:(m + 1) * P], mv, 2 * KD)
                    if prev:
                        pe.wait_ge(S["logits_kept"], BASE + n)
                        pe.wait_ge(S["var_kept"], BASE + n - 1)
                        if e == 0:
                            pe.wait_ge(S["rows_kept"], BASE + c - 1)
                        decode(n - 1, before, 0)
                    pe.wait_ge(S["t1_kept"], BASE + n * KD)
                    group("t1_done", (2, 3), lambda k, m: t1[:, e, k, m * P:(m + 1) * P], mv, 2 * KD)
                    if prev:
                        decode(n - 1, before, 1)
                    pe.wait_ge(S["s1_kept"], BASE + (n + 1) * KD)
                    pe.wait_ge(S["t2_kept"], BASE + n * KD)
                    group("s2_done", (4, 5), lambda k, m: s2[:, e, k, m * P:(m + 1) * P], lambda k: rs1[:, k, :], KD)
                    if prev:
                        decode(n - 1, before, 2)
                        pe.wait_ge(S["d2_kept"], BASE + n)
                    pe.matmul(ps[:, 6, 0:W], rwb[:, e, :], major(z2[:, :])[:, ds(c * TC, TC), :],
                              start=True, stop=True).then_inc(S["logits"], 1)
                    pe.wait_ge(S["t1_kept"], BASE + (n + 1) * KD)
                    pe.wait_ge(S["s2_kept"], BASE + (n + 1) * KD)
                    group("t2_done", (4, 5), lambda k, m: t2[:, e, k, m * P:(m + 1) * P], lambda k: rt1[:, k, :], KD)
                if not first:
                    turn_out(c - 1, c * E + E - 1)

            def turn_out(c, variances):
                pe.wait_ge(S["mixed"], BASE + c + 1)
                pe.wait_ge(S["var_kept"], BASE + variances)
                for j in range(PAIRS_OUT):
                    mm = pe.transpose(ps[:, 7, j * P:(j + 1) * P], acc[:, j * P:(j + 1) * P], ident[:, :])
                mm.then_inc(S["turned"], 1)

            chunk(0, True)
            with pe.Fori(0, CHUNKS - 1) as i:
                chunk(i + 1, False)
            LAST = CHUNKS * E - 1
            pe.wait_ge(S["logits_kept"], BASE + LAST + 1)
            pe.wait_ge(S["var_kept"], BASE + LAST)
            pe.wait_ge(S["rows_kept"], BASE + CHUNKS - 1)
            for step in range(3):
                decode(LAST, E - 1, step)
            turn_out(CHUNKS - 1, LAST + 1)

        @block.vector
        def _(dve):
            dve.wait_ge(vec_turned, BASE + 1)
            dve.tensor_copy(vec[:, :, :], ps[:, 1, 0:E * NHEAD].rearrange("p (e v) -> p e v", v=NHEAD)).then_inc(vec_kept, 1)
            dve.wait_ge(v_in, BASE + 16 * (E * len(HEAD_VECTORS) + 2))
            dve.tensor_copy(rwb[:, :, :], rw[:, :].unsqueeze(2).broadcast_to([P, E, P])).then_inc(prep, 1)
            dve.wait_ge(prep_pe, BASE + 1)
            at, _ = HEAD_VECTORS["dec_b2"]
            dve.tensor_tensor(b2c[:, :], vec[:, :, at], ps[:, 0, 0:E], ALU.subtract).then_inc(prep, 1)
            dve.wait_ge(w_in, BASE + 96)
            dve.tensor_reduce(d2_sum[:, :, :], d2[:, :, :, :], AX.X, ALU.add).then_inc(prep, 1)
            dve.wait_ge(prep, BASE + 3)
            dve.tensor_scalar(d2_mean[:, :, :], d2_sum[:, :, :], 1.0 / P, None, ALU.mult).then_inc(prep, 1)
            dve.wait_ge(prep, BASE + 4)
            dve.tensor_tensor(d2[:, :, :, :], d2[:, :, :, :], d2_mean[:, :, :].unsqueeze(3).broadcast_to([P, E, KD, P]),
                              ALU.subtract).then_inc(prep, 6)

            def relu(n, e, done, kept, banks, dst, name):
                at, _ = HEAD_VECTORS[name]
                for m, bank in enumerate(banks):
                    dve.wait_ge(S[done], BASE + n * KD + m + 1)
                    dve.tensor_scalar(dst[:, m, :], ps[:, bank, 0:W], vec[:, e, at + m:at + m + 1], 0.0,
                                      ALU.add, ALU.max).then_inc(S[kept], 1)

            over = lambda a: a[:, :, :].rearrange("p e w -> p w e")
            all_ = lambda a: a[:, :].unsqueeze(1).broadcast_to([P, E, W])

            def shift_logits(c):
                dve.wait_ge(S["logits_kept"], BASE + (c + 1) * E)
                dve.tensor_reduce(lmax[:, :], over(logit), AX.X, ALU.max).then_inc(S["lmaxed"], 1)
                dve.wait_ge(S["lmaxed"], BASE + c + 1)
                dve.tensor_tensor(lg[:, :, :], logit[:, :, :], all_(lmax), ALU.subtract).then_inc(S["lshifted"], 1)

            def invert_sum(c):
                dve.wait_ge(S["lexped"], BASE + c + 1)
                dve.tensor_reduce(lsum[:, :], over(lg), AX.X, ALU.add).then_inc(S["lsummed"], 1)
                dve.wait_ge(S["lsummed"], BASE + c + 1)
                dve.wait_ge(S["mixed"], BASE + c)
                dve.reciprocal(linv[:, :], lsum[:, :]).then_inc(S["linverted"], 1)

            def scale(c, e):
                n = c * E + e
                dve.wait_ge(S["rooted"], BASE + c + 1)
                dve.reciprocal(inv[:, e, :], sd[:, e, :]).then_inc(S["inverted"], 1)
                dve.wait_ge(S["inverted"], BASE + n + 1)
                dve.wait_ge(S["mixed"], BASE + c)
                at, _ = HEAD_VECTORS["dec_g"]
                dve.scalar_tensor_tensor(out=y[:, e, :], in0=dc[:, e, :], scalar=vec[:, e, at:at + 1],
                                         in1=inv[:, e, :], op0=ALU.mult, op1=ALU.mult).then_inc(S["normed"], 1)
                dve.wait_ge(S["normed"], BASE + n + 1)
                dve.scalar_tensor_tensor(out=y[:, e, :], in0=y[:, e, :], scalar=vec[:, e, at + 1:at + 2],
                                         in1=lg[:, e, :], op0=ALU.add, op1=ALU.mult).then_inc(S["scaled"], 1)

            def keep_d2(p, e):
                dve.wait_ge(S["d2_done"], BASE + p + 1)
                dve.tensor_scalar(dc[:, e, :], ps[:, 6, 0:W], b2c[:, e:e + 1], None, ALU.add).then_inc(S["d2_kept"], 1)

            def keep_var(p, e):
                dve.wait_ge(S["var_done"], BASE + p + 1)
                dve.tensor_copy(var[:, e, :], ps[:, 7, 0:W]).then_inc(S["var_kept"], 1)

            def chunk(c, first):
                for e in range(E):
                    n = c * E + e
                    prev, before = not (first and e == 0), (e - 1) % E
                    if not first:
                        if e == 0:
                            shift_logits(c - 1)
                        elif e < 3:
                            scale(c - 1, 2 * e - 2)
                    if prev:
                        relu(n - 1, before, "d1_done", "d1_kept", (6, 7), rd1, "dec_b1")
                    dve.wait_ge(S["t2_done"], BASE + n * KD)
                    relu(n, e, "t1_done", "t1_kept", (2, 3), rt1, "tan_b1")
                    if prev:
                        keep_d2(n - 1, before)
                        if not first and e == 1:
                            dve.wait_ge(S["rooted"], BASE + c)
                        keep_var(n - 1, before)
                    dve.wait_ge(S["logits"], BASE + n + 1)
                    dve.tensor_scalar(logit[:, e, :], ps[:, 6, 0:W], rb[:, e:e + 1], None,
                                      ALU.add).then_inc(S["logits_kept"], 1)
                    dve.wait_ge(S["t2_kept"], BASE + (n + 1) * KD)
                    dve.tensor_tensor(gg[:, :, :], gs[:, :, :], gt[:, :, :], ALU.mult).then_inc(S["gated"], 1)
                    if not first:
                        if e == 0:
                            invert_sum(c - 1)
                        elif e < 3:
                            scale(c - 1, 2 * e - 1)

            chunk(0, True)
            with dve.Fori(0, CHUNKS - 1) as i:
                chunk(i + 1, False)
            LAST = CHUNKS * E - 1
            shift_logits(CHUNKS - 1)
            relu(LAST, E - 1, "d1_done", "d1_kept", (6, 7), rd1, "dec_b1")
            keep_d2(LAST, E - 1)
            keep_var(LAST, E - 1)
            invert_sum(CHUNKS - 1)
            for e in range(E):
                scale(CHUNKS - 1, e)

        @block.scalar
        def _(act):
            def leave(n, e, done, kept, banks, dst, name, func):
                at, _ = HEAD_VECTORS[name]
                for m, bank in enumerate(banks):
                    act.wait_ge(S[done], BASE + n * KD + m + 1)
                    act.activation(dst[:, m, :], ps[:, bank, 0:W], func, bias=vec[:, e, at + m:at + m + 1]).then_inc(S[kept], 1)

            def exponentials(c):
                act.wait_ge(S["lshifted"], BASE + c + 1)
                act.activation(lg[:, :, :], lg[:, :, :], ACT.Exp).then_inc(S["lexped"], 1)

            def square(p, e):
                act.wait_ge(S["d2_kept"], BASE + p + 1)
                act.wait_ge(S["var_done"], BASE + p)
                act.activation(sq[:, :], dc[:, e, :], ACT.Square).then_inc(S["squared"], 1)

            def roots(c):
                act.wait_ge(S["var_kept"], BASE + (c + 1) * E)
                act.wait_ge(S["inverted"], BASE + c * E)
                act.activation(sd[:, :, :], var[:, :, :], ACT.Sqrt, bias=eps[:, 0:1]).then_inc(S["rooted"], 1)

            def rows_out(c):
                act.wait_ge(S["turned"], BASE + c + 1)
                act.wait_ge(out_done, BASE + c * 32)
                act.copy(rows[:, :, :], ps[:, 7, 0:PAIRS_OUT * P].rearrange("p (j f) -> p j f", f=P)).then_inc(S["rows_kept"], 1)
                act.wait_ge(S["rows_kept"], BASE + c + 1)
                here = out[:, ds(c * TC, TC), :]
                for odd in range(2):
                    act.dma_start(here[:, odd:TC:2, :],
                                  rows[odd * IMAGES:(odd + 1) * IMAGES, 0:(TC + 1 - odd) // 2, :]).then_inc(out_done, 16)

            def chunk(c, first):
                for e in range(E):
                    n = c * E + e
                    leave(n, e, "s1_done", "s1_kept", (0, 1), rs1, "sig_b1", ACT.Relu)
                    if e == 0 and not first:
                        exponentials(c - 1)
                    if not (first and e == 0):
                        square(n - 1, (e - 1) % E)
                    act.wait_ge(S["gated"], BASE + n)
                    leave(n, e, "s2_done", "s2_kept", (4, 5), gs, "sig_b2", ACT.Sigmoid)
                    leave(n, e, "t2_done", "t2_kept", (4, 5), gt, "tan_b2", ACT.Tanh)
                    if e == 0 and not first:
                        roots(c - 1)
                if not first:
                    rows_out(c - 1)

            act.wait_ge(ones, BASE + 2)
            act.wait_ge(vec_kept, BASE + 1)
            chunk(0, True)
            with act.Fori(0, CHUNKS - 1) as i:
                chunk(i + 1, False)
            exponentials(CHUNKS - 1)
            square(CHUNKS * E - 1, E - 1)
            roots(CHUNKS - 1)
            rows_out(CHUNKS - 1)
            act.wait_ge(out_done, BASE + CHUNKS * 32)


def vit_tower(nc, inputs, out):
    first = dict(x="x", tok_W="L0_tok_W", tok_b="L0_tok_b", cls="L0_tok_class_token", pos="L0_tok_pos_embed",
                 w_qkv="L0_attn_w_qkv", w_agg="L0_attn_w_agg", b_agg="L0_attn_b_agg")
    experts = {name[len("L0_ffn_"):]: ap for name, ap in inputs.items() if name.startswith("L0_ffn_")}
    scratch = lambda name, *shape: nc.dram_tensor(name, shape, F32).ap()
    h1 = scratch("h1_scratch", P, TOKENS)
    z2 = scratch("z2_scratch", P, TOKENS)
    x = scratch("x_scratch", EXPERTS, SEQ, P, KD, IMAGES)
    mem = scratch("mem_scratch", EXPERTS, 2, SEQ, P, KD, IMAGES)
    with nc.psum_tensor("banks", [P, 8, 512], F32) as ps:
        stages(nc, ps, first, experts, inputs, h1, z2, x, mem, out)


def stages(nc, ps, first, experts, inputs, h1, z2, x, mem, out):
    front(nc, ps, {key: inputs[name] for key, name in first.items()}, h1, z2)
    experts_stage(nc, ps, experts, z2, x)
    lstm_stage(nc, ps, experts, x, mem)
    head_stage(nc, ps, experts, h1, z2, mem, out)


_FFN = ("router_w router_b enc_w1 enc_b1 enc_w2 enc_b2 enc_g enc_beta attn_in_w attn_in_b attn_out_w attn_out_b "
        "lstm_wi_f lstm_wh_f lstm_b_f lstm_wi_b lstm_wh_b lstm_b_b sig_w1 sig_b1 sig_w2 sig_b2 tan_w1 tan_b1 tan_w2 "
        "tan_b2 dec_w1 dec_b1 dec_w2 dec_b2 dec_g dec_beta").split()
_INS = ["x", "L0_tok_W", "L0_tok_b", "L0_tok_class_token", "L0_tok_pos_embed", "L0_attn_w_qkv", "L0_attn_w_agg",
        "L0_attn_b_agg"] + ["L0_ffn_" + n for n in _FFN]
_OUTS = [((64, 65, 128), "float32")]


def kernel(**inputs):
    import numpy as _np
    import concourse.bacc as _bacc
    from concourse import mybir as _mybir
    from concourse.bass_utils import run_bass_kernel_spmd as _run

    nc = _bacc.Bacc("TRN2", target_bir_lowering=False, num_devices=1)
    arrays, args = {}, {}
    for name in _INS:
        a = _np.ascontiguousarray(inputs[name])
        arrays[f"in_{name}_dram"] = a
        args[name] = nc.dram_tensor(f"in_{name}_dram", a.shape, _mybir.dt.from_np(a.dtype), kind="ExternalInput").ap()
    (shape, dtype), = _OUTS
    out = nc.dram_tensor("out_0_dram", shape, _mybir.dt.from_np(_np.dtype(dtype)), kind="ExternalOutput").ap()
    vit_tower(nc, args, out)
    r = _run(nc, [arrays], core_ids=[0])
    return r.results[0]["out_0_dram"]
```

```python
from contextlib import ExitStack

import concourse.bass as bass
from concourse import mybir

F32 = mybir.dt.float32
F16 = mybir.dt.float16
I32 = mybir.dt.int32
ALU = mybir.AluOpType
ACT = mybir.ActivationFunctionType
AX = mybir.AxisListType
ds = bass.ds

P = 128
IMAGES, CHANNELS, GRID, PATCH = 64, 3, 8, 28
ROWS = CHANNELS * PATCH
SIDE = GRID * PATCH
SEQ = GRID * GRID + 1
TOKENS = IMAGES * SEQ
HID = 128
D = 256
KD = D // P
EXPERTS = 4
HEAD = 16
EPS = 1e-5
BASE = 4
SCALE = HEAD ** -0.5

GROUP = 4
UNIT = GROUP * SEQ
WIDE = 416
WSTEPS = TOKENS // WIDE
PASSES = ((0, 0), (1, 0), (0, 1))
TOP = 2.0 ** 13
TINY = 2.0 ** -50
NORMED = TOP / 16
EXPONENT = 0x7F800000

DEPTH = 2
RING = 4
assert WSTEPS * WIDE == TOKENS and (WSTEPS - DEPTH) % RING == 0


def semaphores(nc, ctx, tag=""):
    made = []

    def sem(name):
        made.append(ctx.enter_context(nc.semaphore(tag + name)))
        return made[-1]
    return sem, made


def open_block(nc, ctx, made):
    def clear():
        with nc.Block() as block:
            @block.sync
            def _(sp):
                for s in made:
                    sp.sem_clear(s)
    ctx.callback(clear)
    with nc.Block() as block:
        @block.sync
        def _(sp):
            for s in made:
                sp.sem_inc(s, BASE)
    return ctx.enter_context(nc.Block())


def wide_steps(eng, body):
    for k in range(DEPTH):
        body(k, k % RING, lambda j, k=k: j <= k)
    with eng.Fori(0, (WSTEPS - DEPTH) // RING) as i:
        for r in range(RING):
            body(i * RING + (DEPTH + r), (DEPTH + r) % RING, lambda j: True)
    for k in range(WSTEPS, WSTEPS + DEPTH):
        body(k, k % RING, lambda j, k=k: k - j < WSTEPS)


def make_identity(pool, tile, zeroed, done):
    pool.memset(tile[:, :], 0.0).then_inc(zeroed, 1)
    pool.wait_ge(zeroed, BASE + 1)
    pool.affine_select(out=tile[:, :], in_=tile[:, :], compare_op=ALU.not_equal, fill=1.0, base=0,
                       pattern=[[-1, P]], channel_multiplier=1).then_inc(done, 1)


def tokens_stage(nc, ps, io, h0, ident):
    XI = 4
    SLOTS = 2
    PADDED = 96
    TRIPS = IMAGES // XI // SLOTS
    NP = GRID * GRID
    with ExitStack() as ctx:
        sb = lambda name, shape: ctx.enter_context(nc.sbuf_tensor(name, shape, F32))
        sem, made = semaphores(nc, ctx)
        image = sb("image", [PADDED, SLOTS, XI, GRID, SIDE])
        w_rows = sb("w_rows", [P, ROWS * PATCH])
        w_cols = sb("w_cols", [PADDED, PATCH, P])
        pos_rows = sb("pos_rows", [SEQ, P])
        pos = sb("pos", [P, SEQ])
        bias = sb("tok_bias", [P, 1])
        cls = sb("cls", [P, 1])
        clsp = sb("clsp", [P, 1])
        loaded = [sem(f"image_loaded{i}") for i in range(SLOTS)]
        consts, w_in = sem("consts_loaded"), sem("w_loaded")
        id_zero, id_done = sem("id_zeroed"), sem("id_done")
        turned, kept = sem("w_turned"), sem("w_kept")
        padded = sem("rows_padded")
        summed, stored, cls_done = sem("tok_summed"), sem("tok_stored"), sem("cls_done")
        block = open_block(nc, ctx, made)
        turns = PATCH // 4

        @block.sync
        def _(sp):
            sp.dma_start(w_rows[:, :], io["tok_W"]).then_inc(w_in, 16)
            sp.dma_start(pos_rows[:, :], io["pos"]).then_inc(consts, 16)
            sp.dma_start(bias[:, :], io["tok_b"].rearrange("(p a) -> p a", a=1)).then_inc(consts, 16)
            sp.dma_start(cls[:, :], io["cls"].rearrange("a p -> p a")).then_inc(consts, 16)

            def load(chunk, s, first=False):
                for c in range(CHANNELS):
                    if first and c == CHANNELS - 1:
                        sp.wait_ge(padded, BASE + 3)
                    for b in range(XI):
                        src = io["x"][ds(chunk * XI + b, 1), c].rearrange("a (g p) w -> p (a g) w", p=PATCH)
                        sp.dma_start(image[c * PATCH:(c + 1) * PATCH, s, b], src).then_inc(loaded[s], 16)

            for s in range(SLOTS):
                load(s, s, s == 0)
            with sp.Fori(0, TRIPS - 1) as i:
                for s in range(SLOTS):
                    sp.wait_ge(summed, BASE + i * SLOTS + s + 1)
                    load((i + 1) * SLOTS + s, s)

        @block.gpsimd
        def _(pool):
            make_identity(pool, ident, id_zero, id_done)
            pool.wait_ge(id_done, BASE + 1)
            pool.memset(image[64:PADDED, 1], 0.0).then_inc(padded, 1)

        @block.tensor
        def _(pe):
            pe.wait_ge(w_in, BASE + 16)
            pe.wait_ge(id_done, BASE + 1)
            w_view = w_rows[:, :].rearrange("p (r q) -> p r q", q=PATCH)
            for g in range(turns):
                if g >= 4:
                    pe.wait_ge(kept, BASE + g - 3)
                for j in range(4):
                    m = pe.transpose(ps[0:ROWS, g % 4, j * P:(j + 1) * P], w_view[:, :, 4 * g + j], ident[:, :])
                m.then_inc(turned, 1)
            pe.wait_ge(consts, BASE + 48)
            pe.wait_ge(kept, BASE + turns)
            pe.transpose(ps[:, 0, 0:SEQ], pos_rows[:, :], ident[0:SEQ, 0:SEQ]).then_inc(turned, 1)
            pe.wait_ge(kept, BASE + turns + 1)
            with pe.Fori(0, TRIPS) as i:
                for s in range(SLOTS):
                    pe.wait_ge(loaded[s], BASE + (i + 1) * 16 * CHANNELS * XI)
                    pe.wait_ge(stored, BASE + i * SLOTS)
                    cols = image[:, s].rearrange("p b g (j q) -> p b g j q", q=PATCH)
                    for q in range(PATCH):
                        m = pe.matmul(ps[:, s % 2, 0:XI * NP], w_cols[:, q, :], cols[:, :, :, :, q],
                                      start=(q == 0), stop=(q == PATCH - 1))
                    m.then_inc(summed, 1)

        @block.vector
        def _(dve):
            dve.memset(image[64:PADDED, 0], 0.0).then_inc(padded, 1)
            dve.memset(w_cols[64:PADDED], 0.0).then_inc(padded, 1)
            dve.wait_ge(padded, BASE + 3)
            for g in range(turns):
                dve.wait_ge(turned, BASE + g + 1)
                dve.tensor_copy(w_cols[0:ROWS, 4 * g:4 * g + 4, :],
                                ps[0:ROWS, g % 4, :].rearrange("p (j m) -> p j m", j=4)).then_inc(kept, 1)
            dve.wait_ge(turned, BASE + turns + 1)
            dve.tensor_copy(pos[:, :], ps[:, 0, 0:SEQ]).then_inc(kept, 1)
            dve.wait_ge(kept, BASE + turns + 1)
            dve.tensor_tensor(clsp[:, :], cls[:, :], pos[:, 0:1], ALU.mult).then_inc(cls_done, 1)
            dve.wait_ge(cls_done, BASE + 1)
            h0_view = h0[:, :].rearrange("p (b s) -> p b s", s=SEQ)
            dve.tensor_copy(h0_view[:, :, 0], clsp[:, :].broadcast_to([P, IMAGES])).then_inc(cls_done, 1)
            with dve.Fori(0, TRIPS) as i:
                for s in range(SLOTS):
                    dve.wait_ge(summed, BASE + i * SLOTS + s + 1)
                    out = h0[:, ds((i * SLOTS + s) * XI * SEQ, XI * SEQ)].rearrange("p (b s) -> p b s", s=SEQ)
                    dve.scalar_tensor_tensor(
                        out=out[:, :, 1:SEQ], in0=ps[:, s % 2, 0:XI * NP].rearrange("p (b t) -> p b t", t=NP),
                        scalar=bias[:, 0:1], in1=pos[:, 1:SEQ].unsqueeze(1).broadcast_to([P, XI, NP]),
                        op0=ALU.add, op1=ALU.mult).then_inc(stored, 1)


def norm_stage(nc, ps, tag, src, dst, add, spill):
    with ExitStack() as ctx:
        sb = lambda name, shape: ctx.enter_context(nc.sbuf_tensor(tag + name, shape, F32))
        sem, made = semaphores(nc, ctx, tag)
        center = sb("center", [P, P])
        mean = sb("mean", [P, P])
        eps = sb("eps", [P, 1])
        xc = sb("xc", [P, 2, WIDE])
        sq = sb("sq", [P, 2, WIDE])
        sd = sb("sd", [P, 2, WIDE])
        rs = sb("rs", [P, 2, WIDE])
        zero, ready = sem("zero"), sem("ready")
        added, centered, copied = sem("added"), sem("centered"), sem("copied")
        squared, varied, rooted = sem("squared"), sem("varied"), sem("rooted")
        inverted, normed, spilled = sem("inverted"), sem("normed"), sem("spilled")
        block = open_block(nc, ctx, made)

        @block.gpsimd
        def _(pool):
            pool.memset(mean[:, :], 1.0 / P).then_inc(ready, 1)
            pool.memset(eps[:, :], EPS).then_inc(ready, 1)
            pool.memset(center[:, :], -1.0 / P).then_inc(zero, 1)
            pool.wait_ge(zero, BASE + 1)
            pool.affine_select(out=center[:, :], in_=center[:, :], compare_op=ALU.not_equal, fill=1.0 - 1.0 / P,
                               base=0, pattern=[[-1, P]], channel_multiplier=1).then_inc(ready, 1)

            def body(k, slot, live):
                par = slot % 2
                if add is not None and live(0):
                    at = ds(k * WIDE, WIDE)
                    pool.tensor_tensor(src[:, at], src[:, at], add[:, at], ALU.add).then_inc(added, 1)
                if live(2):
                    pool.wait_ge(inverted, BASE + k - 1)
                    pool.tensor_tensor(dst[:, ds((k - 2) * WIDE, WIDE)], xc[:, par, :], rs[:, par, :],
                                       ALU.mult).then_inc(normed, 1)
            wide_steps(pool, body)

        @block.tensor
        def _(pe):
            pe.wait_ge(ready, BASE + 3)

            def body(k, slot, live):
                par = slot % 2
                if live(0):
                    if add is not None:
                        pe.wait_ge(added, BASE + k + 1)
                    if live(2):
                        pe.wait_ge(copied, BASE + k - 1)
                    pe.matmul(ps[:, par, 0:WIDE], center[:, :], src[:, ds(k * WIDE, WIDE)],
                              start=True, stop=True).then_inc(centered, 1)
                if live(1):
                    pe.wait_ge(squared, BASE + k)
                    if live(3):
                        pe.wait_ge(rooted, BASE + k - 2)
                    pe.matmul(ps[:, 3 - par, 0:WIDE], mean[:, :], sq[:, 1 - par, :],
                              start=True, stop=True).then_inc(varied, 1)
            wide_steps(pe, body)

        @block.scalar
        def _(act):
            def body(k, slot, live):
                par = slot % 2
                if live(1):
                    act.wait_ge(varied, BASE + k)
                    if live(3):
                        act.wait_ge(inverted, BASE + k - 2)
                    act.activation(sd[:, 1 - par, :], ps[:, 3 - par, 0:WIDE], ACT.Sqrt,
                                   bias=eps[:, 0:1]).then_inc(rooted, 1)
                if live(0):
                    act.wait_ge(centered, BASE + k + 1)
                    if live(2):
                        act.wait_ge(normed, BASE + k - 1)
                    act.copy(xc[:, par, :], ps[:, par, 0:WIDE]).then_inc(copied, 1)
                    act.wait_ge(copied, BASE + k + 1)
                    act.activation(sq[:, par, :], xc[:, par, :], ACT.Square).then_inc(squared, 1)
            wide_steps(act, body)

        @block.vector
        def _(dve):
            def body(k, slot, live):
                par = slot % 2
                if live(1):
                    dve.wait_ge(rooted, BASE + k)
                    if live(3):
                        dve.wait_ge(normed, BASE + k - 2)
                    dve.reciprocal(rs[:, 1 - par, :], sd[:, 1 - par, :]).then_inc(inverted, 1)
            wide_steps(dve, body)

        if spill:
            @block.sync
            def _(sp):
                sp.wait_ge(normed, BASE + WSTEPS)
                sp.dma_start(spill[0], src[:, :]).then_inc(spilled, 16)
                sp.dma_start(spill[1], dst[:, :]).then_inc(spilled, 16)
                sp.wait_ge(spilled, BASE + 32)


class Attention:
    UNITS = IMAGES // GROUP
    HALF = 4
    CLS = 32

    def __init__(self, nc, ctx, make_sem, tag, C, split=False):
        sb = lambda name, shape, dt=F32: ctx.enter_context(nc.sbuf_tensor(tag + name, shape, dt))
        self.split = split
        self.passes = PASSES if split else ((0, 0),)
        sem = lambda name: make_sem(tag + name)
        self.C, self.NH = C, P // HEAD
        self.steps = GROUP * C
        self.TURN = 3 if self.steps > 4 else 2
        self.WEIGH = self.TURN + 1
        assert self.steps % 4 == 0
        self.x = sb("x", [P, 2, 2, C, UNIT], F16) if split else sb("x", [P, 2, 1, C, UNIT])
        self.q = sb("q", [P, 2, C, UNIT])
        self.k = sb("k", [P, 2, C, UNIT])
        self.km = sb("km", [P, 2, self.NH, SEQ])
        self.qc = sb("qc", [P, 2, GROUP, self.CLS])
        self.v = sb("v", [SEQ, 2 * GROUP, C * 4, 4, HEAD])
        self.p = sb("p", [P, 4, self.HALF + 1, SEQ])
        self.pt = sb("pt", [SEQ, GROUP, C, self.NH, SEQ])
        self.o = sb("o", [P, 2, C, UNIT])
        self.mx = sb("mx", [P, 2, self.HALF + 1])
        self.sm = sb("sm", [P, 4, self.HALF + 1])
        self.ri = sb("ri", [P, 4, self.HALF + 1])
        self.mask = sb("mask", [P, self.CLS])
        (self.v_zeroed, self.mask_done, self.x_high, self.x_copied, self.keys_masked, self.class_masked, self.scored, self.maxed,
         self.shifted, self.exped, self.summed, self.inverted, self.normed, self.turned, self.turn_kept,
         self.class_turned, self.class_kept, self.weighed, self.o_kept, self.piece_done, self.piece_kept, self.out_done, self.out_kept) = [
             sem(n) for n in (
                 "v_zeroed", "mask_done", "x_high", "x_copied", "keys_masked", "class_masked", "scored", "maxed", "shifted", "exped",
                 "summed", "inverted", "normed", "turned", "turn_kept", "class_turned", "class_kept", "weighed", "o_kept", "piece_done",
                 "piece_kept", "out_done", "out_kept")]
        self.order = [("q", c) for c in range(C)] + [("k", c) for c in range(C)] + [("v", b) for b in range(GROUP)]
        self.pieces = len(self.order)
        self.index = {x: n for n, x in enumerate(self.order)}
        assert self.pieces % 2 == 0
        per = -(-self.pieces // self.steps)
        self.after = [self.order[s * per:(s + 1) * per] for s in range(self.steps)]

    def place(self, s):
        return s % self.steps // self.C, s % self.C

    def slots(self, s):
        return self.HALF + (s % self.steps < self.C)

    def run(self, eng, base, unit):
        unit(base, 0, 0, True, False)
        with eng.Fori(0, self.UNITS // 2 - 1) as i:
            for r in range(2):
                unit(base + i * 2 + 1 + r, i * 2 + 1 + r, 1 - r, False, False)
        unit(base + self.UNITS - 1, self.UNITS - 1, 1, False, True)

    def pool_setup(self, pool):
        pool.memset(self.v[:, :, :, :, :], 0.0).then_inc(self.v_zeroed, 1)
        pool.memset(self.mask[:, :], 1.0).then_inc(self.mask_done, 1)
        pool.wait_ge(self.mask_done, BASE + 1)
        pool.affine_select(out=self.mask[:, :], in_=self.mask[:, :], compare_op=ALU.is_ge, fill=0.0, base=0,
                           pattern=[[-HEAD, self.CLS]], channel_multiplier=1).then_inc(self.mask_done, 1)
        pool.wait_ge(self.mask_done, BASE + 2)
        pool.affine_select(out=self.mask[:, :], in_=self.mask[:, :], compare_op=ALU.is_ge, fill=0.0, base=HEAD - 1,
                           pattern=[[HEAD, self.CLS]], channel_multiplier=-1).then_inc(self.mask_done, 1)
        pool.wait_ge(self.mask_done, BASE + 3)

    def pool_run(self, pool, base):
        C, n, NP = self.C, self.steps, self.pieces

        def mask_keys(unit, par, s, start):
            b, c = self.place(s)
            pool.wait_ge(self.piece_kept, BASE + unit * NP + self.index["k", c] + 1)
            pool.wait_ge(self.scored, BASE + unit * n + (0 if start else s - 1))
            if s < C:
                pool.tensor_tensor(
                    self.qc[:, s % 2],
                    self.q[:, par, c, 0:UNIT:SEQ].unsqueeze(2).broadcast_to([P, GROUP, self.CLS]),
                    self.mask[:, :].unsqueeze(1).broadcast_to([P, GROUP, self.CLS]), ALU.mult).then_inc(self.class_masked, 1)
            pool.tensor_tensor(
                self.km[:, s % 2],
                self.k[:, par, c, b * SEQ:(b + 1) * SEQ].unsqueeze(1).broadcast_to([P, self.NH, SEQ]),
                self.mask[:, 0:self.NH].unsqueeze(2).broadcast_to([P, self.NH, SEQ]), ALU.mult).then_inc(self.keys_masked, 1)

        def norm(unit, s):
            pool.wait_ge(self.inverted, BASE + unit * n + s)
            v, k = (s - 1) % 4, self.slots(s - 1)
            pool.tensor_tensor(self.p[:, v, 0:k], self.p[:, v, 0:k],
                               self.ri[:, v, 0:k].unsqueeze(2).broadcast_to([P, k, SEQ]),
                               ALU.mult).then_inc(self.normed, 1)

        def unit_(unit, at, par, first, last):
            for s in range(n):
                if s + 1 < n:
                    mask_keys(unit, par, s + 1, False)
                elif not last:
                    mask_keys(unit + 1, 1 - par, 0, False)
                if s or not first:
                    norm(unit, s)

        mask_keys(base, 0, 0, True)
        self.run(pool, base, unit_)
        norm(base + self.UNITS, 0)

    def pe_piece(self, pe, ps, w_in, unit, par, idx):
        C = self.C
        kind, m = self.order[idx]
        bank = ps[:, 6 + idx % 2, :]
        for k in range(C):
            for i, (a, b) in enumerate(self.passes):
                flags = dict(start=(k == 0 and i == 0), stop=(k == C - 1 and i == len(self.passes) - 1))
                if kind == "v":
                    mm = pe.matmul(bank[0:SEQ, 0:C * P], self.x[:, par, a, k, m * SEQ:(m + 1) * SEQ],
                                   w_in[:, k, b, 2 * C * P:3 * C * P], **flags)
                else:
                    at = (m if kind == "q" else C + m) * P
                    mm = pe.matmul(bank[:, 0:UNIT], w_in[:, k, b, at:at + P], self.x[:, par, a, k, :], **flags)
        mm.then_inc(self.piece_done, 1)

    def pe_run(self, pe, base, ps, w_in, w_out, ident):
        C, n, NP = self.C, self.steps, self.pieces

        def behind(unit, par, s, first, pieces):
            g = unit * n + s
            if s >= self.TURN or not first:
                pe.wait_ge(self.normed, BASE + g - self.TURN + 1)
                before = s - self.TURN - 1
                pe.wait_ge(self.turn_kept, BASE + unit * n + (max(before, 0) if first else before))
                self.pe_turn(pe, ps, s - self.TURN, ident)
                v = s - self.TURN
                if 0 <= v < C:
                    pe.wait_ge(self.o_kept, BASE + unit * n + (max(v - 1, 0) if first else v - 1))
                    pe.transpose(ps[0:SEQ, 4 + v % 2, 0:P], self.p[:, v % 4, self.HALF, :],
                                 ident[:, :]).then_inc(self.class_turned, 1)
            if s >= self.WEIGH or not first:
                v = s - self.WEIGH
                own = v >= 0
                (b, c), vpar = self.place(v), par if own else 1 - par
                pe.wait_ge(self.turn_kept, BASE + g - self.WEIGH + 1)
                if 0 <= v < C:
                    pe.wait_ge(self.class_kept, BASE + unit * C + c + 1)
                pe.wait_ge(self.piece_kept, BASE + (unit if own else unit - 1) * NP + self.index["v", b] + 1)
                pe.wait_ge(self.o_kept, BASE + unit * n + (max(v - 1, 0) if first else v - 1))
                self.pe_weigh(pe, ps, v, vpar)
            if s == self.WEIGH and not first:
                pe.wait_ge(self.o_kept, BASE + unit * n)
                pe.wait_ge(self.piece_kept, BASE + pieces)
                for m in range(C):
                    for k in range(C):
                        mm = pe.matmul(ps[:, 6 + m, 0:UNIT], w_out[:, k, m * P:(m + 1) * P],
                                       self.o[:, 1 - par, k, :], start=(k == 0), stop=(k == C - 1))
                    mm.then_inc(self.out_done, 1)

        def unit_(unit, at, par, first, last):
            issued = 0
            for s in range(n):
                b, c = self.place(s)
                g = unit * n + s
                pe.wait_ge(self.piece_kept, BASE + unit * NP + self.index["q", c] + 1)
                pe.wait_ge(self.keys_masked, BASE + g + 1)
                pe.wait_ge(self.shifted, BASE + unit * n + (max(s - 1, 0) if first else s - 1))
                if s < C:
                    pe.wait_ge(self.class_masked, BASE + unit * C + c + 1)
                    for b_ in range(GROUP):
                        pe.matmul(ps[b_ * self.CLS:(b_ + 1) * self.CLS, s % 2, self.HALF * SEQ:(self.HALF + 1) * SEQ],
                                  self.qc[:, s % 2, b_, :], self.k[:, par, c, b_ * SEQ:(b_ + 1) * SEQ],
                                  start=True, stop=True)
                for a in range(2):
                    mm = pe.matmul(ps[64 * a:64 * a + 64, s % 2, 0:self.HALF * SEQ],
                                   self.q[:, par, c, b * SEQ + 1:(b + 1) * SEQ],
                                   self.km[:, s % 2, self.HALF * a:self.HALF * (a + 1), :], start=True, stop=True)
                mm.then_inc(self.scored, 1)
                behind(unit, par, s, first, (unit + 1) * NP + issued)
                for piece in [] if last else self.after[s]:
                    idx = self.index[piece]
                    issued = idx + 1
                    pe.wait_ge(self.x_copied, BASE + unit + 2)
                    pe.wait_ge(self.piece_kept, BASE + (unit + 1) * NP + idx - 1)
                    pe.wait_ge(self.out_kept, BASE + (unit if first or s >= self.WEIGH else unit - 1) * C)
                    self.pe_piece(pe, ps, w_in, unit + 1, 1 - par, idx)

        pe.wait_ge(self.x_copied, BASE + base + 1)
        pe.wait_ge(self.v_zeroed, BASE + 1)
        for idx in range(NP):
            pe.wait_ge(self.piece_kept, BASE + base * NP + max(idx - 1, 0))
            self.pe_piece(pe, ps, w_in, base, 0, idx)
        self.run(pe, base, unit_)
        for s in range(self.WEIGH + 1):
            if s == self.WEIGH:
                end = base + self.UNITS
                pe.wait_ge(self.o_kept, BASE + end * n)
                for m in range(C):
                    for k in range(C):
                        mm = pe.matmul(ps[:, 6 + m, 0:UNIT], w_out[:, k, m * P:(m + 1) * P],
                                       self.o[:, 1, k, :], start=(k == 0), stop=(k == C - 1))
                    mm.then_inc(self.out_done, 1)
            else:
                self.pe_tail(pe, ps, base + self.UNITS, s, ident)

    def pe_turn(self, pe, ps, v, ident):
        src = self.p[:, v % 4]
        for h in range(self.HALF):
            mm = pe.transpose(ps[0:SEQ, 2 + v % 2, h * P:(h + 1) * P], src[:, h, :], ident[:, :])
        mm.then_inc(self.turned, 1)

    def pe_weigh(self, pe, ps, v, vpar):
        b, c = self.place(v)
        for odd in range(2):
            for j in range(4):
                mm = pe.matmul(
                    ps[32 * j:32 * j + 32, 4 + v % 2, 0:SEQ],
                    self.v[:, vpar * GROUP + b, 4 * c + j, 2 * odd:2 * odd + 2, :].rearrange("p a d -> p (a d)"),
                    self.pt[:, b, c, 2 * j + odd, :], start=(odd == 0), stop=(odd == 1))
        mm.then_inc(self.weighed, 1)

    def pe_tail(self, pe, ps, end, s, ident):
        g = end * self.steps + s
        if s < self.TURN:
            pe.wait_ge(self.normed, BASE + g - self.TURN + 1)
            pe.wait_ge(self.turn_kept, BASE + g - self.TURN - 1)
            self.pe_turn(pe, ps, s - self.TURN, ident)
        pe.wait_ge(self.turn_kept, BASE + g - self.WEIGH + 1)
        pe.wait_ge(self.o_kept, BASE + g - self.WEIGH - 1)
        self.pe_weigh(pe, ps, s - self.WEIGH, 1)

    def dve_run(self, dve, base, ps, src, extra=None):
        n = self.steps

        def take(unit, at, par, before):
            dve.wait_ge(self.piece_done, BASE + before * self.pieces)
            now = src[:, :, ds(at * UNIT, UNIT)]
            if self.split:
                dve.tensor_scalar(self.x[:, par, 0], now, NORMED, None, ALU.mult).then_inc(self.x_high, 1)
                dve.wait_ge(self.x_high, BASE + unit + 1)
                dve.scalar_tensor_tensor(out=self.x[:, par, 1], in0=now, scalar=NORMED, in1=self.x[:, par, 0],
                                         op0=ALU.mult, op1=ALU.subtract).then_inc(self.x_copied, 1)
            else:
                dve.tensor_copy(self.x[:, par, 0], now).then_inc(self.x_copied, 1)

        def sums(unit, s):
            g, v, k = unit * n + s, (s - 1) % 4, self.slots(s - 1)
            dve.wait_ge(self.exped, BASE + g)
            dve.tensor_reduce(self.sm[:, v, 0:k], self.p[:, v, 0:k], AX.X, ALU.add).then_inc(self.summed, 1)
            dve.wait_ge(self.summed, BASE + g)
            dve.reciprocal(self.ri[:, v, 0:k], self.sm[:, v, 0:k]).then_inc(self.inverted, 1)

        def unit_(unit, at, par, first, last):
            for s in range(n):
                g = unit * n + s
                if s == 0 and not last:
                    take(unit + 1, at + 1, 1 - par, unit)
                dve.wait_ge(self.scored, BASE + g + 1)
                outputs = extra is not None and s == self.steps - 2 and not first
                k = self.slots(s)
                scores = ps[:, s % 2, 0:k * SEQ].rearrange("p (h k) -> p h k", k=SEQ)
                dve.tensor_reduce(self.mx[:, s % 2, 0:k], scores, AX.X, ALU.max).then_inc(self.maxed, 1)
                dve.wait_ge(self.maxed, BASE + g + 1)
                dve.wait_ge(self.turned, BASE + unit * n + (max(s - 3, 0) if first else s - 3))
                dve.tensor_tensor(self.p[:, s % 4, 0:k], scores,
                                  self.mx[:, s % 2, 0:k].unsqueeze(2).broadcast_to([P, k, SEQ]),
                                  ALU.subtract).then_inc(self.shifted, 1)
                if outputs:
                    dve.wait_ge(self.out_kept, BASE + unit * self.C)
                if s or not first:
                    sums(unit, s)
                if outputs:
                    extra(at)

        take(base, 0, 0, base)
        self.run(dve, base, unit_)
        sums(base + self.UNITS, 0)
        if extra is not None:
            dve.wait_ge(self.out_kept, BASE + (base + self.UNITS) * self.C)
            dve.wait_ge(self.summed, BASE + (base + self.UNITS) * n)
            extra(self.UNITS)

    def act_piece(self, act, ps, bias_q, factor, unit, par, idx):
        C = self.C
        kind, m = self.order[idx]
        act.wait_ge(self.piece_done, BASE + unit * self.pieces + idx + 1)
        bank = ps[:, 6 + idx % 2, :]
        if kind == "v":
            dst = self.v[:, par * GROUP + m, :, 0:4:3, :]
            now = bank[0:SEQ, 0:C * P].rearrange("p (j a d) -> p j a d", a=2, d=HEAD)
            op = act.activation(dst, now, ACT.Identity, scale=factor[0:SEQ, :]) if self.split else act.copy(dst, now)
        else:
            dst = (self.q if kind == "q" else self.k)[:, par, m, :]
            if bias_q is None:
                op = act.copy(dst, bank[:, 0:UNIT])
            else:
                col = m if kind == "q" else C + m
                op = act.activation(dst, bank[:, 0:UNIT], ACT.Identity, bias=bias_q[:, col:col + 1], scale=factor)
        op.then_inc(self.piece_kept, 1)

    def act_run(self, act, base, ps, bias_q, bias_o, store_o, factor=1.0):
        C, n = self.C, self.steps

        def keep_turned(unit, s):
            v = s - self.TURN
            b, c = self.place(v)
            act.wait_ge(self.turned, BASE + unit * n + v + 1)
            act.copy(self.pt[:, b, c, :, 1:SEQ].rearrange("p (a h) q -> p h a q", a=2),
                     ps[0:SEQ, 2 + v % 2, :].rearrange("p (h a q) -> p h a q", h=self.HALF, a=2)).then_inc(self.turn_kept, 1)

        def keep_class(unit, s):
            v = s - self.TURN
            act.wait_ge(self.class_turned, BASE + unit * C + v + 1)
            act.copy(self.pt[:, :, v, :, 0],
                     ps[0:SEQ, 4 + v % 2, 0:P].rearrange("p (b h) -> p b h", h=self.CLS)[:, :, 0:self.NH]).then_inc(self.class_kept, 1)

        def keep_weighed(unit, par, s):
            v = s - self.WEIGH
            b, c = self.place(v)
            act.wait_ge(self.weighed, BASE + unit * n + v + 1)
            act.copy(self.o[:, par if v >= 0 else 1 - par, c, b * SEQ:(b + 1) * SEQ],
                     ps[:, 4 + v % 2, 0:SEQ]).then_inc(self.o_kept, 1)

        def outputs(unit, at):
            for m in range(C):
                act.wait_ge(self.out_done, BASE + (unit - 1) * C + m + 1)
                store_o(at - 1, m, ps[:, 6 + m, 0:UNIT], bias_o[:, m:m + 1]).then_inc(self.out_kept, 1)

        def unit_(unit, at, par, first, last):
            for s in range(n):
                if s >= self.TURN or not first:
                    keep_turned(unit, s)
                act.wait_ge(self.shifted, BASE + unit * n + s + 1)
                k = self.slots(s)
                act.activation(self.p[:, s % 4, 0:k], self.p[:, s % 4, 0:k], ACT.Exp, scale=SCALE).then_inc(self.exped, 1)
                if s >= self.WEIGH or not first:
                    keep_weighed(unit, par, s)
                if 0 <= s - self.TURN < C:
                    keep_class(unit, s)
                if s == self.WEIGH and not first:
                    outputs(unit, at)
                for piece in [] if last else self.after[s]:
                    self.act_piece(act, ps, bias_q, factor, unit + 1, 1 - par, self.index[piece])

        for idx in range(self.pieces):
            self.act_piece(act, ps, bias_q, factor, base, 0, idx)
        self.run(act, base, unit_)
        end = base + self.UNITS
        for s in range(self.WEIGH):
            if s < self.TURN:
                keep_turned(end, s)
            keep_weighed(end, 0, s)
        outputs(end, self.UNITS)


def first_attention_stage(nc, ps, io, z, out, ident):
    with ExitStack() as ctx:
        sb = lambda name, shape: ctx.enter_context(nc.sbuf_tensor(name, shape, F32))
        sem, made = semaphores(nc, ctx)
        att = Attention(nc, ctx, sem, "a1_", 1)
        rows = sb("a1_rows", [P, 4, HID])
        cols = sb("a1_cols", [P, 4, P])
        bias = sb("a1_bias", [P, 1])
        loaded, turned, kept = sem("a1_loaded"), sem("a1_w_turned"), sem("a1_w_kept")
        block = open_block(nc, ctx, made)
        w_in, w_out = cols[:, 0:3, :].rearrange("p a b -> p (a b)").unsqueeze(1).unsqueeze(1), cols[:, 3:4, :]

        @block.sync
        def _(sp):
            sp.dma_start(rows[:, 0:3, :], io["w_qkv"].rearrange("(a p) d -> p a d", p=P)).then_inc(loaded, 16)
            sp.dma_start(rows[:, 3, :], io["w_agg"]).then_inc(loaded, 16)
            sp.dma_start(bias[:, :], io["b_agg"].rearrange("(p a) -> p a", a=1)).then_inc(loaded, 16)

        @block.gpsimd
        def _(pool):
            att.pool_setup(pool)
            att.pool_run(pool, 0)

        @block.tensor
        def _(pe):
            pe.wait_ge(loaded, BASE + 48)
            for a in range(4):
                m = pe.transpose(ps[:, 0, a * P:(a + 1) * P], rows[:, a, :], ident[:, :])
            m.then_inc(turned, 1)
            pe.wait_ge(kept, BASE + 1)
            att.pe_run(pe, 0, ps, w_in, w_out, ident)

        @block.vector
        def _(dve):
            dve.wait_ge(turned, BASE + 1)
            dve.tensor_copy(cols[:, :, :], ps[:, 0, :].rearrange("p (a m) -> p a m", a=4)).then_inc(kept, 1)
            att.dve_run(dve, 0, ps, z[:, :].unsqueeze(1))

        @block.scalar
        def _(act):
            def store(at, m, bank, b):
                return act.activation(out[:, ds(at * UNIT, UNIT)], bank, ACT.Identity, bias=b)
            act.wait_ge(att.v_zeroed, BASE + 1)
            act.wait_ge(loaded, BASE + 48)
            att.act_run(act, 0, ps, None, bias, store)


def front(nc, ps, io, h1_dram, z2_dram):
    with ExitStack() as ctx:
        sb = lambda name, shape: ctx.enter_context(nc.sbuf_tensor(name, shape, F32))
        ident = sb("ident", [P, P])
        h = sb("h", [P, TOKENS])
        tokens_stage(nc, ps, io, h, ident)
        z = sb("z", [P, TOKENS])
        attended = sb("attended", [P, TOKENS])
        norm_stage(nc, ps, "n1_", h, z, None, None)
        first_attention_stage(nc, ps, io, z, attended, ident)
        norm_stage(nc, ps, "n2_", h, z, attended, (h1_dram, z2_dram))


VECTORS = dict(b1=(0, KD), b2=(2, KD), g=(4, KD), beta=(6, KD), in_b=(8, 3 * KD), out_b=(14, KD))
NVEC = 16


def experts_stage(nc, ps, io, z2_dram, x_dram, peak_dram):
    with ExitStack() as ctx:
        sb = lambda name, shape: ctx.enter_context(nc.sbuf_tensor(name, shape, F32))
        sem, made = semaphores(nc, ctx)
        ident = sb("x_ident", [P, P])
        z = sb("x_z", [P, TOKENS])
        h = sb("x_h", [P, KD, TOKENS])
        xo = sb("x_out", [P, SEQ, KD, IMAGES])
        vec_rows = sb("x_vec_rows", [EXPERTS * NVEC, P])
        vec_all = sb("x_vec_all", [P, EXPERTS, NVEC])
        vec = sb("x_vec", [P, NVEC])
        raw_w1 = sb("raw_w1", [P, D])
        raw_w2 = sb("raw_w2", [P, KD, D])
        raw_in = sb("raw_in", [P, KD, 3 * D])
        raw_out = sb("raw_out", [P, KD, D])
        w1 = sb("w1", [P, D])
        w2 = sb("w2", [P, KD, D])
        w_in = ctx.enter_context(nc.sbuf_tensor("w_in", [P, KD, 2, 3 * D], F16))
        most = sb("x_most", [P, 1])
        row_most = sb("x_row_most", [1, 1])
        units = sb("x_units", [1, P])
        bound = sb("x_bound", [P, 1])
        power = sb("x_power", [P, 1])
        inv_power = sb("x_inv_power", [P, 1])
        w_scale = sb("x_w_scale", [P, 1])
        factor = sb("x_factor", [P, 1])
        w_out = sb("w_out", [P, KD, D])
        row_sum = sb("row_sum", [P, KD])
        row_mean = sb("row_mean", [P, KD])
        b2_mean = sb("b2_mean", [P, 1])
        b2c = sb("b2c", [P, KD])
        in_b = sb("in_b", [P, 3 * KD])
        out_b = sb("out_b", [P, KD])
        mean = sb("x_mean", [P, P])
        eps = sb("x_eps", [P, 1])
        h1 = sb("x_h1", [P, 2, KD, WIDE])
        hc = sb("x_hc", [P, RING, KD, WIDE])
        sq = sb("x_sq", [P, 2, KD, WIDE])
        sd = sb("x_sd", [P, 2, WIDE])
        rs = sb("x_rs", [P, 2, WIDE])
        att = Attention(nc, ctx, sem, "ax_", KD, split=True)
        peak = sb("x_peak", [P, EXPERTS * att.UNITS])
        peaked = sem("x_peaked")
        gained, measured, most_turned, most_shared, sizing, w_high, w_low = [
            sem("x_" + n) for n in ("gained", "measured", "most_turned", "most_shared", "sizing", "w_high", "w_low")]
        SIZING = 6
        consts, z_in, id_zero, id_done, ones = (sem("x_consts"), sem("x_z_in"), sem("x_id_zero"), sem("x_id_done"),
                                                sem("x_ones"))
        vec_turned, vec_kept = sem("x_vec_turned"), sem("x_vec_kept")
        raw_loaded, prepared = sem("raw_loaded"), sem("prepared")
        prep_step, prep_sums = sem("prep_step"), sem("prep_sums")
        h1_done, h1_kept, h2_done, h2_kept = sem("h1_done"), sem("h1_kept"), sem("h2_done"), sem("h2_kept")
        squared, varied, rooted, inverted, h_ready = (sem("x_squared"), sem("x_varied"), sem("x_rooted"),
                                                      sem("x_inverted"), sem("x_h_ready"))
        saved = sem("x_saved")
        block = open_block(nc, ctx, made)
        STEPS = WSTEPS
        PREP = 11

        @block.sync
        def _(sp):
            def load(e):
                sp.dma_start(raw_w1[:, :], io["enc_w1"][ds(e, 1)].rearrange("a k n -> (a k) n")).then_inc(raw_loaded, 16)
                for raw, name in ((raw_w2, "enc_w2"), (raw_in, "attn_in_w"), (raw_out, "attn_out_w")):
                    sp.dma_start(raw[:, :, :], io[name][ds(e, 1)].rearrange("a (k p) n -> p (a k) n", p=P)).then_inc(raw_loaded, 16)

            def save(e):
                sp.wait_ge(att.out_kept, BASE + (e + 1) * att.UNITS * KD)
                sp.dma_start(x_dram[ds(e, 1)].rearrange("a t f k b -> f (a t) (k b)"),
                             xo[:, :, :, :].rearrange("p t k b -> p t (k b)")).then_inc(saved, 16)

            load(0)
            sp.dma_start(z[:, :], z2_dram).then_inc(z_in, 16)
            with sp.Fori(0, EXPERTS - 1) as e:
                sp.wait_ge(w_low, BASE + e + 1)
                load(e + 1)
                save(e)
            save(EXPERTS - 1)
            sp.wait_ge(peaked, BASE + EXPERTS * att.UNITS)
            sp.dma_start(peak_dram, peak[:, :]).then_inc(saved, 16)
            sp.wait_ge(saved, BASE + 16 * (EXPERTS + 1))

        @block.gpsimd
        def _(pool):
            make_identity(pool, ident, id_zero, id_done)
            pool.memset(mean[:, :], 1.0 / D).then_inc(ones, 1)
            pool.memset(eps[:, :], EPS).then_inc(ones, 1)
            pool.memset(units[:, :], 1.0).then_inc(ones, 1)
            pool.wait_ge(id_done, BASE + 1)
            pool.wait_ge(ones, BASE + 3)
            att.pool_setup(pool)
            with pool.Fori(0, EXPERTS) as e:
                def body(k, slot, live):
                    par = slot % 2
                    if live(2):
                        pool.wait_ge(inverted, BASE + e * STEPS + k - 1)
                        pool.tensor_tensor(h[:, :, ds((k - 2) * WIDE, WIDE)], hc[:, (slot - 2) % RING],
                                           rs[:, par, :].unsqueeze(1).broadcast_to([P, KD, WIDE]),
                                           ALU.mult).then_inc(h_ready, 1)
                wide_steps(pool, body)
                att.pool_run(pool, e * att.UNITS)

        @block.tensor
        def _(pe):
            pe.wait_ge(ones, BASE + 3)
            pe.wait_ge(id_done, BASE + 1)
            pe.wait_ge(consts, BASE + 16 * len(VECTORS))
            pe.transpose(ps[:, 0, 0:EXPERTS * NVEC], vec_rows[:, :],
                         ident[0:EXPERTS * NVEC, 0:EXPERTS * NVEC]).then_inc(vec_turned, 1)
            pe.wait_ge(z_in, BASE + 16)
            with pe.Fori(0, EXPERTS) as e:
                pe.wait_ge(raw_loaded, BASE + (e + 1) * 64)
                pe.wait_ge(prep_step, BASE + e * PREP + 1)
                at = VECTORS["b2"][0]
                pe.matmul(ps[:, 5, 0:KD], mean[:, :], vec[:, at:at + KD], start=True, stop=True).then_inc(prep_sums, 1)
                at = VECTORS["beta"][0]
                for m in range(3 * KD):
                    for k in range(KD):
                        mm = pe.matmul(ps[:, 6, m:m + 1], raw_in[:, k, m * P:(m + 1) * P], vec[:, at + k:at + k + 1],
                                       start=(k == 0), stop=(k == KD - 1))
                mm.then_inc(prep_sums, 1)
                pe.wait_ge(prep_step, BASE + e * PREP + 3)
                for m in range(KD):
                    for k in range(KD):
                        mm = pe.matmul(ps[:, 7, m:m + 1], raw_out[:, k, m * P:(m + 1) * P],
                                       in_b[:, 2 * KD + k:2 * KD + k + 1], start=(k == 0), stop=(k == KD - 1))
                mm.then_inc(prep_sums, 1)
                pe.wait_ge(measured, BASE + e + 1)
                pe.transpose(ps[0:1, 0, 0:P], most[:, :], ident[:, :]).then_inc(most_turned, 1)
                pe.wait_ge(sizing, BASE + e * SIZING + 1)
                pe.matmul(ps[:, 1, 0:1], units[:, :], row_most[:, :], start=True, stop=True).then_inc(most_shared, 1)
                pe.wait_ge(prepared, BASE + e + 1)

                def body(k, slot, live):
                    par = slot % 2
                    at = e * STEPS + k
                    if live(0):
                        pe.wait_ge(h1_kept, BASE + at * KD)
                        for m in range(KD):
                            pe.matmul(ps[:, m, 0:WIDE], w1[:, m * P:(m + 1) * P], z[:, ds(k * WIDE, WIDE)],
                                      start=True, stop=True).then_inc(h1_done, 1)
                    if live(1):
                        pe.wait_ge(h1_kept, BASE + at * KD)
                        pe.wait_ge(h2_kept, BASE + (at - 1) * KD)
                        for m in range(KD):
                            for kk in range(KD):
                                mm = pe.matmul(ps[:, 2 + m, 0:WIDE], w2[:, kk, m * P:(m + 1) * P], h1[:, 1 - par, kk, :],
                                               start=(kk == 0), stop=(kk == KD - 1))
                            mm.then_inc(h2_done, 1)
                    if live(2):
                        pe.wait_ge(squared, BASE + at - 1)
                        pe.wait_ge(rooted, BASE + at - 2)
                        for kk in range(KD):
                            mm = pe.matmul(ps[:, 4, 0:WIDE], mean[:, :], sq[:, par, kk, :],
                                           start=(kk == 0), stop=(kk == KD - 1))
                        mm.then_inc(varied, 1)
                wide_steps(pe, body)
                pe.wait_ge(w_low, BASE + e + 1)
                att.pe_run(pe, e * att.UNITS, ps, w_in, w_out, ident)

        @block.vector
        def _(dve):
            dve.wait_ge(vec_turned, BASE + 1)
            for at, k in VECTORS.values():
                dve.tensor_copy(vec_all[:, :, at:at + k],
                                ps[:, 0, EXPERTS * at:EXPERTS * (at + k)].rearrange("p (e k) -> p e k", k=k)).then_inc(vec_kept, 1)
            dve.wait_ge(vec_kept, BASE + len(VECTORS))
            with dve.Fori(0, EXPERTS) as e:
                V = {name: vec[:, at:at + k] for name, (at, k) in VECTORS.items()}
                b = e * PREP
                dve.wait_ge(att.out_kept, BASE + e * att.UNITS * KD)
                dve.wait_ge(raw_loaded, BASE + (e + 1) * 64)
                dve.tensor_copy(vec[:, :], vec_all[:, ds(e, 1), :].rearrange("p a v -> p (a v)")).then_inc(prep_step, 1)
                dve.tensor_reduce(row_sum[:, :], raw_w2[:, :, :], AX.X, ALU.add).then_inc(prep_step, 1)
                dve.wait_ge(prep_sums, BASE + e * 3 + 2)
                dve.wait_ge(prep_step, BASE + b + 2)
                dve.tensor_tensor(in_b[:, :], ps[:, 6, 0:3 * KD], V["in_b"], ALU.add).then_inc(prep_step, 1)
                for k in range(KD):
                    dve.tensor_scalar(raw_in[:, k, :], raw_in[:, k, :], V["g"][:, k:k + 1], None,
                                      ALU.mult).then_inc(gained, 1)
                dve.wait_ge(gained, BASE + (e + 1) * KD)
                dve.tensor_reduce(most[:, :], raw_in[:, :, :], AX.XY, ALU.max, apply_absolute_value=True).then_inc(measured, 1)
                dve.tensor_reduce(b2_mean[:, :], ps[:, 5, 0:KD], AX.X, ALU.add).then_inc(prep_step, 1)
                dve.tensor_scalar(row_mean[:, :], row_sum[:, :], 1.0 / D, None, ALU.mult).then_inc(prep_step, 1)
                dve.wait_ge(prep_step, BASE + b + 5)
                dve.tensor_scalar(b2c[:, :], V["b2"], b2_mean[:, 0:1], None, ALU.subtract).then_inc(prep_step, 1)
                for k in range(KD):
                    dve.tensor_scalar(w2[:, k, :], raw_w2[:, k, :], row_mean[:, k:k + 1], None,
                                      ALU.subtract).then_inc(prep_step, 1)
                dve.tensor_copy(w1[:, :], raw_w1[:, :]).then_inc(prep_step, 1)
                dve.tensor_copy(w_out[:, :, :], raw_out[:, :, :]).then_inc(prep_step, 1)
                dve.wait_ge(prep_sums, BASE + e * 3 + 3)
                dve.tensor_tensor(out_b[:, :], ps[:, 7, 0:KD], V["out_b"], ALU.add).then_inc(prep_step, 1)
                dve.wait_ge(most_turned, BASE + e + 1)
                dve.tensor_reduce(row_most[:, :], ps[0:1, 0, 0:P], AX.X, ALU.max).then_inc(sizing, 1)
                dve.wait_ge(most_shared, BASE + e + 1)
                at = e * SIZING
                dve.tensor_scalar(bound[:, :], ps[:, 1, 0:1], TINY, None, ALU.max).then_inc(sizing, 1)
                dve.wait_ge(sizing, BASE + at + 2)
                dve.tensor_scalar(power[:, :].bitcast(I32), bound[:, :].bitcast(I32), EXPONENT, None,
                                  ALU.bitwise_and).then_inc(sizing, 1)
                dve.wait_ge(sizing, BASE + at + 3)
                dve.reciprocal(inv_power[:, :], power[:, :]).then_inc(sizing, 1)
                dve.tensor_scalar(factor[:, :], power[:, :], 1.0 / TOP / NORMED, None, ALU.mult).then_inc(sizing, 1)
                dve.wait_ge(sizing, BASE + at + 4)
                dve.tensor_scalar(w_scale[:, :], inv_power[:, :], TOP, None, ALU.mult).then_inc(sizing, 1)
                dve.wait_ge(prep_step, BASE + b + PREP)
                dve.sem_inc(prepared, 1)

                def body(k, slot, live):
                    par = slot % 2
                    at = e * STEPS + k
                    if live(1):
                        if live(RING + 1):
                            dve.wait_ge(h_ready, BASE + at - RING)
                        for m in range(KD):
                            dve.wait_ge(h2_done, BASE + (at - 1) * KD + m + 1)
                            dve.tensor_scalar(hc[:, (slot - 1) % RING, m, :], ps[:, 2 + m, 0:WIDE], b2c[:, m:m + 1], None,
                                              ALU.add).then_inc(h2_kept, 1)
                    if live(2):
                        dve.wait_ge(rooted, BASE + at - 1)
                        if live(4):
                            dve.wait_ge(h_ready, BASE + at - 3)
                        dve.reciprocal(rs[:, par, :], sd[:, par, :]).then_inc(inverted, 1)
                wide_steps(dve, body)
                dve.wait_ge(w_high, BASE + e + 1)
                for k in range(KD):
                    op = dve.scalar_tensor_tensor(out=w_in[:, k, 1, :], in0=raw_in[:, k, :], scalar=w_scale[:, 0:1],
                                                  in1=w_in[:, k, 0, :], op0=ALU.mult, op1=ALU.subtract)
                op.then_inc(w_low, 1)
                dve.wait_ge(h_ready, BASE + (e + 1) * STEPS)

                def largest(at):
                    dve.tensor_reduce(peak[:, ds(e * att.UNITS + at - 1, 1)],
                                      xo[:, :, :, ds((at - 1) * GROUP, GROUP)].rearrange("p t k b -> p (t k) b"),
                                      AX.XY, ALU.max, apply_absolute_value=True).then_inc(peaked, 1)
                att.dve_run(dve, e * att.UNITS, ps, h, largest)

        @block.scalar
        def _(act):
            for name, key in (("b1", "enc_b1"), ("b2", "enc_b2"), ("g", "enc_g"), ("beta", "enc_beta"),
                              ("in_b", "attn_in_b"), ("out_b", "attn_out_b")):
                at, k = VECTORS[name]
                act.dma_start(vec_rows[EXPERTS * at:EXPERTS * (at + k), :],
                              io[key].rearrange("e (k p) -> (e k) p", p=P)).then_inc(consts, 16)
            with act.Fori(0, EXPERTS) as e:
                act.wait_ge(prepared, BASE + e + 1)
                at = VECTORS["b1"][0]

                def body(k, slot, live):
                    par = slot % 2
                    at_ = e * STEPS + k
                    if live(0):
                        for m in range(KD):
                            act.wait_ge(h1_done, BASE + at_ * KD + m + 1)
                            if live(2):
                                act.wait_ge(h2_done, BASE + (at_ - 1) * KD)
                            act.activation(h1[:, par, m, :], ps[:, m, 0:WIDE], ACT.Relu,
                                           bias=vec[:, at + m:at + m + 1]).then_inc(h1_kept, 1)
                    if live(1):
                        act.wait_ge(h2_kept, BASE + at_ * KD)
                        if live(3):
                            act.wait_ge(varied, BASE + at_ - 2)
                        act.activation(sq[:, 1 - par], hc[:, (slot - 1) % RING], ACT.Square).then_inc(squared, 1)
                    if live(2):
                        act.wait_ge(varied, BASE + at_ - 1)
                        if live(4):
                            act.wait_ge(inverted, BASE + at_ - 3)
                        act.activation(sd[:, par, :], ps[:, 4, 0:WIDE], ACT.Sqrt, bias=eps[:, 0:1]).then_inc(rooted, 1)
                wide_steps(act, body)
                act.wait_ge(sizing, BASE + (e + 1) * SIZING)
                act.activation(w_in[:, :, 0, :], raw_in[:, :, :], ACT.Identity, scale=w_scale[:, 0:1]).then_inc(w_high, 1)
                act.wait_ge(saved, BASE + e * 16)
                def store(at, m, bank, b):
                    dst = xo[:, :, m, ds(at * GROUP, GROUP)].rearrange("p t b -> p b t")
                    return act.activation(dst, bank.rearrange("p (b t) -> p b t", t=SEQ), ACT.Identity, bias=b)
                act.wait_ge(att.v_zeroed, BASE + 1)
                att.act_run(act, e * att.UNITS, ps, in_b, out_b, store, factor[:, 0:1])


def lstm_stage(nc, ps, io, x_dram, peak_dram, mem_dram):
    HALF = IMAGES
    G4 = 4 * D
    COLUMNS = ((0, 0, 2 * D), (2 * D, 3 * D, D), (3 * D, 2 * D, D))
    TRIPS = (SEQ - 1) // 2
    GROUPS = EXPERTS * 2
    MATRICES = GROUPS * 2
    STAGES = 4
    UNITS = IMAGES // GROUP
    with ExitStack() as ctx:
        sb = lambda name, shape, dt=F32: ctx.enter_context(nc.sbuf_tensor(name, shape, dt))
        sem, made = semaphores(nc, ctx)
        ident = sb("l_ident", [P, P])
        ones = sb("l_ones", [3, P])
        peak = sb("l_peak", [P, EXPERTS, UNITS])
        w = sb("l_w", [P, EXPERTS, 2, 2 * KD, 2, G4], F16)
        bias = sb("l_bias", [P, EXPERTS, G4])
        x = sb("l_x", [P, 2, EXPERTS, KD, IMAGES])
        xs = sb("l_xs", [P, 2, 2, 2, EXPERTS, KD, IMAGES], F16)
        hs = sb("l_hs", [P, EXPERTS, 2, 2, KD, IMAGES], F16)
        cell = sb("l_cell", [P, EXPERTS, D])
        gates = sb("l_gates", [P, 2, G4])
        ig = sb("l_ig", [P, D])
        tc = sb("l_tc", [P, D])
        hid = sb("l_hid", [P, 2, D])
        stage = [sb(f"l_stage{i}", [P, KD, G4]) for i in range(STAGES - 1)] + [gates]
        most = sb("l_most", [P, GROUPS, 3])
        row_most = sb("l_row_most", [3, 1])
        diag = sb("l_diag", [3, 3])
        bound = sb("l_bound", [P, 3])
        power = sb("l_power", [P, 3])
        inv_power = sb("l_inv_power", [P, 3])
        s1 = sb("l_s1", [P, 1])
        total = sb("l_total", [P, 1])
        scale = sb("l_scale", [P, GROUPS, 2])
        x_scale = sb("l_x_scale", [P, EXPERTS])
        unscale = sb("l_unscale", [P, EXPERTS])
        bias_in, peak_in, id_zero, id_done, ones_done = [
            sem("l_" + n) for n in ("bias_in", "peak_in", "id_zero", "id_done", "ones_done")]
        stage_in = [sem(f"l_stage_in{i}") for i in range(STAGES)]
        x_in, x_high, x_low = sem("l_x_in"), sem("l_x_high"), sem("l_x_low")
        measured, most_turned, most_shared, sizing, scaled, w_high, w_low = [
            sem("l_" + n) for n in ("measured", "most_turned", "most_shared", "sizing", "scaled", "w_high", "w_low")]
        summed, biased, gated, ig_done, fc_done, cell_done, squashed, h_done, turned, h_high, h_low = [
            sem("l_" + n) for n in ("summed", "biased", "gated", "ig_done", "fc_done", "cell_done", "squashed",
                                    "h_done", "turned", "h_high", "h_low")]
        saved = [sem(f"l_saved{e}") for e in range(EXPERTS)]
        block = open_block(nc, ctx, made)
        SIZING = 11

        def now_h(e):
            return ps[:, 6 + e % 2, 0:2 * P].rearrange("p (k d b) -> p d k b", k=KD, d=2)

        def load_x(sp, t, split):
            sp.wait_ge(x_low, BASE + split)
            for d in range(2):
                pos = t if d == 0 else SEQ - 1 - t
                src = x_dram[:, ds(pos, 1)].rearrange("e a f k b -> f (e a) (k b)")
                sp.dma_start(x[:, d].rearrange("p e k b -> p e (k b)"), src).then_inc(x_in, 16)

        def save_h(sp, t, e):
            sp.wait_ge(h_low, BASE + t * EXPERTS + e + 1)
            for d in range(2):
                pos = t if d == 0 else SEQ - 1 - t
                sp.dma_start(mem_dram[e, d][ds(pos, 1)].rearrange("a f q k b -> f (a q) (k b)"),
                             hs[:, e, :, d].rearrange("p q k b -> p q (k b)")).then_inc(saved[e], 16)

        @block.sync
        def _(sp):
            sp.dma_start(peak[:, :, :].rearrange("p e u -> p (e u)"), peak_dram).then_inc(peak_in, 16)
            for q in range(MATRICES):
                e, d, j = q // 4, q // 2 % 2, q % 2
                if q >= STAGES:
                    sp.wait_ge(w_low, BASE + q - STAGES + 1)
                src = io["lstm_w" + "ih"[j] + "_" + "fb"[d]][e].rearrange("(k p) n -> p k n", p=P)
                for to, frm, width in COLUMNS:
                    sp.dma_start(stage[q % STAGES][:, :, to:to + width], src[:, :, frm:frm + width]).then_inc(stage_in[q % STAGES], 16)
                if q == 1:
                    load_x(sp, 0, 0)
                if q == STAGES - 1:
                    for e in range(EXPERTS):
                        for d, name in enumerate(("lstm_b_f", "lstm_b_b")):
                            for to, frm, width in COLUMNS:
                                sp.dma_start(bias[d * HALF:(d + 1) * HALF, e, to:to + width],
                                             io[name][e, frm:frm + width].partition_broadcast(HALF)).then_inc(bias_in, 16)
            load_x(sp, 1, EXPERTS)
            for e in range(EXPERTS):
                save_h(sp, 0, e)

            def trip(i, last):
                for r in range(2):
                    t = i * 2 + 1 + r
                    for e in range(EXPERTS):
                        if e == 0 and not (last and r == 1):
                            load_x(sp, t + 1, (t + 1) * EXPERTS)
                        save_h(sp, t, e)

            with sp.Fori(0, TRIPS - 1) as i:
                trip(i, False)
            trip(TRIPS - 1, True)
            for e in range(EXPERTS):
                sp.wait_ge(saved[e], BASE + SEQ * 32)

        @block.gpsimd
        def _(pool):
            make_identity(pool, ident, id_zero, id_done)
            pool.wait_ge(id_done, BASE + 1)
            pool.memset(ones[:, :], 1.0).then_inc(ones_done, 1)
            for q in range(MATRICES):
                e, d, j = q // 4, q // 2 % 2, q % 2
                part = w[:, e, d, KD * j:KD * (j + 1)]
                pool.wait_ge(w_high, BASE + q + 1)
                pool.tensor_tensor(part[:, :, 1, :], stage[q % STAGES][:, :, :], part[:, :, 0, :],
                                   ALU.subtract).then_inc(w_low, 1)

        @block.tensor
        def _(pe):
            def products(t, e, first):
                v = t * EXPERTS + e
                z = v % 2 if first else e % 2
                if not first or e >= 2:
                    pe.wait_ge(biased, BASE + v - 1)
                pe.wait_ge(x_low, BASE + v + 1)
                last = (KD if first else 2 * KD) - 1
                for kk in range(last + 1):
                    if kk == KD:
                        pe.wait_ge(h_low, BASE + v - EXPERTS + 1)
                    for turn_, (a, b) in enumerate(PASSES):
                        for n in range(2):
                            for d in range(2):
                                lhsT = xs[:, PAR(t, first), a, d, e, kk, :] if kk < KD else hs[:, e, a, d, kk - KD, :]
                                mm = pe.matmul(ps[d * HALF:(d + 1) * HALF, 2 * z + n, :], lhsT,
                                               w[:, e, d, kk, b, n * 512:(n + 1) * 512],
                                               start=(kk == 0 and turn_ == 0), stop=(kk == last and turn_ == 2))
                mm.then_inc(summed, 1)

            def turn(v, par):
                pe.wait_ge(h_done, BASE + v + 1)
                for k in range(KD):
                    mm = pe.transpose(ps[:, 6 + par, k * P:(k + 1) * P], hid[:, par, k * P:(k + 1) * P], ident[:, :])
                mm.then_inc(turned, 1)

            PAR = lambda t, first: 0 if first else parity[0]
            parity = [0]
            pe.wait_ge(id_done, BASE + 1)
            pe.wait_ge(ones_done, BASE + 1)
            for g in range(GROUPS):
                pe.wait_ge(measured, BASE + 3 * (g + 1))
                pe.transpose(ps[0:3, 4, 0:P], most[:, g, :], ident[:, :]).then_inc(most_turned, 1)
                pe.wait_ge(sizing, BASE + SIZING * g + 2)
                pe.matmul(ps[:, 5, 0:3], ones[:, :], diag[:, :], start=True, stop=True).then_inc(most_shared, 1)
            for e in range(EXPERTS):
                pe.wait_ge(w_low, BASE + 4 * (e + 1))
                products(0, e, True)
                if e:
                    if e >= 3:
                        pe.wait_ge(h_low, BASE + e - 2)
                    turn(e - 1, (e - 1) % 2)
            with pe.Fori(0, TRIPS) as i:
                for r in range(2):
                    t, parity[0] = i * 2 + 1 + r, 1 - r
                    for e in range(EXPERTS):
                        v = t * EXPERTS + e
                        products(t, e, False)
                        pe.wait_ge(h_low, BASE + v - 2)
                        turn(v - 1, (e - 1) % 2)
            turn(SEQ * EXPERTS - 1, 1)

        def splits(e):
            return {0: (), 1: (0,), 2: (1,), 3: (2, 3)}[e]

        @block.vector
        def _(dve):
            def low_x(t, par, e):
                dve.wait_ge(x_high, BASE + t * EXPERTS + e + 1)
                dve.scalar_tensor_tensor(out=xs[:, par, 1, :, e], in0=x[:, :, e], scalar=x_scale[:, e:e + 1],
                                         in1=xs[:, par, 0, :, e], op0=ALU.mult, op1=ALU.subtract).then_inc(x_low, 1)

            def low_h(v, e):
                dve.wait_ge(h_high, BASE + v + 1)
                for k in range(KD):
                    op = dve.scalar_tensor_tensor(out=hs[:, e, 1, :, k, :], in0=now_h(e)[:, :, k, :], scalar=TOP,
                                                  in1=hs[:, e, 0, :, k, :], op0=ALU.mult, op1=ALU.subtract)
                op.then_inc(h_low, 1)

            dve.wait_ge(peak_in, BASE + 16)
            dve.wait_ge(id_done, BASE + 1)
            for g in range(GROUPS):
                e, d = g // 2, g % 2
                rows = slice(d * HALF, (d + 1) * HALF)
                dve.tensor_reduce(most[:, g, 0:1], peak[:, e, :], AX.X, ALU.max).then_inc(measured, 1)
                for j in range(2):
                    q = 2 * g + j
                    dve.wait_ge(stage_in[q % STAGES], BASE + (q // STAGES + 1) * 16 * len(COLUMNS))
                    dve.tensor_reduce(most[:, g, 1 + j:2 + j], stage[q % STAGES][:, :, :], AX.XY, ALU.max,
                                      apply_absolute_value=True).then_inc(measured, 1)
                step = [SIZING * g]

                def then(op, after=True):
                    op.then_inc(sizing, 1)
                    step[0] += 1
                    if after:
                        dve.wait_ge(sizing, BASE + step[0])

                dve.wait_ge(most_turned, BASE + g + 1)
                then(dve.tensor_reduce(row_most[:, :], ps[0:3, 4, 0:P], AX.X, ALU.max))
                then(dve.tensor_scalar(diag[:, :], ident[0:3, 0:3], row_most[:, 0:1], None, ALU.mult), after=False)
                dve.wait_ge(most_shared, BASE + g + 1)
                then(dve.tensor_scalar(bound[:, :], ps[:, 5, 0:3], TINY, None, ALU.max))
                then(dve.tensor_scalar(power[:, :].bitcast(I32), bound[:, :].bitcast(I32), EXPONENT, None, ALU.bitwise_and))
                then(dve.reciprocal(inv_power[:, :], power[:, :]))
                then(dve.tensor_scalar(s1[:, :], inv_power[:, 0:1], inv_power[:, 1:2], TOP * TOP, ALU.mult, ALU.mult))
                then(dve.tensor_scalar(x_scale[:, e:e + 1], inv_power[:, 0:1], TOP, None, ALU.mult), after=False)
                then(dve.scalar_tensor_tensor(out=total[:, :], in0=inv_power[:, 2:3], scalar=TOP * TOP, in1=s1[:, :],
                                              op0=ALU.mult, op1=ALU.min))
                then(dve.tensor_scalar(scale[:, g, 0:1], total[:, :], power[:, 0:1], 1.0 / TOP, ALU.mult, ALU.mult), after=False)
                then(dve.tensor_scalar(scale[:, g, 1:2], total[:, :], 1.0 / TOP, None, ALU.mult), after=False)
                then(dve.reciprocal(unscale[rows, e:e + 1], total[rows, :]))
                assert step[0] == SIZING * (g + 1)
            for e in range(EXPERTS):
                low_x(0, 0, e)
            dve.wait_ge(bias_in, BASE + 16 * 2 * EXPERTS * len(COLUMNS))
            dve.wait_ge(w_low, BASE + MATRICES)

            def update(t, e, first, par, last):
                v, z = t * EXPERTS + e, e % 2
                gz = gates[:, z, :]
                dve.wait_ge(summed, BASE + v + 1)
                if not first or e >= 2:
                    dve.wait_ge(h_done, BASE + v - 1)
                dve.scalar_tensor_tensor(
                    out=gz.rearrange("p (n c) -> p n c", n=2), in0=ps[:, 2 * z:2 * z + 2, :], scalar=unscale[:, e:e + 1],
                    in1=bias[:, e, :].rearrange("p (n c) -> p n c", n=2), op0=ALU.mult, op1=ALU.add).then_inc(biased, 1)
                if not first or e:
                    low_h(v - 1, (e - 1) % EXPERTS)
                dve.wait_ge(gated, BASE + (v + 1) * 2)
                if first:
                    dve.tensor_tensor(cell[:, e, :], gz[:, 0:D], gz[:, 3 * D:4 * D], ALU.mult).then_inc(cell_done, 1)
                else:
                    dve.tensor_tensor(ig[:, :], gz[:, 0:D], gz[:, 3 * D:4 * D], ALU.mult).then_inc(ig_done, 1)
                    dve.tensor_tensor(cell[:, e, :], gz[:, D:2 * D], cell[:, e, :], ALU.mult).then_inc(fc_done, 1)
                    dve.wait_ge(ig_done, BASE + v - EXPERTS + 1)
                    dve.wait_ge(fc_done, BASE + v - EXPERTS + 1)
                    dve.tensor_tensor(cell[:, e, :], cell[:, e, :], ig[:, :], ALU.add).then_inc(cell_done, 1)
                dve.wait_ge(squashed, BASE + v + 1)
                if not first or e >= 2:
                    dve.wait_ge(turned, BASE + v - 1)
                dve.tensor_tensor(hid[:, z, :], gz[:, 2 * D:3 * D], tc[:, :], ALU.mult).then_inc(h_done, 1)
                if not last:
                    for e_ in splits(e):
                        low_x(t + 1, par, e_)

            def trip(i, last):
                for r in range(2):
                    for e in range(EXPERTS):
                        update(i * 2 + 1 + r, e, False, r, last and r == 1)

            for e in range(EXPERTS):
                update(0, e, True, 1, False)
            with dve.Fori(0, TRIPS - 1) as i:
                trip(i, False)
            trip(TRIPS - 1, True)
            low_h(SEQ * EXPERTS - 1, EXPERTS - 1)

        @block.scalar
        def _(act):
            def high_x(t, par, e):
                act.wait_ge(x_in, BASE + (t + 1) * 32)
                act.activation(xs[:, par, 0, :, e], x[:, :, e], ACT.Identity, scale=x_scale[:, e:e + 1]).then_inc(x_high, 1)

            def keep_h(v, e, t):
                act.wait_ge(turned, BASE + v + 1)
                if t is not None:
                    act.wait_ge(saved[e], BASE + t * 32)
                act.activation(hs[:, e, 0], now_h(e), ACT.Identity, scale=TOP).then_inc(h_high, 1)

            def squash(t, e, par, last):
                v, z = t * EXPERTS + e, e % 2
                act.wait_ge(biased, BASE + v + 1)
                act.activation(gates[:, z, 0:3 * D], gates[:, z, 0:3 * D], ACT.Sigmoid).then_inc(gated, 1)
                act.activation(gates[:, z, 3 * D:4 * D], gates[:, z, 3 * D:4 * D], ACT.Tanh).then_inc(gated, 1)
                act.wait_ge(cell_done, BASE + v + 1)
                act.wait_ge(h_done, BASE + v)
                act.activation(tc[:, :], cell[:, e, :], ACT.Tanh).then_inc(squashed, 1)
                if not last:
                    for e_ in splits(e):
                        high_x(t + 1, par, e_)

            for q in range(MATRICES):
                e, d, j = q // 4, q // 2 % 2, q % 2
                act.wait_ge(sizing, BASE + SIZING * (q // 2 + 1))
                act.activation(stage[q % STAGES][:, :, :], stage[q % STAGES][:, :, :], ACT.Identity,
                               scale=scale[:, q // 2, j:j + 1]).then_inc(scaled, 1)
                act.wait_ge(scaled, BASE + q + 1)
                act.copy(w[:, e, d, KD * j:KD * (j + 1), 0, :], stage[q % STAGES][:, :, :]).then_inc(w_high, 1)
            for e in range(EXPERTS):
                high_x(0, 0, e)

            def trip(i, last):
                for r in range(2):
                    t = i * 2 + 1 + r
                    for e in range(EXPERTS):
                        keep_h(t * EXPERTS + e - 1, (e - 1) % EXPERTS, t if e else t - 1)
                        squash(t, e, r, last and r == 1)

            for e in range(EXPERTS):
                if e:
                    keep_h(e - 1, e - 1, None)
                squash(0, e, 1, False)
            with act.Fori(0, TRIPS - 1) as i:
                trip(i, False)
            trip(TRIPS - 1, True)
            keep_h(SEQ * EXPERTS - 1, EXPERTS - 1, SEQ - 1)


HEAD_VECTORS = dict(sig_b1=(0, KD), sig_b2=(2, KD), tan_b1=(4, KD), tan_b2=(6, KD), dec_b1=(8, KD), dec_b2=(10, 1),
                    dec_g=(11, 1), dec_beta=(12, 1))
NHEAD = 13


def head_stage(nc, ps, io, h1_dram, z2_dram, mem_dram, out):
    TC = 5
    W = TC * IMAGES
    CHUNKS = SEQ // TC
    with ExitStack() as ctx:
        sb = lambda name, shape, dt=F32: ctx.enter_context(nc.sbuf_tensor(name, shape, dt))
        sem, made = semaphores(nc, ctx)
        ident = sb("h_ident", [P, P])
        h1 = sb("h_h1", [P, TOKENS])
        z2 = sb("h_z2", [P, TOKENS])
        PLACE, at = {}, 0
        for name, k, width in (("s1", 2 * KD, D), ("t1", 2 * KD, D), ("d1", KD, D), ("s2", KD, D), ("t2", KD, D), ("d2", KD, P)):
            PLACE[name] = (at, k, width)
            at += k * width
        raw = sb("h_raw", [P, 2, at])
        w = sb("h_w", [P, EXPERTS, 2, at], F16)
        OURS = PLACE["s2"][0]
        NW = len(PLACE)
        most = sb("h_most", [P, EXPERTS, NW + 3])
        row_most = sb("h_row_most", [NW + 3, 1])
        diag = sb("h_diag", [NW + 3, NW + 3])
        units = sb("h_units", [NW + 3, P])
        bound = sb("h_bound", [P, NW + 3])
        power = sb("h_power", [P, NW + 3])
        inv_power = sb("h_inv_power", [P, NW + 3])
        w_scale = sb("h_w_scale", [P, EXPERTS, NW])
        r_scale = sb("h_r_scale", [P, 3])
        factor = sb("h_factor", [P, EXPERTS, NW])
        bias1 = sb("h_bias1", [P, EXPERTS, 3, KD])
        d2_sum = sb("h_d2_sum", [P, KD])
        d2_mean = sb("h_d2_mean", [P, KD])
        vec_rows = sb("h_vec_rows", [EXPERTS * NHEAD, P])
        vec = sb("h_vec", [P, EXPERTS, NHEAD])
        b2c = sb("h_b2c", [P, EXPERTS])
        rw = sb("h_rw", [P, EXPERTS])
        rwb = sb("h_rwb", [P, EXPERTS, P])
        rb = sb("h_rb", [P, EXPERTS])
        mean = sb("h_mean", [P, P])
        eps = sb("h_eps", [P, 1])
        mem = sb("h_mem", [P, 2, 2, TC, 2, KD, IMAGES], F16)
        rs1 = sb("h_rs1", [P, KD, W])
        rt1 = sb("h_rt1", [P, KD, W])
        rs1s, rt1s, ggs, rd1s = [sb(n, [P, 2, KD, W], F16) for n in ("h_rs1s", "h_rt1s", "h_ggs", "h_rd1s")]
        gs = sb("h_gs", [P, KD, W])
        gt = sb("h_gt", [P, KD, W])
        gg = sb("h_gg", [P, KD, W])
        rd1 = sb("h_rd1", [P, KD, W])
        dc = sb("h_dc", [P, EXPERTS, W])
        sq = sb("h_sq", [P, W])
        var = sb("h_var", [P, EXPERTS, W])
        y = sb("h_y", [P, EXPERTS, W])
        PAIRS_OUT = -(-TC // 2)
        acc = sb("h_acc", [P, PAIRS_OUT * P])
        logit = sb("h_logit", [P, EXPERTS, W])
        lg = sb("h_lg", [P, EXPERTS, W])
        lmax = sb("h_lmax", [P, W])
        lsum = sb("h_lsum", [P, W])
        linv = sb("h_linv", [P, W])
        rows = sb("h_rows", [P, PAIRS_OUT, P])
        names = ("s1_done s1_kept t1_done t1_kept s2_done s2_kept t2_done t2_kept d1_done d1_kept d2_done d2_kept "
                 "squared var_done var_kept gated logits logits_kept lmaxed lshifted lexped lsummed linverted "
                 "s1_high t1_high d1_high g_high s1_split t1_split d1_split g_split "
                 "rooted inverted normed scaled stepped divided mixed turned rows_kept")
        S = {n: sem("h_" + n) for n in names.split()}
        v_in, z2_in, h1_in, id_zero, id_done, ones, prep, prep_pe = [
            sem("h_" + n) for n in ("v_in", "z2_in", "h1_in", "id_zero", "id_done", "ones", "prep", "prep_pe")]
        raw_in = [sem(f"h_raw_in{q}") for q in range(2)]
        centred, measured, most_turned, most_shared, sizing, w_scaled, w_high, w_low, w_low2 = [
            sem("h_" + n) for n in ("centred", "measured", "most_turned", "most_shared", "sizing", "w_scaled", "w_high",
                                    "w_low", "w_low2")]
        mem_in = [sem(f"h_mem_in{q}") for q in range(2)]
        out_done, vec_turned, vec_kept = sem("h_out_done"), sem("h_vec_turned"), sem("h_vec_kept")
        block = open_block(nc, ctx, made)
        E = EXPERTS
        HIDDEN = ("sig_b1", "tan_b1", "dec_b1")
        SECOND = lambda a: a[:, NW:NW + 3]
        SIZING = 13
        tiles = lambda a: a.rearrange("p (t b) -> p t b", b=IMAGES)
        major = lambda a: a.rearrange("p (b s) -> p s b", s=SEQ)

        @block.sync
        def _(sp):
            for name, (at, k) in HEAD_VECTORS.items():
                sp.dma_start(vec_rows[E * at:E * (at + k), :],
                             io[name].rearrange("e (k p) -> (e k) p", p=P)).then_inc(v_in, 16)
            sp.dma_start(rw[:, :], io["router_w"]).then_inc(v_in, 16)
            sp.dma_start(rb[:, :], io["router_b"].partition_broadcast(P)).then_inc(v_in, 16)

            def load_mem(c, e):
                for d in range(2):
                    sp.dma_start(mem[:, e % 2, d].rearrange("p t q k b -> p t (q k b)"),
                                 mem_dram[e, d][ds(c * TC, TC)].rearrange("t f q k b -> f t (q k b)")).then_inc(mem_in[e % 2], 16)

            NAMES = dict(s1="sig_w1", t1="tan_w1", d1="dec_w1", s2="sig_w2", t2="tan_w2", d2="dec_w2")
            for e in range(E):
                if e >= 2:
                    sp.wait_ge(w_low, BASE + e - 1)
                    sp.wait_ge(w_low2, BASE + e - 1)
                for name, (at, k, width) in PLACE.items():
                    sp.dma_start(raw[:, e % 2, at:at + k * width].rearrange("p (k n) -> p k n", n=width),
                                 io[NAMES[name]][e].rearrange("(k p) n -> p k n", p=P)).then_inc(raw_in[e % 2], 16)
                if e == 1:
                    load_mem(0, 0)
                    load_mem(0, 1)
                    sp.dma_start(z2[:, :], z2_dram).then_inc(z2_in, 16)
            sp.dma_start(h1[:, :], h1_dram).then_inc(h1_in, 16)
            for e in range(2, E):
                sp.wait_ge(S["t1_done"], BASE + (e - 1) * KD)
                load_mem(0, e)
            with sp.Fori(0, CHUNKS - 1) as i:
                for e in range(E):
                    sp.wait_ge(S["t1_done"], BASE + ((i + 1) * E + e - 1) * KD)
                    load_mem(i + 1, e)

        @block.gpsimd
        def _(pool):
            make_identity(pool, ident, id_zero, id_done)
            pool.memset(mean[:, :], 1.0 / P).then_inc(ones, 1)
            pool.memset(eps[:, :], EPS).then_inc(ones, 1)
            pool.memset(units[:, :], 1.0).then_inc(ones, 1)
            pool.memset(acc[:, :], 0.0).then_inc(ones, 1)
            pool.wait_ge(ones, BASE + 4)
            pool.wait_ge(id_done, BASE + 1)
            for e in range(E):
                pool.wait_ge(w_high, BASE + e + 1)
                pool.tensor_tensor(w[:, e, 1, 0:OURS], raw[:, e % 2, 0:OURS], w[:, e, 0, 0:OURS], ALU.subtract).then_inc(w_low, 1)

            def low(name, n, scaled, split):
                pool.wait_ge(S[name + "_high"], BASE + n + 1)
                pool.tensor_tensor(split[:, 1], scaled[:, :, :], split[:, 0], ALU.subtract).then_inc(S[name + "_split"], 1)

            def mix(c, e):
                n = c * (E - 1) + e
                if e == 1:
                    pool.wait_ge(S["turned"], BASE + c)
                else:
                    pool.wait_ge(S["stepped"], BASE + n - 1)
                pool.wait_ge(S["scaled"], BASE + c * E + e + 1)
                pool.tensor_tensor(acc[:, 0:W], y[:, 0, :] if e == 1 else acc[:, 0:W], y[:, e, :],
                                   ALU.add).then_inc(S["stepped"], 1)

            def finish(c):
                pool.wait_ge(S["stepped"], BASE + (c + 1) * (E - 1))
                pool.wait_ge(S["linverted"], BASE + c + 1)
                pool.tensor_tensor(acc[:, 0:W], acc[:, 0:W], linv[:, :], ALU.mult).then_inc(S["divided"], 1)
                pool.wait_ge(S["divided"], BASE + c + 1)
                pool.tensor_tensor(tiles(acc[:, 0:W]), tiles(acc[:, 0:W]), major(h1[:, :])[:, ds(c * TC, TC), :],
                                   ALU.add).then_inc(S["mixed"], 1)

            def chunk(c, first):
                for e in range(E):
                    n = c * E + e
                    low("s1", n, rs1, rs1s)
                    if not first and e == 3:
                        mix(c - 1, 2)
                    if not (first and e == 0):
                        low("d1", n - 1, rd1, rd1s)
                    low("t1", n, rt1, rt1s)
                    if not first and e == 2:
                        mix(c - 1, 1)
                    if not first and e == 3:
                        mix(c - 1, 3)
                        finish(c - 1)
                    low("g", n, gg, ggs)

            chunk(0, True)
            pool.wait_ge(h1_in, BASE + 16)
            with pool.Fori(0, CHUNKS - 1) as i:
                chunk(i + 1, False)
            low("d1", CHUNKS * E - 1, rd1, rd1s)
            for e in range(1, E):
                mix(CHUNKS - 1, e)
            finish(CHUNKS - 1)

        @block.tensor
        def _(pe):
            pe.wait_ge(ones, BASE + 3)
            pe.wait_ge(v_in, BASE + 16 * (len(HEAD_VECTORS) + 2))
            pe.wait_ge(id_done, BASE + 1)
            pe.transpose(ps[:, 1, 0:E * NHEAD], vec_rows[:, :],
                         ident[0:E * NHEAD, 0:E * NHEAD]).then_inc(vec_turned, 1)
            pe.wait_ge(vec_kept, BASE + len(HEAD_VECTORS))
            for e in range(E):
                at, _ = HEAD_VECTORS["dec_b2"]
                mm = pe.matmul(ps[:, 0, e:e + 1], mean[:, :], vec[:, e, at:at + 1], start=True, stop=True)
            mm.then_inc(prep_pe, 1)
            for e in range(E):
                pe.wait_ge(measured, BASE + e + 1)
                pe.transpose(ps[0:NW + 3, 2, 0:P], most[:, e, :], ident[:, :]).then_inc(most_turned, 1)
                pe.wait_ge(sizing, BASE + SIZING * e + 2)
                pe.matmul(ps[:, 3, 0:NW + 3], units[:, :], diag[:, :], start=True, stop=True).then_inc(most_shared, 1)
            pe.wait_ge(prep, BASE + 2)
            pe.wait_ge(sizing, BASE + SIZING * E)
            pe.wait_ge(w_low, BASE + E)
            pe.wait_ge(w_low2, BASE + E)
            pe.wait_ge(id_done, BASE + 1)

            def group(name, e, banks, moving):
                at, nk, width = PLACE[name]
                for m, bank in enumerate(banks):
                    for k in range(nk):
                        for turn_, (a, b) in enumerate(PASSES):
                            here = at + k * width + m * P
                            mm = pe.matmul(ps[:, bank, 0:W], w[:, e, b, here:here + P], moving(k, a),
                                           start=(k == 0 and turn_ == 0), stop=(k == nk - 1 and turn_ == 2))
                    mm.then_inc(S[name + "_done"], 1)

            part_of = lambda split: lambda k, a: split[:, a, k, :]

            def decode(p, e, step):
                if step == 0:
                    pe.wait_ge(S["g_split"], BASE + p + 1)
                    group("d1", e, (6, 7), part_of(ggs))
                elif step == 1:
                    pe.wait_ge(S["d1_split"], BASE + p + 1)
                    group("d2", e, (6,), part_of(rd1s))
                else:
                    pe.wait_ge(S["squared"], BASE + p + 1)
                    pe.matmul(ps[:, 7, 0:W], mean[:, :], sq[:, :], start=True, stop=True).then_inc(S["var_done"], 1)

            def chunk(c, first):
                for e in range(E):
                    n = c * E + e
                    prev, before = not (first and e == 0), (e - 1) % E
                    q = e % 2
                    pe.wait_ge(mem_in[q], BASE + (c * 2 + e // 2 + 1) * 32)
                    mv = lambda k, a, q=q: mem[:, q, k // KD, :, a, k % KD, :]
                    pe.wait_ge(S["s1_kept"], BASE + n * KD)
                    group("s1", e, (0, 1), mv)
                    if prev:
                        pe.wait_ge(S["logits_kept"], BASE + n)
                        pe.wait_ge(S["var_kept"], BASE + n - 1)
                        if e == 0:
                            pe.wait_ge(S["rows_kept"], BASE + c - 1)
                        decode(n - 1, before, 0)
                    pe.wait_ge(S["t1_kept"], BASE + n * KD)
                    group("t1", e, (2, 3), mv)
                    if prev:
                        decode(n - 1, before, 1)
                    pe.wait_ge(S["s1_split"], BASE + n + 1)
                    pe.wait_ge(S["t2_kept"], BASE + n * KD)
                    group("s2", e, (4, 5), part_of(rs1s))
                    if prev:
                        decode(n - 1, before, 2)
                        pe.wait_ge(S["d2_kept"], BASE + n)
                    if first and e == 0:
                        pe.wait_ge(z2_in, BASE + 16)
                    pe.matmul(ps[:, 6, 0:W], rwb[:, e, :], major(z2[:, :])[:, ds(c * TC, TC), :],
                              start=True, stop=True).then_inc(S["logits"], 1)
                    pe.wait_ge(S["t1_split"], BASE + n + 1)
                    pe.wait_ge(S["s2_kept"], BASE + (n + 1) * KD)
                    group("t2", e, (4, 5), part_of(rt1s))
                if not first:
                    turn_out(c - 1, c * E + E - 1)

            def turn_out(c, variances):
                pe.wait_ge(S["mixed"], BASE + c + 1)
                pe.wait_ge(S["var_kept"], BASE + variances)
                for j in range(PAIRS_OUT):
                    mm = pe.transpose(ps[:, 7, j * P:(j + 1) * P], acc[:, j * P:(j + 1) * P], ident[:, :])
                mm.then_inc(S["turned"], 1)

            chunk(0, True)
            with pe.Fori(0, CHUNKS - 1) as i:
                chunk(i + 1, False)
            LAST = CHUNKS * E - 1
            pe.wait_ge(S["logits_kept"], BASE + LAST + 1)
            pe.wait_ge(S["var_kept"], BASE + LAST)
            pe.wait_ge(S["rows_kept"], BASE + CHUNKS - 1)
            for step in range(3):
                decode(LAST, E - 1, step)
            turn_out(CHUNKS - 1, LAST + 1)

        @block.vector
        def _(dve):
            dve.wait_ge(vec_turned, BASE + 1)
            for at, k in HEAD_VECTORS.values():
                dve.tensor_copy(vec[:, :, at:at + k],
                                ps[:, 1, E * at:E * (at + k)].rearrange("p (e k) -> p e k", k=k)).then_inc(vec_kept, 1)
            dve.wait_ge(v_in, BASE + 16 * (len(HEAD_VECTORS) + 2))
            dve.tensor_copy(rwb[:, :, :], rw[:, :].unsqueeze(2).broadcast_to([P, E, P])).then_inc(prep, 1)
            dve.wait_ge(prep_pe, BASE + 1)
            at, _ = HEAD_VECTORS["dec_b2"]
            dve.tensor_tensor(b2c[:, :], vec[:, :, at], ps[:, 0, 0:E], ALU.subtract).then_inc(prep, 1)
            dve.wait_ge(vec_kept, BASE + len(HEAD_VECTORS))
            dve.wait_ge(id_done, BASE + 1)
            dve.wait_ge(ones, BASE + 4)

            def low_w(e):
                dve.wait_ge(w_high, BASE + e + 1)
                dve.tensor_tensor(w[:, e, 1, OURS:], raw[:, e % 2, OURS:], w[:, e, 0, OURS:], ALU.subtract).then_inc(w_low2, 1)

            for e in range(E):
                here = raw[:, e % 2]
                dve.wait_ge(raw_in[e % 2], BASE + (e // 2 + 1) * 16 * NW)
                at, k, width = PLACE["d2"]
                d2 = here[:, at:at + k * width].rearrange("p (k n) -> p k n", n=width)
                dve.tensor_reduce(d2_sum[:, :], d2, AX.X, ALU.add).then_inc(centred, 1)
                dve.wait_ge(centred, BASE + 3 * e + 1)
                dve.tensor_scalar(d2_mean[:, :], d2_sum[:, :], 1.0 / P, None, ALU.mult).then_inc(centred, 1)
                dve.wait_ge(centred, BASE + 3 * e + 2)
                dve.tensor_tensor(d2, d2, d2_mean[:, :].unsqueeze(2).broadcast_to([P, k, width]), ALU.subtract).then_inc(centred, 1)
                dve.wait_ge(centred, BASE + 3 * e + 3)
                for n, (at, k, width) in enumerate(PLACE.values()):
                    dve.tensor_reduce(most[:, e, n:n + 1], here[:, at:at + k * width], AX.X, ALU.max, apply_absolute_value=True)
                for n, name in enumerate(HIDDEN):
                    at, k = HEAD_VECTORS[name]
                    op = dve.tensor_reduce(most[:, e, NW + n:NW + n + 1], vec[:, e, at:at + k], AX.X, ALU.max,
                                           apply_absolute_value=True)
                op.then_inc(measured, 1)
                step = [SIZING * e]

                def then(op, after=True):
                    op.then_inc(sizing, 1)
                    step[0] += 1
                    if after:
                        dve.wait_ge(sizing, BASE + step[0])

                dve.wait_ge(most_turned, BASE + e + 1)
                then(dve.tensor_reduce(row_most[:, :], ps[0:NW + 3, 2, 0:P], AX.X, ALU.max))
                then(dve.tensor_scalar(diag[:, :], ident[0:NW + 3, 0:NW + 3], row_most[:, 0:1], None, ALU.mult), after=False)
                dve.wait_ge(most_shared, BASE + e + 1)
                then(dve.tensor_scalar(bound[:, 0:NW], ps[:, 3, 0:NW], TINY, None, ALU.max))
                then(dve.scalar_tensor_tensor(out=bound[:, NW:NW + 3], in0=bound[:, 0:3], scalar=2.0 * D, in1=ps[:, 3, NW:NW + 3],
                                              op0=ALU.mult, op1=ALU.add))
                then(dve.tensor_scalar(power[:, :].bitcast(I32), bound[:, :].bitcast(I32), EXPONENT, None, ALU.bitwise_and))
                then(dve.reciprocal(inv_power[:, :], power[:, :]))
                then(dve.tensor_scalar(w_scale[:, e, :], inv_power[:, 0:NW], TOP, None, ALU.mult), after=False)
                then(dve.tensor_scalar(r_scale[:, :], inv_power[:, NW:NW + 3], TOP, None, ALU.mult), after=False)
                then(dve.scalar_tensor_tensor(out=factor[:, e, 0:3], in0=power[:, 0:3], scalar=1.0 / TOP,
                                              in1=inv_power[:, NW:NW + 3], op0=ALU.mult, op1=ALU.mult), after=False)
                then(dve.scalar_tensor_tensor(out=factor[:, e, 3:NW], in0=power[:, 3:NW], scalar=1.0 / TOP / TOP,
                                              in1=SECOND(power), op0=ALU.mult, op1=ALU.mult))
                for n, name in enumerate(HIDDEN):
                    at, k = HEAD_VECTORS[name]
                    then(dve.tensor_scalar(bias1[:, e, n, :], vec[:, e, at:at + k], r_scale[:, n:n + 1], None, ALU.mult), after=False)
                assert step[0] == SIZING * (e + 1)
                if e:
                    low_w(e - 1)
            low_w(E - 1)

            def high(name, n, scaled, split, readers):
                dve.wait_ge(S[name + "_kept"], BASE + (n + 1) * KD)
                dve.wait_ge(S[readers], BASE + n * (KD if readers != "d2_done" else 1))
                dve.tensor_copy(split[:, 0], scaled[:, :, :]).then_inc(S[name + "_high"], 1)

            over = lambda a: a[:, :, :].rearrange("p e w -> p w e")
            all_ = lambda a: a[:, :].unsqueeze(1).broadcast_to([P, E, W])

            def shift_logits(c):
                dve.wait_ge(S["logits_kept"], BASE + (c + 1) * E)
                dve.tensor_reduce(lmax[:, :], over(logit), AX.X, ALU.max).then_inc(S["lmaxed"], 1)
                dve.wait_ge(S["lmaxed"], BASE + c + 1)
                dve.tensor_tensor(lg[:, :, :], logit[:, :, :], all_(lmax), ALU.subtract).then_inc(S["lshifted"], 1)

            def sum_up(c):
                dve.wait_ge(S["lexped"], BASE + c + 1)
                dve.tensor_reduce(lsum[:, :], over(lg), AX.X, ALU.add).then_inc(S["lsummed"], 1)

            def invert_sum(c):
                dve.wait_ge(S["lsummed"], BASE + c + 1)
                dve.wait_ge(S["mixed"], BASE + c)
                dve.reciprocal(linv[:, :], lsum[:, :]).then_inc(S["linverted"], 1)

            def scale(c, e):
                n = c * E + e
                dve.wait_ge(S["rooted"], BASE + c + 1)
                dve.reciprocal(var[:, e, :], var[:, e, :]).then_inc(S["inverted"], 1)
                dve.wait_ge(S["inverted"], BASE + n + 1)
                dve.wait_ge(S["mixed"], BASE + c)
                at, _ = HEAD_VECTORS["dec_g"]
                dve.scalar_tensor_tensor(out=y[:, e, :], in0=dc[:, e, :], scalar=vec[:, e, at:at + 1],
                                         in1=var[:, e, :], op0=ALU.mult, op1=ALU.mult).then_inc(S["normed"], 1)
                dve.wait_ge(S["normed"], BASE + n + 1)
                dve.scalar_tensor_tensor(out=y[:, e, :], in0=y[:, e, :], scalar=vec[:, e, at + 1:at + 2],
                                         in1=lg[:, e, :], op0=ALU.add, op1=ALU.mult).then_inc(S["scaled"], 1)

            def keep_d2(p, e):
                dve.wait_ge(S["d2_done"], BASE + p + 1)
                dve.tensor_scalar(dc[:, e, :], ps[:, 6, 0:W], factor[:, e, 5:6], b2c[:, e:e + 1],
                                  ALU.mult, ALU.add).then_inc(S["d2_kept"], 1)

            def keep_var(p, e):
                dve.wait_ge(S["var_done"], BASE + p + 1)
                dve.tensor_copy(var[:, e, :], ps[:, 7, 0:W]).then_inc(S["var_kept"], 1)

            def chunk(c, first):
                for e in range(E):
                    n = c * E + e
                    prev, before = not (first and e == 0), (e - 1) % E
                    if not first:
                        if e == 0:
                            shift_logits(c - 1)
                    high("s1", n, rs1, rs1s, "s2_done")
                    if prev:
                        high("d1", n - 1, rd1, rd1s, "d2_done")
                    if not first and e:
                        scale(c - 1, (0, 0, 1, 3)[e])
                    high("t1", n, rt1, rt1s, "t2_done")
                    if prev:
                        keep_d2(n - 1, before)
                        if not first and e == 1:
                            dve.wait_ge(S["rooted"], BASE + c)
                        keep_var(n - 1, before)
                    dve.wait_ge(S["logits"], BASE + n + 1)
                    dve.tensor_scalar(logit[:, e, :], ps[:, 6, 0:W], rb[:, e:e + 1], None,
                                      ALU.add).then_inc(S["logits_kept"], 1)
                    dve.wait_ge(S["t2_kept"], BASE + (n + 1) * KD)
                    dve.wait_ge(S["g_split"], BASE + n)
                    dve.scalar_tensor_tensor(out=gg[:, :, :], in0=gs[:, :, :], scalar=TOP, in1=gt[:, :, :],
                                             op0=ALU.mult, op1=ALU.mult).then_inc(S["gated"], 1)
                    dve.wait_ge(S["gated"], BASE + n + 1)
                    dve.wait_ge(S["d1_done"], BASE + n * KD)
                    dve.tensor_copy(ggs[:, 0], gg[:, :, :]).then_inc(S["g_high"], 1)
                    if not first:
                        if e == 0:
                            sum_up(c - 1)
                        elif e == 1:
                            invert_sum(c - 1)
                        elif e == 2:
                            scale(c - 1, 2)

            chunk(0, True)
            with dve.Fori(0, CHUNKS - 1) as i:
                chunk(i + 1, False)
            LAST = CHUNKS * E - 1
            shift_logits(CHUNKS - 1)
            high("d1", LAST, rd1, rd1s, "d2_done")
            keep_d2(LAST, E - 1)
            keep_var(LAST, E - 1)
            sum_up(CHUNKS - 1)
            invert_sum(CHUNKS - 1)
            for e in range(E):
                scale(CHUNKS - 1, e)

        @block.scalar
        def _(act):
            order = list(PLACE)

            def leave(n, e, name, banks, dst, bias, func):
                for m, bank in enumerate(banks):
                    act.wait_ge(S[name + "_done"], BASE + n * KD + m + 1)
                    at = order.index(name)
                    act.activation(dst[:, m, :], ps[:, bank, 0:W], func, bias=bias(m),
                                   scale=factor[:, e, at:at + 1]).then_inc(S[name + "_kept"], 1)

            def hidden(n, e, name, banks, dst):
                act.wait_ge(S[name + "_split"], BASE + n)
                leave(n, e, name, banks, dst, lambda m: bias1[:, e, order.index(name), m:m + 1], ACT.Relu)

            def column(e, name):
                at, _ = HEAD_VECTORS[name]
                return lambda m: vec[:, e, at + m:at + m + 1]

            def exponentials(c):
                act.wait_ge(S["lshifted"], BASE + c + 1)
                act.activation(lg[:, :, :], lg[:, :, :], ACT.Exp).then_inc(S["lexped"], 1)

            def square(p, e):
                act.wait_ge(S["d2_kept"], BASE + p + 1)
                act.wait_ge(S["var_done"], BASE + p)
                act.activation(sq[:, :], dc[:, e, :], ACT.Square).then_inc(S["squared"], 1)

            def roots(c):
                act.wait_ge(S["var_kept"], BASE + (c + 1) * E)
                act.activation(var[:, :, :], var[:, :, :], ACT.Sqrt, bias=eps[:, 0:1]).then_inc(S["rooted"], 1)

            def rows_out(c):
                act.wait_ge(S["turned"], BASE + c + 1)
                act.wait_ge(out_done, BASE + c * 32)
                act.copy(rows[:, :, :], ps[:, 7, 0:PAIRS_OUT * P].rearrange("p (j f) -> p j f", f=P)).then_inc(S["rows_kept"], 1)
                act.wait_ge(S["rows_kept"], BASE + c + 1)
                here = out[:, ds(c * TC, TC), :]
                for odd in range(2):
                    act.dma_start(here[:, odd:TC:2, :],
                                  rows[odd * IMAGES:(odd + 1) * IMAGES, 0:(TC + 1 - odd) // 2, :]).then_inc(out_done, 16)

            def chunk(c, first):
                for e in range(E):
                    n = c * E + e
                    hidden(n, e, "s1", (0, 1), rs1)
                    if not (first and e == 0):
                        hidden(n - 1, (e - 1) % E, "d1", (6, 7), rd1)
                    if e == 0 and not first:
                        exponentials(c - 1)
                    hidden(n, e, "t1", (2, 3), rt1)
                    if not (first and e == 0):
                        square(n - 1, (e - 1) % E)
                    act.wait_ge(S["gated"], BASE + n)
                    leave(n, e, "s2", (4, 5), gs, column(e, "sig_b2"), ACT.Sigmoid)
                    leave(n, e, "t2", (4, 5), gt, column(e, "tan_b2"), ACT.Tanh)
                    if e == 0 and not first:
                        roots(c - 1)
                if not first:
                    rows_out(c - 1)

            act.wait_ge(ones, BASE + 2)
            act.wait_ge(vec_kept, BASE + len(HEAD_VECTORS))
            for e in range(E):
                for n, (at, k, width) in enumerate(PLACE.values()):
                    act.wait_ge(sizing, BASE + SIZING * (e + 1))
                    act.activation(raw[:, e % 2, at:at + k * width], raw[:, e % 2, at:at + k * width], ACT.Identity,
                                   scale=w_scale[:, e, n:n + 1]).then_inc(w_scaled, 1)
                act.wait_ge(w_scaled, BASE + NW * (e + 1))
                act.copy(w[:, e, 0, :], raw[:, e % 2, :]).then_inc(w_high, 1)
            chunk(0, True)
            with act.Fori(0, CHUNKS - 1) as i:
                chunk(i + 1, False)
            hidden(CHUNKS * E - 1, E - 1, "d1", (6, 7), rd1)
            exponentials(CHUNKS - 1)
            square(CHUNKS * E - 1, E - 1)
            roots(CHUNKS - 1)
            rows_out(CHUNKS - 1)
            act.wait_ge(out_done, BASE + CHUNKS * 32)


def vit_tower(nc, inputs, out):
    first = dict(x="x", tok_W="L0_tok_W", tok_b="L0_tok_b", cls="L0_tok_class_token", pos="L0_tok_pos_embed",
                 w_qkv="L0_attn_w_qkv", w_agg="L0_attn_w_agg", b_agg="L0_attn_b_agg")
    experts = {name[len("L0_ffn_"):]: ap for name, ap in inputs.items() if name.startswith("L0_ffn_")}
    scratch = lambda name, *shape: nc.dram_tensor(name, shape, F32).ap()
    h1 = scratch("h1_scratch", P, TOKENS)
    z2 = scratch("z2_scratch", P, TOKENS)
    x = scratch("x_scratch", EXPERTS, SEQ, P, KD, IMAGES)
    peak = scratch("peak_scratch", P, EXPERTS * IMAGES // GROUP)
    mem = nc.dram_tensor("mem_scratch", (EXPERTS, 2, SEQ, P, 2, KD, IMAGES), F16).ap()
    with nc.psum_tensor("banks", [P, 8, 512], F32) as ps:
        stages(nc, ps, first, experts, inputs, h1, z2, x, peak, mem, out)


def stages(nc, ps, first, experts, inputs, h1, z2, x, peak, mem, out):
    front(nc, ps, {key: inputs[name] for key, name in first.items()}, h1, z2)
    experts_stage(nc, ps, experts, z2, x, peak)
    lstm_stage(nc, ps, experts, x, peak, mem)
    head_stage(nc, ps, experts, h1, z2, mem, out)


_FFN = ("router_w router_b enc_w1 enc_b1 enc_w2 enc_b2 enc_g enc_beta attn_in_w attn_in_b attn_out_w attn_out_b "
        "lstm_wi_f lstm_wh_f lstm_b_f lstm_wi_b lstm_wh_b lstm_b_b sig_w1 sig_b1 sig_w2 sig_b2 tan_w1 tan_b1 tan_w2 "
        "tan_b2 dec_w1 dec_b1 dec_w2 dec_b2 dec_g dec_beta").split()
_INS = ["x", "L0_tok_W", "L0_tok_b", "L0_tok_class_token", "L0_tok_pos_embed", "L0_attn_w_qkv", "L0_attn_w_agg",
        "L0_attn_b_agg"] + ["L0_ffn_" + n for n in _FFN]
_OUTS = [((64, 65, 128), "float32")]


def kernel(**inputs):
    import numpy as _np
    import concourse.bacc as _bacc
    from concourse import mybir as _mybir
    from concourse.bass_utils import run_bass_kernel_spmd as _run

    nc = _bacc.Bacc("TRN2", target_bir_lowering=False, num_devices=1)
    arrays, args = {}, {}
    for name in _INS:
        a = _np.ascontiguousarray(inputs[name])
        arrays[f"in_{name}_dram"] = a
        args[name] = nc.dram_tensor(f"in_{name}_dram", a.shape, _mybir.dt.from_np(a.dtype), kind="ExternalInput").ap()
    (shape, dtype), = _OUTS
    out = nc.dram_tensor("out_0_dram", shape, _mybir.dt.from_np(_np.dtype(dtype)), kind="ExternalOutput").ap()
    vit_tower(nc, args, out)
    r = _run(nc, [arrays], core_ids=[0])
    return r.results[0]["out_0_dram"]
```
